# Optimizing a Trainium2 kernel written in Bass

```python
import numpy as np
import jax
import jax.numpy as jnp

def _softmax(x, axis=-1):
    return jax.nn.softmax(x, axis=axis)

def _gelu(x):
    return jax.nn.gelu(x, approximate=True)

def _silu(x):
    return jax.nn.silu(x)

def _sigmoid(x):
    return jax.nn.sigmoid(x)

def _layernorm(x, axis=-1, eps=1e-05):
    m = jnp.mean(x, axis=axis, keepdims=True)
    v = jnp.var(x, axis=axis, keepdims=True)
    return (x - m) / jnp.sqrt(v + eps)

def _scatter_add(tgt, idx, src, axis=0):
    return tgt.at[idx].add(src)

def _segment_sum(src, seg, n):
    return jax.ops.segment_sum(src, seg, n)
kernel_name = 'mk_gnn_preln_d2_gnn_r32_36e432'

def setup_inputs(seed: int=0):
    np.random.seed(seed)
    _w = jnp.asarray

    def _rec_inputs():
        import jax
        import jax.numpy as jnp
        _gk = jax.random.key(seed)
        x = -0.0003713 + 1 * jax.random.normal(jax.random.fold_in(_gk, 1), (50000, 256), jnp.float32)
        src = jax.random.randint(jax.random.fold_in(_gk, 2), (25000,), 0, 50000, jnp.int32)
        dst = jax.random.randint(jax.random.fold_in(_gk, 3), (25000,), 0, 50000, jnp.int32)
        _o = jnp.argsort(dst, stable=True)
        src = src[_o]
        dst = dst[_o]
        edge_type_16 = jax.random.randint(jax.random.fold_in(_gk, 13), (25000,), 0, 16, jnp.int32)
        return (x, src, dst, edge_type_16)
    x, src, dst, edge_type_16 = _rec_inputs()

    def _L0_gnn_setup():
        import jax, jax.numpy as jnp
        import numpy as np
        N = 50000
        E = 25000
        D = 256
        EPS = 1e-05

        def _gcn_conv(x, W, b, row, col):
            h = x @ W
            deg = jnp.zeros((N,), x.dtype).at[col].add(jnp.ones((row.shape[0],), x.dtype))
            dinv = jax.lax.rsqrt(deg)
            norm = dinv[row] * dinv[col]
            msg = h[row] * norm[:, None]
            out = jnp.zeros_like(h).at[col].add(msg)
            return out + b

        def _bn(x, gamma, beta):
            m = jnp.mean(x, axis=0)
            v = jnp.var(x, axis=0)
            return (x - m) * jax.lax.rsqrt(v + EPS) * gamma + beta
        key = jax.random.key(seed)
        ks = jax.random.split(key, 4)
        x = jax.random.normal(ks[0], (N, D), dtype=jnp.float32)
        edge_index = jax.random.randint(ks[1], (2, E), 0, N, dtype=jnp.int64)
        s = 1.0 / np.sqrt(D)
        W1 = jax.random.uniform(ks[2], (D, D), jnp.float32, -s, s)
        W2 = jax.random.uniform(ks[3], (D, D), jnp.float32, -s, s)
        z = jnp.zeros((D,), jnp.float32)
        o = jnp.ones((D,), jnp.float32)
        return {'x': x, 'edge_index': edge_index, 'W1': W1, 'b1': z, 'g1': o, 'be1': z, 'W2': W2, 'b2': z, 'g2': o, 'be2': z}
    _L0_gnn_all = _L0_gnn_setup()
    _L0_gnn_in = {k: v for k, v in _L0_gnn_all.items() if k in ('W1', 'b1', 'g1', 'be1', 'W2', 'b2', 'g2', 'be2')}
    del _L0_gnn_all

    def _L1_gnn_setup():
        import jax, jax.numpy as jnp
        import numpy as np
        N_NODES = 50000
        N_EDGES = 25000
        HDIM = 256
        NUMRELS = 16

        def _gru_cell(x, h, w_ih, w_hh, b_ih, b_hh):
            gi = x @ w_ih.T + b_ih
            gh = h @ w_hh.T + b_hh
            i_r, i_z, i_n = jnp.split(gi, 3, axis=-1)
            h_r, h_z, h_n = jnp.split(gh, 3, axis=-1)
            r = jax.nn.sigmoid(i_r + h_r)
            z = jax.nn.sigmoid(i_z + h_z)
            n = jnp.tanh(i_n + r * h_n)
            return (1.0 - z) * n + z * h
        key = jax.random.key(seed)
        ks = jax.random.split(key, 9)
        h = jax.random.normal(ks[0], (N_NODES, HDIM), dtype=jnp.float32)
        relvectors = jax.random.normal(ks[1], (NUMRELS, HDIM), dtype=jnp.float32)
        s = 1.0 / np.sqrt(HDIM)
        w_ih = jax.random.uniform(ks[2], (3 * HDIM, HDIM), minval=-s, maxval=s, dtype=jnp.float32)
        w_hh = jax.random.uniform(ks[3], (3 * HDIM, HDIM), minval=-s, maxval=s, dtype=jnp.float32)
        b_ih = jax.random.uniform(ks[4], (3 * HDIM,), minval=-s, maxval=s, dtype=jnp.float32)
        b_hh = jax.random.uniform(ks[5], (3 * HDIM,), minval=-s, maxval=s, dtype=jnp.float32)
        edge_src = jax.random.randint(ks[6], (N_EDGES,), 0, N_NODES, dtype=jnp.int32)
        edge_dst = jax.random.randint(ks[7], (N_EDGES,), 0, N_NODES, dtype=jnp.int32)
        edge_rel = jax.random.randint(ks[8], (N_EDGES,), 0, NUMRELS, dtype=jnp.int32)
        return {'h': h, 'relvectors': relvectors, 'w_ih': w_ih, 'w_hh': w_hh, 'b_ih': b_ih, 'b_hh': b_hh, 'edge_src': edge_src, 'edge_dst': edge_dst, 'edge_rel': edge_rel}
    _L1_gnn_all = _L1_gnn_setup()
    _L1_gnn_in = {k: v for k, v in _L1_gnn_all.items() if k in ('relvectors', 'w_ih', 'w_hh', 'b_ih', 'b_hh')}
    del _L1_gnn_all
    return {'x': x, 'src': src, 'dst': dst, 'edge_type_16': edge_type_16, 'L0_gnn_W1': _L0_gnn_in['W1'], 'L0_gnn_b1': _L0_gnn_in['b1'], 'L0_gnn_g1': _L0_gnn_in['g1'], 'L0_gnn_be1': _L0_gnn_in['be1'], 'L0_gnn_W2': _L0_gnn_in['W2'], 'L0_gnn_b2': _L0_gnn_in['b2'], 'L0_gnn_g2': _L0_gnn_in['g2'], 'L0_gnn_be2': _L0_gnn_in['be2'], 'L1_gnn_relvectors': _L1_gnn_in['relvectors'], 'L1_gnn_w_ih': _L1_gnn_in['w_ih'], 'L1_gnn_w_hh': _L1_gnn_in['w_hh'], 'L1_gnn_b_ih': _L1_gnn_in['b_ih'], 'L1_gnn_b_hh': _L1_gnn_in['b_hh']}

def reference(x, src, dst, edge_type_16, L0_gnn_W1, L0_gnn_b1, L0_gnn_g1, L0_gnn_be1, L0_gnn_W2, L0_gnn_b2, L0_gnn_g2, L0_gnn_be2, L1_gnn_relvectors, L1_gnn_w_ih, L1_gnn_w_hh, L1_gnn_b_ih, L1_gnn_b_hh):
    import jax
    import jax.numpy as jnp

    def _L0_gnn_ref(x, edge_index, W1, b1, g1, be1, W2, b2, g2, be2):
        import jax, jax.numpy as jnp
        import numpy as np
        N = 50000
        E = 25000
        D = 256
        EPS = 1e-05

        def _gcn_conv(x, W, b, row, col):
            h = x @ W
            deg = jnp.zeros((N,), x.dtype).at[col].add(jnp.ones((row.shape[0],), x.dtype))
            dinv = jax.lax.rsqrt(deg)
            norm = dinv[row] * dinv[col]
            msg = h[row] * norm[:, None]
            out = jnp.zeros_like(h).at[col].add(msg)
            return out + b

        def _bn(x, gamma, beta):
            m = jnp.mean(x, axis=0)
            v = jnp.var(x, axis=0)
            return (x - m) * jax.lax.rsqrt(v + EPS) * gamma + beta
        loops = jnp.arange(N, dtype=edge_index.dtype)
        row = jnp.concatenate([edge_index[0], loops])
        col = jnp.concatenate([edge_index[1], loops])
        h = _gcn_conv(x, W1, b1, row, col)
        h = jax.nn.relu(_bn(h, g1, be1))
        h = _gcn_conv(h, W2, b2, row, col)
        h = jax.nn.relu(_bn(h, g2, be2))
        return h

    def _L1_gnn_ref(h, relvectors, w_ih, w_hh, b_ih, b_hh, edge_src, edge_dst, edge_rel):
        import jax, jax.numpy as jnp
        import numpy as np
        N_NODES = 50000
        N_EDGES = 25000
        HDIM = 256
        NUMRELS = 16

        def _gru_cell(x, h, w_ih, w_hh, b_ih, b_hh):
            gi = x @ w_ih.T + b_ih
            gh = h @ w_hh.T + b_hh
            i_r, i_z, i_n = jnp.split(gi, 3, axis=-1)
            h_r, h_z, h_n = jnp.split(gh, 3, axis=-1)
            r = jax.nn.sigmoid(i_r + h_r)
            z = jax.nn.sigmoid(i_z + h_z)
            n = jnp.tanh(i_n + r * h_n)
            return (1.0 - z) * n + z * h
        msg = h[edge_src] + relvectors[edge_rel]
        red = jax.ops.segment_sum(msg, edge_dst, num_segments=h.shape[0])
        return _gru_cell(red, h, w_ih, w_hh, b_ih, b_hh)
    edge_index = jnp.stack([src, dst])
    h = jnp.maximum(_layernorm(x, axis=-1), 0.0)
    x = x + _L0_gnn_ref(h, edge_index, L0_gnn_W1, L0_gnn_b1, L0_gnn_g1, L0_gnn_be1, L0_gnn_W2, L0_gnn_b2, L0_gnn_g2, L0_gnn_be2)
    h = jnp.maximum(_layernorm(x, axis=-1), 0.0)
    x = x + _L1_gnn_ref(h, L1_gnn_relvectors, L1_gnn_w_ih, L1_gnn_w_hh, L1_gnn_b_ih, L1_gnn_b_hh, src, dst, edge_type_16)
    return x

_drawn_inputs = setup_inputs


def setup_inputs(seed=0):
    import zlib

    import numpy as np

    out = dict(_drawn_inputs(seed))
    spreads = {'L0_gnn_b1': (0.0, 0.8),
     'L0_gnn_g1': (1.0, 0.2),
     'L0_gnn_be1': (0.0, 0.1),
     'L0_gnn_b2': (0.0, 0.8),
     'L0_gnn_g2': (1.0, 0.2),
     'L0_gnn_be2': (0.0, 0.1)}
    factors = {'L1_gnn_b_ih': 5.169, 'L1_gnn_b_hh': 8.0}
    for name, (base, spread) in spreads.items():
        noise = np.random.default_rng([zlib.crc32(name.encode()), seed]).standard_normal(out[name].shape)
        drawn = base * np.exp(spread * noise) if base else spread * noise
        out[name] = jnp.asarray(drawn.astype(out[name].dtype))
    for name, factor in factors.items():
        out[name] = (out[name] * factor).astype(out[name].dtype)
    return out
```

```python
def build_program(nc, x, dst_row, dst_col, src_col, type_row, W1, b1, g1, be1, W2, b2, g2, be2,
                  rel, w_ih, w_hh, b_ih, b_hh, out):
    from contextlib import ExitStack
    import concourse.bass as bass
    from concourse import mybir

    F32 = mybir.dt.float32
    F32R = mybir.dt.float32r
    F16 = mybir.dt.float16
    I32 = mybir.dt.int32
    ALU = mybir.AluOpType
    ACT = mybir.ActivationFunctionType
    AX = mybir.AxisListType

    P = 128
    N, D = x.shape
    E = 25000
    Q = 4
    BLK = P * Q
    NB = -(-N // BLK)
    TAIL = (N - (NB - 1) * BLK) // Q
    NCOL = NB * Q
    NPAD = NB * BLK
    NT = dst_col.shape[1]
    NG = NT // Q
    KD = D // P
    G3 = w_ih.shape[0] // P
    NREL = rel.shape[0]
    EPS = 1e-5
    ROW = Q * D
    ds = bass.ds

    assert TAIL * Q + (NB - 1) * BLK == N and NG * Q == NT

    dinv_tab = nc.dram_tensor("dinv_tab", (P * NCOL, 1), F32, kind="Internal").ap()
    seg = nc.dram_tensor("seg", (NT * P, D), F32, kind="Internal").ap()
    o1t = nc.dram_tensor("o1t", (NB * P, ROW), F32, kind="Internal").ap()
    g2s = nc.dram_tensor("g2s", (NPAD, D), F32, kind="Internal").ap()
    o2t = nc.dram_tensor("o2t", (NB * P, ROW), F32, kind="Internal").ap()
    x1s = nc.dram_tensor("x1s", (NPAD, D), F32, kind="Internal").ap()

    def rows4(t):
        return t.rearrange("(r q) d -> r (q d)", q=Q)

    x_r, out_r, g2_r, x1_r = rows4(x), rows4(out), rows4(g2s), rows4(x1s)
    seg_t = seg.rearrange("(t p) d -> p t d", p=P)

    def steps(eng, n, lag, step, unroll=2):
        head = -(-(lag + 4) // unroll) * unroll
        end = head + (n - 1 - head) // unroll * unroll
        for t in range(head):
            step(t, t % unroll)
        with eng.Fori(head // unroll, end // unroll) as k:
            for u in range(unroll):
                step(k * unroll + u, u)
        for t in range(end, n + lag):
            step(t, t % unroll)

    def live(b, n):
        return not isinstance(b, int) or 0 <= b < n

    def after(b, slots=2):
        return not isinstance(b, int) or b >= slots

    def turn(b, slots=2):
        if isinstance(b, int):
            return b // slots + 1
        return None

    with ExitStack() as keep:
        def ksb(name, shape, dt=F32):
            return keep.enter_context(nc.sbuf_tensor(name, shape, dt))

        ident = ksb("ident", [P, P])
        pidx = ksb("pidx", [P, 1])
        eps = ksb("eps", [P, 1])
        zero = ksb("zero", [P, 1])
        dinv = ksb("dinv", [P, NCOL])
        dinv2 = ksb("dinv2", [P, NCOL])
        has = ksb("has", [P, NCOL])
        dh = ksb("dh", [P, NB, 2, Q])
        end_index = ksb("end_index", [P, NCOL], I32)
        dst_f = ksb("dst_f", [P, NT])
        carry_f = ksb("carry_f", [P, NT])
        src_i = ksb("src_i", [P, NT], I32)
        src_pos = ksb("src_pos", [P, NT], I32)
        w1 = ksb("w1", [P, KD, D])
        w2 = ksb("w2", [P, KD, D])
        rel_sb = ksb("rel_sb", [NREL, D])
        bn_in = {k: ksb(k, [P, KD]) for k in ("b1c", "g1c", "be1c", "b2c", "g2c", "be2c")}
        bih = ksb("bih", [P, G3])
        bhh = ksb("bhh", [P, G3])
        brz = ksb("brz", [P, G3])
        whi = {k: ksb(f"{k}_hi", [P, KD, G3 * P], F32R) for k in ("ih", "hh")}
        wlo = {k: ksb(f"{k}_lo", [P, KD, G3 * P], F32R) for k in ("ih", "hh")}
        bn_s = ksb("bn_s", [P, KD])
        bn_t = ksb("bn_t", [P, KD])
        issuing = keep.enter_context(nc.semaphore("issuing"))
        mv1 = ksb("mv1", [P, NCOL, 2])
        snb = ksb("snb", [P, NB, 2, Q])

        def setup():
            with ExitStack() as ctx:
                def sb(name, shape, dt=F32):
                    return ctx.enter_context(nc.sbuf_tensor(name, shape, dt))

                def sem(name):
                    return ctx.enter_context(nc.semaphore(name))

                dst_i = sb("dst_i", [P, NT], I32)
                ia, ib, ic = (sb(n, [P, NT], I32) for n in ("ia", "ib", "ic"))
                fa, fb = sb("fa", [P, NT]), sb("fb", [P, NT])
                dst_a, dst_p = sb("dst_a", [P, NT], F16), sb("dst_p", [P, NT], F16)
                row_i = sb("row_i", [P, NCOL], I32)
                row_h = sb("row_h", [P, NCOL], F16)
                row_f = sb("row_f", [P, P])
                pidx_i = sb("pidx_i", [P, 1], I32)
                last = sb("last", [P, 1])
                node_mask = sb("node_mask", [P, 1])
                tri = sb("tri", [P, P])
                ones = sb("ones", [P, P])
                hot_a = [sb(f"hot_a{i}", [P, Q, NCOL], F16) for i in range(2)]
                hot_p = [sb(f"hot_p{i}", [P, Q, P], F16) for i in range(2)]
                wraw = {k: sb(f"w{k}_raw", [P, G3, D]) for k in ("ih", "hh")}
                cnt = sb("cnt", [P, NB, Q])
                deg = sb("deg", [P, NCOL])
                blk_sum = sb("blk_sum", [P, NB])
                base, tot, run = sb("base", [P, NB]), sb("tot", [P, NB]), sb("run", [P, NB])
                cum = sb("cum", [P, NB, Q])
                big = sb("big", [P, NCOL])
                ps_w = [ctx.enter_context(nc.psum_tensor(f"ps_w{i}", [P, KD, G3 * P], F32)) for i in range(2)]
                ps_c = ctx.enter_context(nc.psum_tensor("ps_c", [P, NCOL], F32))
                ps_b = ctx.enter_context(nc.psum_tensor("ps_b", [P, 2, NB], F32))
                loaded_dst, loaded_src, loaded_w, tab_stored = (sem(n) for n in (
                    "loaded_dst", "loaded_src", "loaded_w", "tab_stored"))
                iotas, consts, hots, hists, wts, sums, sums_ps, deg_ready, sd_ready, dve_step, tab_ready = (
                    sem(n) for n in ("iotas", "consts", "hots", "hists", "wts", "sums", "sums_ps",
                                     "deg_ready", "sd_ready", "dve_step", "tab_ready"))

                with nc.Block() as block:
                    @block.sync
                    def _(sp):
                        sp.dma_start(dst_i[:], dst_col).then_inc(loaded_dst, 16)
                        sp.dma_start(src_i[:], src_col).then_inc(loaded_src, 16)
                        n = 0
                        for k, w in (("ih", w_ih), ("hh", w_hh)):
                            sp.dma_start(wraw[k][:], w.rearrange("(c p) d -> p c d", p=P)).then_inc(loaded_w, 16)
                            n += 16
                        for t, w in ((w1, W1), (w2, W2)):
                            sp.dma_start(t[:], w.rearrange("(c p) d -> p c d", p=P)).then_inc(loaded_w, 16)
                            n += 16
                        sp.dma_start(rel_sb[:], rel).then_inc(loaded_w, 16)
                        n += 16
                        for k, v in (("b1c", b1), ("g1c", g1), ("be1c", be1), ("b2c", b2), ("g2c", g2), ("be2c", be2)):
                            sp.dma_start(bn_in[k][:], v).then_inc(loaded_w, 16)
                            n += 16
                        for t, v in ((bih, b_ih), (bhh, b_hh)):
                            sp.dma_start(t[:], v).then_inc(loaded_w, 16)
                            n += 16
                        assert n == 16 * LOADS_W
                        sp.wait_ge(tab_ready, 1)
                        sp.dma_start(dinv_tab.rearrange("(p a) o -> p (a o)", p=P), dinv[:]).then_inc(tab_stored, 16)
                        sp.wait_ge(tab_stored, 16)

                    @block.gpsimd
                    def _(pool):
                        nc.gpsimd.iota(row_i[:], pattern=[[1, NCOL]], base=0, channel_multiplier=0)
                        nc.gpsimd.memset(ones[:], 1.0)
                        nc.gpsimd.memset(eps[:], EPS)
                        nc.gpsimd.memset(zero[:], 0.0)
                        nc.gpsimd.iota(pidx_i[:], pattern=[[1, 1]], base=0, channel_multiplier=1).then_inc(iotas, 1)

                    @block.scalar
                    def _(act):
                        act.wait_ge(deg_ready, 1)
                        nc.scalar.activation(big[:], deg[:], ACT.Sqrt).then_inc(sd_ready, 1)

                    @block.vector
                    def _(dve):
                        done = [0]

                        def link(ins):
                            done[0] += 1
                            ins.then_inc(dve_step, 1)
                            dve.wait_ge(dve_step, done[0])

                        v = nc.vector
                        dve.wait_ge(iotas, 1)
                        link(v.tensor_copy(pidx[:], pidx_i[:]))
                        v.tensor_copy(row_h[:], row_i[:])
                        link(v.tensor_copy(row_f[:], row_i[:, 0:P]))
                        v.tensor_scalar(tri[:], row_f[:], pidx[:], None, ALU.is_gt)
                        v.tensor_scalar(last[:], pidx[:], float(P - 1), None, ALU.is_equal)
                        v.tensor_scalar(node_mask[:], pidx[:], float(TAIL), None, ALU.is_lt)
                        link(v.tensor_scalar(ident[:], row_f[:], pidx[:], None, ALU.is_equal))
                        v.sem_inc(consts, 1)

                        def column(node_i):
                            v.tensor_scalar(ia[:], node_i[:], 9, 2, ALU.logical_shift_right, ALU.logical_shift_left)
                            link(v.tensor_scalar(ib[:], node_i[:], 3, None, ALU.bitwise_and))
                            v.tensor_scalar(ic[:], node_i[:], 2, P - 1, ALU.logical_shift_right, ALU.bitwise_and)
                            link(v.tensor_tensor(ia[:], ia[:], ib[:], ALU.bitwise_or))

                        dve.wait_ge(loaded_dst, 16)
                        column(dst_i)
                        v.tensor_copy(dst_a[:], ia[:])
                        v.tensor_copy(dst_f[:], dst_i[:])
                        link(v.tensor_copy(dst_p[:], ic[:]))

                        def hot(t, u):
                            if live(t, NG):
                                if after(t):
                                    dve.wait_ge(hists, t - 1)
                                v.tensor_tensor(hot_a[u][:], row_h[:].unsqueeze(1).broadcast_to([P, Q, NCOL]),
                                                dst_a[:, ds(t * Q, Q)].unsqueeze(2).broadcast_to([P, Q, NCOL]),
                                                ALU.is_equal)
                                v.tensor_tensor(hot_p[u][:], row_h[:, 0:P].unsqueeze(1).broadcast_to([P, Q, P]),
                                                dst_p[:, ds(t * Q, Q)].unsqueeze(2).broadcast_to([P, Q, P]),
                                                ALU.is_equal).then_inc(hots, 1)

                        steps(dve, NG, 0, hot)

                        for i, k in enumerate(("ih", "hh")):
                            dve.wait_ge(wts, i + 1)
                            link(v.tensor_copy(whi[k][:], ps_w[i][:]))
                            v.tensor_tensor(wlo[k][:], ps_w[i][:], whi[k][:].bitcast(F32), ALU.subtract)
                        dve.wait_ge(loaded_w, 16 * LOADS_W)
                        v.tensor_tensor(brz[:], bih[:], bhh[:], ALU.add)

                        v.memset(carry_f[:, 0:1], -1.0)
                        link(v.tensor_scalar(carry_f[:, 1:NT], dst_f[:, 0:NT - 1], 1.0, None, ALU.add))
                        link(v.tensor_scalar(carry_f[:, 1:NT], carry_f[:, 1:NT], last[:], -1.0, ALU.mult, ALU.add))

                        dve.wait_ge(loaded_src, 16)
                        column(src_i)
                        v.tensor_copy(fa[:], ia[:])
                        link(v.tensor_copy(fb[:], ic[:]))
                        link(v.scalar_tensor_tensor(fa[:], fb[:], float(NCOL), fa[:], ALU.mult, ALU.add))
                        link(v.tensor_copy(src_pos[:], fa[:]))

                        dve.wait_ge(hists, NG)
                        c2 = cnt[:].rearrange("p b q -> p (b q)")
                        link(v.tensor_copy(c2, ps_c[:]))
                        v.tensor_scalar(deg[:], c2, 1.0, None, ALU.add).then_inc(deg_ready, 1)
                        v.tensor_scalar(has[:], c2, 0.5, None, ALU.is_gt)
                        v.tensor_copy(cum[:, :, 0], cnt[:, :, 0])
                        v.tensor_reduce(blk_sum[:], cnt[:], AX.X, ALU.add).then_inc(sums, 1)
                        done[0] += 1
                        v.sem_inc(dve_step, 1)
                        dve.wait_ge(sums, 1)
                        for q in range(1, Q):
                            link(v.tensor_tensor(cum[:, :, q], cum[:, :, q - 1], cnt[:, :, q], ALU.add))
                        dve.wait_ge(sums_ps, 1)
                        link(v.tensor_copy(tot[:], ps_b[:, 1, :]))
                        link(v.tensor_tensor_scan(run[:], ones[:, 0:NB], tot[:], 0.0, ALU.mult, ALU.add))
                        link(v.tensor_tensor(run[:], run[:], tot[:], ALU.subtract))
                        link(v.tensor_tensor(base[:], ps_b[:, 0, :], run[:], ALU.add))
                        link(v.tensor_tensor(cum[:], cum[:], base[:].unsqueeze(2).broadcast_to([P, NB, Q]), ALU.add))
                        dve.wait_ge(sd_ready, 1)
                        link(v.reciprocal(dinv[:], big[:]))
                        link(v.tensor_scalar(dinv[:, NCOL - Q:NCOL], dinv[:, NCOL - Q:NCOL], node_mask[:], None,
                                             ALU.mult))
                        v.sem_inc(tab_ready, 1)
                        v.tensor_tensor(dinv2[:], dinv[:], dinv[:], ALU.mult)
                        d3 = dinv[:].rearrange("p (b q) -> p b q", q=Q)
                        h3 = has[:].rearrange("p (b q) -> p b q", q=Q)
                        v.tensor_copy(dh[:, :, 0, :], d3)
                        v.tensor_tensor(dh[:, :, 1, :], d3, h3, ALU.mult)
                        link(v.tensor_scalar(big[:], has[:], -1.0e6, 1.0e6 - 1.0, ALU.mult, ALU.add))
                        link(v.tensor_tensor(big[:], big[:], cum[:].rearrange("p b q -> p (b q)"), ALU.add))
                        link(v.tensor_copy(end_index[:], big[:]))

                    @block.tensor
                    def _(pe):
                        pe.wait_ge(consts, 1)
                        pe.wait_ge(loaded_w, 16 * LOADS_W)
                        for i, k in enumerate(("ih", "hh")):
                            for c in range(G3):
                                for h in range(KD):
                                    t = nc.tensor.transpose(ps_w[i][:, h, c * P:(c + 1) * P],
                                                            wraw[k][:, c, h * P:(h + 1) * P], ident[:])
                            t.then_inc(wts, 1)

                        def hist(t, u):
                            pe.wait_ge(hots, t + 1)
                            for k in range(Q):
                                m = nc.tensor.matmul(ps_c[:], hot_p[u][:, k, :], hot_a[u][:, k, :],
                                                     start=isinstance(t, int) and t == 0 and k == 0,
                                                     stop=isinstance(t, int) and t == NG - 1 and k == Q - 1)
                            m.then_inc(hists, 1)

                        steps(pe, NG, 0, hist)
                        pe.wait_ge(sums, 1)
                        nc.tensor.matmul(ps_b[:, 0, :], tri[:], blk_sum[:], start=True, stop=True)
                        nc.tensor.matmul(ps_b[:, 1, :], ones[:], blk_sum[:], start=True, stop=True).then_inc(sums_ps, 1)

        LOADS_W = 13

        def edges(tag, table, layernorm, edge_dinv, relations):
            rows = table.shape[0]
            with ExitStack() as ctx:
                def sb(name, shape, dt=F32):
                    return ctx.enter_context(nc.sbuf_tensor(f"{tag}_{name}", shape, dt))

                def sem(name):
                    return ctx.enter_context(nc.semaphore(f"{tag}_{name}"))

                def two(name, shape, dt=F32):
                    return [sb(f"{name}{i}", shape, dt) for i in range(2)]

                dstb = two("dstb", [P, Q, P], I32)
                eq = two("eq", [P, Q, P])
                cr = two("cr", [P, Q, P])
                idx = two("idx", [P, Q], I32)
                msg = two("msg", [P, Q, D])
                res = two("res", [P, Q, D])
                dst_loaded = [sem(f"dst_loaded{i}") for i in range(2)]
                rows_in = [sem(f"rows_in{i}") for i in range(2)]
                stored = [sem(f"stored{i}") for i in range(2)]
                idx_ready, eq_ready, eq_used, cr_used, summed, msg_ready = (
                    sem(n) for n in ("idx_ready", "eq_ready", "eq_used", "cr_used", "summed", "msg_ready"))
                if layernorm:
                    bs = two("bs", [P, Q, 6])
                    mv = two("mv", [P, Q, 2])
                    sd = two("sd", [P, Q])
                    sc = two("sc", [P, Q])
                    nb = two("nb", [P, Q])
                    stat_step, sd_ready, sc_step, normed = (
                        sem(n) for n in ("stat_step", "sd_ready", "sc_step", "normed"))
                if edge_dinv:
                    dpos = two("dpos", [P, Q], I32)
                    dsrc = two("dsrc", [P, Q])
                    dinv_in = [sem(f"dinv_in{i}") for i in range(2)]
                if relations:
                    typ = two("typ", [NREL, Q, P], I32)
                    hot = two("hot", [NREL, Q, P])
                    ps_rel = ctx.enter_context(nc.psum_tensor(f"{tag}_ps_rel", [P, Q, D], F32))
                    hot_ready, rel_ready = sem("hot_ready"), sem("rel_ready")
                bank = [ctx.enter_context(nc.psum_tensor(f"{tag}_bank{k}", [P, 512], F32)) for k in range(Q)]
                n_dst = 32 if relations else 16

                with nc.Block() as block:
                    @block.sync
                    def _(sp):
                        def step(t, u):
                            g, s = t, u
                            if live(g, NG):
                                if after(g):
                                    sp.wait_ge(eq_ready, g - 1)
                                sp.dma_start(dstb[s][:].rearrange("p k e -> p (k e)"),
                                             dst_row[0:1, ds(g * BLK, BLK)].broadcast_to([P, BLK])
                                             ).then_inc(dst_loaded[s], 16)
                                if relations:
                                    if after(g):
                                        sp.wait_ge(hot_ready, g - 1)
                                    sp.dma_start(typ[s][:].rearrange("p k e -> p (k e)"),
                                                 type_row[0:1, ds(g * BLK, BLK)].broadcast_to([NREL, BLK])
                                                 ).then_inc(dst_loaded[s], 16)
                            g = t - 3
                            s = (u - 3) % 2
                            if live(g, NG):
                                sp.wait_ge(summed, g * Q + Q)
                                sp.dma_start(seg_t[:, ds(g * Q, Q), :], res[s][:]).then_inc(stored[s], 16)

                        steps(sp, NG, 3, step)
                        sp.wait_ge(stored[0], 16 * ((NG + 1) // 2))
                        sp.wait_ge(stored[1], 16 * (NG // 2))

                    @block.gpsimd
                    def _(pool):
                        bound = nc.gpsimd.to_reg(rows - 1)
                        if edge_dinv:
                            bound_d = nc.gpsimd.to_reg(P * NCOL - 1)

                        def step(t, s):
                            g = t
                            if after(g):
                                pool.wait_ge(eq_used, g * Q - Q)
                            if edge_dinv:
                                nc.gpsimd.tensor_copy(dpos[s][:], src_pos[:, ds(g * Q, Q)])
                            nc.gpsimd.tensor_copy(idx[s][:], src_i[:, ds(g * Q, Q)]).then_inc(idx_ready, 1)
                            pool.wait_ge(idx_ready, g + 1)
                            pool.sem_inc(issuing, 1)
                            for k in range(Q):
                                nc.gpsimd.indirect_dma_start(
                                    msg[s][:, k, :], None, table,
                                    bass.IndirectOffsetOnAxis(ap=idx[s][:, k:k + 1], axis=0),
                                    bounds_check=bound, oob_is_err=False).then_inc(rows_in[s], 16)
                            if edge_dinv:
                                for k in range(Q):
                                    nc.gpsimd.indirect_dma_start(
                                        dsrc[s][:, k:k + 1], None, dinv_tab,
                                        bass.IndirectOffsetOnAxis(ap=dpos[s][:, k:k + 1], axis=0),
                                        bounds_check=bound_d, oob_is_err=False).then_inc(dinv_in[s], 16)

                        steps(pool, NG, 0, step)

                    @block.scalar
                    def _(act):
                        def step(t, u):
                            g, s = t - 2, u % 2
                            def evac(k):
                                act.wait_ge(cr_used, g * Q + k + 1)
                                nc.scalar.activation(res[s][:, k, :], bank[k][:, 0:D], ACT.Copy).then_inc(summed, 1)

                            if live(g, NG):
                                if after(g):
                                    act.wait_ge(stored[s], half(g) * 16)
                                evac(0)
                                evac(1)
                            g1, s1 = t - 1, (u - 1) % 2
                            if layernorm and live(g1, NG):
                                act.wait_ge(stat_step, g1 * 2 + 2)
                                nc.scalar.activation(sd[s1][:], mv[s1][:, :, 1], ACT.Sqrt,
                                                     bias=eps[:]).then_inc(sd_ready, 1)
                                act.wait_ge(sc_step, g1 * 3 + 3)
                                for k in range(Q):
                                    i = nc.scalar.activation(msg[s1][:, k, :], msg[s1][:, k, :], ACT.Relu,
                                                             bias=nb[s1][:, k:k + 1], scale=sc[s1][:, k:k + 1])
                                i.then_inc(normed, 1)
                            if live(g, NG):
                                evac(2)
                                evac(3)

                        steps(act, NG, 2, step)

                    @block.vector
                    def _(dve):
                        v = nc.vector
                        v.memset(res[1][:, Q - 1, :], 0.0).then_inc(msg_ready, 1)

                        def step(t, u):
                            g, s = t - 1, (u - 1) % 2
                            if not live(g, NG):
                                return
                            if layernorm:
                                dve.wait_ge(rows_in[s], half(g) * 16 * Q + 16 * Q)
                                for k in range(Q):
                                    i = v.bn_stats(bs[s][:, k, :], msg[s][:, k, :])
                                i.then_inc(stat_step, 1)
                            dve.wait_ge(dst_loaded[s], half(g) * n_dst + n_dst)
                            if after(g):
                                dve.wait_ge(cr_used, g * Q - Q)
                            v.tensor_tensor(eq[s][:], dstb[s][:],
                                            dst_f[:, ds(g * Q, Q)].unsqueeze(2).broadcast_to([P, Q, P]), ALU.is_equal)
                            if layernorm:
                                dve.wait_ge(stat_step, g * 2 + 1)
                            v.tensor_tensor(cr[s][:], dstb[s][:],
                                            carry_f[:, ds(g * Q, Q)].unsqueeze(2).broadcast_to([P, Q, P]),
                                            ALU.is_equal).then_inc(eq_ready, 1)
                            if relations:
                                v.tensor_scalar(hot[s][:], typ[s][:], pidx[0:NREL, :], None,
                                                ALU.is_equal).then_inc(hot_ready, 1)
                            if layernorm:
                                for k in range(Q):
                                    i = v.bn_aggr(mv[s][:, k, :], bs[s][:, k, :])
                                i.then_inc(stat_step, 1)
                                dve.wait_ge(sd_ready, g + 1)
                                v.reciprocal(sc[s][:], sd[s][:]).then_inc(sc_step, 1)
                                dve.wait_ge(sc_step, g * 3 + 1)
                                if edge_dinv:
                                    dve.wait_ge(dinv_in[s], half(g) * 16 * Q + 16 * Q)
                                    v.tensor_tensor(sc[s][:], sc[s][:], dsrc[s][:], ALU.mult).then_inc(sc_step, 1)
                                else:
                                    v.sem_inc(sc_step, 1)
                                dve.wait_ge(sc_step, g * 3 + 2)
                                v.scalar_tensor_tensor(nb[s][:], mv[s][:, :, 0], -1.0, sc[s][:],
                                                       ALU.mult, ALU.mult).then_inc(sc_step, 1)
                            if relations:
                                dve.wait_ge(rel_ready, g + 1)
                                dve.wait_ge(normed, g + 1)
                                v.tensor_tensor(msg[s][:], msg[s][:], ps_rel[:], ALU.add).then_inc(msg_ready, 1)

                        steps(dve, NG, 1, step)

                    @block.tensor
                    def _(pe):
                        pe.wait_ge(msg_ready, 1)

                        def inside(g, s, k):
                            if k == 0:
                                pe.wait_ge(eq_ready, g + 1)
                                if relations:
                                    pe.wait_ge(msg_ready, g + 2)
                                elif layernorm:
                                    pe.wait_ge(normed, g + 1)
                                else:
                                    pe.wait_ge(rows_in[s], half(g) * 16 * Q + 16 * Q)
                            if not isinstance(g, int) or g >= 1:
                                pe.wait_ge(summed, g * Q + k - 3)
                            nc.tensor.matmul(bank[k][:, 0:D], eq[s][:, k, :], msg[s][:, k, :],
                                             start=True, stop=False).then_inc(eq_used, 1)

                        def carry(g, s, k):
                            if not isinstance(g, int) or g * Q + k >= 1:
                                pe.wait_ge(summed, g * Q + k)
                            before = res[s][:, k - 1, :] if k else res[1 - s][:, Q - 1, :]
                            nc.tensor.matmul(bank[k][:, 0:D], cr[s][:, k, :], before,
                                             start=False, stop=True).then_inc(cr_used, 1)

                        def step(t, u):
                            g1, s1 = t - 1, (u - 1) % 2
                            if relations and live(g1, NG):
                                pe.wait_ge(hot_ready, g1 + 1)
                                if not isinstance(g1, int) or g1 >= 1:
                                    pe.wait_ge(msg_ready, g1 + 1)
                                for k in range(Q):
                                    i = nc.tensor.matmul(ps_rel[:, k, :], hot[s1][:, k, :], rel_sb[:],
                                                         start=True, stop=True)
                                i.then_inc(rel_ready, 1)
                            g, s = t - 2, u % 2
                            for k in range(Q):
                                if k < 2:
                                    if live(g, NG):
                                        inside(g, s, k + 2)
                                elif live(g1, NG):
                                    inside(g1, s1, k - 2)
                                if live(g, NG):
                                    carry(g, s, k)

                        steps(pe, NG, 2, step)

        def half(b):
            return b // 2 if isinstance(b, int) else b >> 1

        def batch_norm_coefficients(tag, stats, b_c, g_c, be_c):
            r = NPAD / N
            with ExitStack() as ctx:
                mv = ctx.enter_context(nc.sbuf_tensor(f"{tag}_mv", [P, KD, 2], F32))
                m = ctx.enter_context(nc.sbuf_tensor(f"{tag}_m", [P, KD], F32))
                w = ctx.enter_context(nc.sbuf_tensor(f"{tag}_w", [P, KD], F32))
                dve_step = ctx.enter_context(nc.semaphore(f"{tag}_dve_step"))
                var_ready = ctx.enter_context(nc.semaphore(f"{tag}_var_ready"))
                sd_ready = ctx.enter_context(nc.semaphore(f"{tag}_sd_ready"))
                with nc.Block() as block:
                    @block.scalar
                    def _(act):
                        act.wait_ge(var_ready, 1)
                        nc.scalar.activation(w[:], w[:], ACT.Sqrt, bias=eps[:]).then_inc(sd_ready, 1)

                    @block.vector
                    def _(dve):
                        done = [0]

                        def link(ins):
                            done[0] += 1
                            ins.then_inc(dve_step, 1)
                            dve.wait_ge(dve_step, done[0])

                        v = nc.vector
                        v.bn_aggr(mv[:, 0, :], stats[:, 0, :, :].rearrange("p b k -> p (b k)"))
                        link(v.bn_aggr(mv[:, 1, :], stats[:, 1, :, :].rearrange("p b k -> p (b k)")))
                        link(v.tensor_tensor(w[:], mv[:, :, 0], mv[:, :, 0], ALU.mult))
                        link(v.scalar_tensor_tensor(w[:], w[:], -(r - 1.0), mv[:, :, 1], ALU.mult, ALU.add))
                        v.tensor_scalar(w[:], w[:], r, None, ALU.mult).then_inc(var_ready, 1)
                        link(v.scalar_tensor_tensor(m[:], mv[:, :, 0], r, b_c[:], ALU.mult, ALU.add))
                        dve.wait_ge(sd_ready, 1)
                        link(v.reciprocal(w[:], w[:]))
                        link(v.tensor_tensor(bn_s[:], w[:], g_c[:], ALU.mult))
                        link(v.tensor_tensor(m[:], b_c[:], m[:], ALU.subtract))
                        link(v.tensor_tensor(m[:], m[:], bn_s[:], ALU.mult))
                        link(v.tensor_tensor(bn_t[:], m[:], be_c[:], ALU.add))

        def load_rows(sp, dst, rows, b, arrived):
            if isinstance(b, int) and b == NB - 1 and rows.shape[0] != NB * P:
                sp.dma_start(dst[0:TAIL], rows[b * P:b * P + TAIL, :]).then_inc(arrived, 16)
            else:
                sp.dma_start(dst[:], rows[ds(b * P, P), :]).then_inc(arrived, 16)

        def flat(t):
            return t[:].rearrange("p q d -> p (q d)")

        def aggregate(tag, src, layernorm, dst_t, stats):
            first = layernorm
            with ExitStack() as ctx:
                def sb(name, shape, dt=F32):
                    return ctx.enter_context(nc.sbuf_tensor(f"{tag}_{name}", shape, dt))

                def ps(name):
                    return ctx.enter_context(nc.psum_tensor(f"{tag}_{name}", [P, KD, BLK], F32))

                def sem(name):
                    return ctx.enter_context(nc.semaphore(f"{tag}_{name}"))

                def two(name, shape, dt=F32):
                    return [sb(f"{name}{i}", shape, dt) for i in range(2)]

                xb = two("xb", [P, Q, D])
                own = two("own", [P, Q, D])
                gath = two("gath", [P, Q, D])
                idx = two("idx", [P, Q], I32)
                scal = two("scal", [P, 2, Q])
                ob = two("ob", [P, KD, BLK])
                ps_t = [ps(f"ps_t{i}") for i in range(2)]
                x_in = [sem(f"x_in{i}") for i in range(2)]
                seg_in = [sem(f"seg_in{i}") for i in range(2)]
                stored = [sem(f"stored{i}") for i in range(2)]
                (cleared, idx_ready, scal_ready, own_ready, combined, turned, copied, counted) = (
                    sem(n) for n in ("cleared", "idx_ready", "scal_ready", "own_ready", "combined", "turned",
                                     "copied", "counted"))
                if first:
                    bs = two("bs", [P, Q, 6])
                    mv = two("mv", [P, Q, 2])
                    sd = two("sd", [P, Q])
                    sc = two("sc", [P, Q])
                    nb = two("nb", [P, Q])
                    ht = two("ht", [P, KD, BLK])
                    ps_m = [ps(f"ps_m{i}") for i in range(2)]
                    stat_step, sd_ready, sc_step, ht_ready, multiplied = (
                        sem(n) for n in ("stat_step", "sd_ready", "sc_step", "ht_ready", "multiplied"))
                made, ps_o = (multiplied, ps_m) if first else (turned, ps_t)
                lag_o = 4 if first else 3

                with nc.Block() as block:
                    @block.sync
                    def _(sp):
                        def step(t, u):
                            if live(t, NB):
                                if isinstance(t, int) and t < 2 and first:
                                    sp.wait_ge(cleared, 1)
                                if after(t):
                                    sp.wait_ge(own_ready, t - 1)
                                load_rows(sp, xb[u % 2][:].rearrange("p q d -> p (q d)"), src, t, x_in[u % 2])
                            b, s = t - lag_o, (u - lag_o) % 2
                            if live(b, NB):
                                sp.wait_ge(copied, b + 1)
                                sp.dma_start(dst_t[ds(b * P, P), :],
                                             ob[s][:].rearrange("p c n -> p (c n)")).then_inc(stored[s], 16)

                        steps(sp, NB, lag_o, step)
                        sp.wait_ge(stored[0], 16 * (NB // 2))
                        sp.wait_ge(stored[1], 16 * (NB // 2))

                    @block.gpsimd
                    def _(pool):
                        for i in range(2):
                            if first:
                                nc.gpsimd.memset(xb[i][:], 0.0)
                            nc.gpsimd.memset(gath[i][:], 0.0).then_inc(idx_ready, 1)
                        pool.wait_ge(idx_ready, 2)
                        pool.sem_inc(cleared, 1)
                        bound = nc.gpsimd.to_reg(E - 1)

                        def step(t, u):
                            if after(t):
                                pool.wait_ge(combined, t - 1)
                            nc.gpsimd.tensor_copy(idx[u][:], end_index[:, ds(t * Q, Q)]).then_inc(idx_ready, 1)
                            pool.wait_ge(idx_ready, t + 3)
                            pool.sem_inc(issuing, 1)
                            for q in range(Q):
                                nc.gpsimd.indirect_dma_start(
                                    gath[u][:, q, :], None, seg,
                                    bass.IndirectOffsetOnAxis(ap=idx[u][:, q:q + 1], axis=0),
                                    bounds_check=bound, oob_is_err=False).then_inc(seg_in[u], 16)

                        steps(pool, NB, 0, step)

                    @block.scalar
                    def _(act):
                        def step(t, u):
                            b, s = t - 2, u % 2
                            if live(b, NB):
                                if after(b):
                                    act.wait_ge(turned, b - 1)
                                act.wait_ge(scal_ready, b + 1)
                                if not first:
                                    act.wait_ge(x_in[s], half(b) * 16 + 16)
                                for q in range(Q):
                                    if first:
                                        i = nc.scalar.activation(own[s][:, q, :], xb[s][:, q, :], ACT.Relu,
                                                                 bias=nb[s][:, q:q + 1], scale=sc[s][:, q:q + 1])
                                    else:
                                        i = nc.scalar.activation(own[s][:, q, :], xb[s][:, q, :], ACT.Copy,
                                                                 scale=scal[s][:, 0, q:q + 1])
                                i.then_inc(own_ready, 1)
                            b, s = t - lag_o, (u - lag_o) % 2
                            if live(b, NB):
                                act.wait_ge(made, b + 1)
                                if after(b):
                                    act.wait_ge(counted, b - 1)
                                    act.wait_ge(stored[s], half(b) * 16)
                                nc.scalar.activation(ob[s][:], ps_o[s][:], ACT.Copy).then_inc(copied, 1)
                            if first:
                                b, s = t - 1, (u - 1) % 2
                                if live(b, NB):
                                    act.wait_ge(stat_step, 2 * b + 2)
                                    nc.scalar.activation(sd[s][:], mv[s][:, :, 1], ACT.Sqrt,
                                                         bias=eps[:]).then_inc(sd_ready, 1)
                                b, s = t - 2, u % 2
                                if live(b, NB):
                                    act.wait_ge(turned, b + 1)
                                    if after(b):
                                        act.wait_ge(multiplied, b - 1)
                                    nc.scalar.activation(ht[s][:], ps_t[s][:], ACT.Copy).then_inc(ht_ready, 1)

                        steps(act, NB, lag_o, step)

                    @block.vector
                    def _(dve):
                        v = nc.vector

                        def step(t, u):
                            b, s = t - 1, (u - 1) % 2
                            if first and live(b, NB):
                                dve.wait_ge(x_in[s], half(b) * 16 + 16)
                                for q in range(Q):
                                    i = v.bn_stats(bs[s][:, q, :], xb[s][:, q, :])
                                i.then_inc(stat_step, 1)
                                if after(b):
                                    dve.wait_ge(combined, b - 1)
                                dve.wait_ge(stat_step, 2 * b + 1)
                                v.tensor_copy(scal[s][:].rearrange("p a q -> p (a q)"),
                                              dh[:, ds(b, 1), :, :].rearrange("p b a q -> p (b a q)"))
                                for q in range(Q):
                                    i = v.bn_aggr(mv[s][:, q, :], bs[s][:, q, :])
                                i.then_inc(stat_step, 1)
                            b, s = t - 2, u % 2
                            if live(b, NB):
                                dve.wait_ge(own_ready, b + 1)
                                dve.wait_ge(seg_in[s], half(b) * 16 * Q + 16 * Q)
                                for q in range(Q):
                                    i = v.scalar_tensor_tensor(own[s][:, q, :], gath[s][:, q, :],
                                                               scal[s][:, 1, q:q + 1], own[s][:, q, :],
                                                               ALU.mult, ALU.add)
                                i.then_inc(combined, 1)
                            b, s = t - 1, (u - 1) % 2
                            if live(b, NB):
                                if first:
                                    dve.wait_ge(sd_ready, b + 1)
                                    v.reciprocal(sc[s][:], sd[s][:]).then_inc(sc_step, 1)
                                    dve.wait_ge(sc_step, 2 * b + 1)
                                    v.tensor_tensor(sc[s][:], sc[s][:], dinv2[:, ds(b * Q, Q)],
                                                    ALU.mult).then_inc(sc_step, 1)
                                    dve.wait_ge(sc_step, 2 * b + 2)
                                    v.scalar_tensor_tensor(nb[s][:], mv[s][:, :, 0], -1.0, sc[s][:],
                                                           ALU.mult, ALU.mult).then_inc(scal_ready, 1)
                                else:
                                    v.tensor_copy(scal[s][:].rearrange("p a q -> p (a q)"),
                                                  dh[:, ds(b, 1), :, :].rearrange("p b a q -> p (b a q)")
                                                  ).then_inc(scal_ready, 1)
                            b, s = t - lag_o, (u - lag_o) % 2
                            if live(b, NB):
                                dve.wait_ge(copied, b + 1)
                                for c in range(KD):
                                    i = v.bn_stats(stats[:, c, ds(b, 1), :].rearrange("p b k -> p (b k)"),
                                                   ob[s][:, c, :])
                                i.then_inc(counted, 1)

                        steps(dve, NB, lag_o, step)

                    @block.tensor
                    def _(pe):
                        def step(t, u):
                            b, s = t - 3, (u - 3) % 2
                            if first and live(b, NB):
                                pe.wait_ge(ht_ready, b + 1)
                                if after(b):
                                    pe.wait_ge(copied, b - 1)
                                for o in range(KD):
                                    for c in range(KD):
                                        i = nc.tensor.matmul(ps_m[s][:, o, :], w1[:, c, o * P:(o + 1) * P],
                                                             ht[s][:, c, :], start=(c == 0), stop=(c == KD - 1))
                                i.then_inc(multiplied, 1)
                            b, s = t - 2, u % 2
                            if live(b, NB):
                                pe.wait_ge(combined, b + 1)
                                if after(b):
                                    if first:
                                        pe.wait_ge(ht_ready, b - 1)
                                    else:
                                        pe.wait_ge(copied, b - 1)
                                for c in range(KD):
                                    for q in range(Q):
                                        i = nc.tensor.transpose(ps_t[s][:, c, q * P:(q + 1) * P],
                                                                own[s][:, q, c * P:(c + 1) * P], ident[:])
                                i.then_inc(turned, 1)

                        steps(pe, NB, 3, step)

        def lin2():
            with ExitStack() as ctx:
                def sb(name, shape, dt=F32):
                    return ctx.enter_context(nc.sbuf_tensor(f"l2_{name}", shape, dt))

                def sem(name):
                    return ctx.enter_context(nc.semaphore(f"l2_{name}"))

                zb = [sb(f"zb{i}", [P, KD, BLK]) for i in range(2)]
                hb = [sb(f"hb{i}", [P, KD, BLK]) for i in range(2)]
                gb = [sb(f"gb{i}", [P, Q, D]) for i in range(2)]
                ps_g = [ctx.enter_context(nc.psum_tensor(f"l2_ps{i}", [P, Q, D], F32)) for i in range(2)]
                z_in = [sem(f"z_in{i}") for i in range(2)]
                stored = [sem(f"stored{i}") for i in range(2)]
                h_ready, multiplied, scaled = (sem(n) for n in ("h_ready", "multiplied", "scaled"))
                with nc.Block() as block:
                    @block.sync
                    def _(sp):
                        def step(t, u):
                            if live(t, NB):
                                if after(t):
                                    sp.wait_ge(h_ready, t - 1)
                                sp.dma_start(zb[u % 2][:].rearrange("p c n -> p (c n)"),
                                             o1t[ds(t * P, P), :]).then_inc(z_in[u % 2], 16)
                            b, s = t - 2, u % 2
                            if live(b, NB):
                                sp.wait_ge(scaled, b + 1)
                                sp.dma_start(g2_r[ds(b * P, P), :],
                                             gb[s][:].rearrange("p q d -> p (q d)")).then_inc(stored[s], 16)

                        steps(sp, NB, 2, step)
                        sp.wait_ge(stored[0], 16 * (NB // 2))
                        sp.wait_ge(stored[1], 16 * (NB // 2))

                    @block.scalar
                    def _(act):
                        def step(b, s):
                            act.wait_ge(z_in[s], half(b) * 16 + 16)
                            if after(b):
                                act.wait_ge(multiplied, b - 1)
                            for c in range(KD):
                                i = nc.scalar.activation(hb[s][:, c, :], zb[s][:, c, :], ACT.Relu,
                                                         bias=bn_t[:, c:c + 1], scale=bn_s[:, c:c + 1])
                            i.then_inc(h_ready, 1)

                        steps(act, NB, 0, step)

                    @block.tensor
                    def _(pe):
                        def step(b, s):
                            pe.wait_ge(h_ready, b + 1)
                            if after(b):
                                pe.wait_ge(scaled, b - 1)
                            for q in range(Q):
                                for c in range(KD):
                                    i = nc.tensor.matmul(ps_g[s][:, q, :], hb[s][:, c, q * P:(q + 1) * P],
                                                         w2[:, c, :], start=(c == 0), stop=(c == KD - 1))
                            i.then_inc(multiplied, 1)

                        steps(pe, NB, 0, step)

                    @block.vector
                    def _(dve):
                        def step(b, s):
                            dve.wait_ge(multiplied, b + 1)
                            if after(b):
                                dve.wait_ge(stored[s], half(b) * 16)
                            nc.vector.tensor_tensor(gb[s][:], ps_g[s][:],
                                                    dinv[:, ds(b * Q, Q)].unsqueeze(2).broadcast_to([P, Q, D]),
                                                    ALU.mult).then_inc(scaled, 1)

                        steps(dve, NB, 0, step)

        def residual():
            with ExitStack() as ctx:
                def sb(name, shape, dt=F32):
                    return ctx.enter_context(nc.sbuf_tensor(f"rs_{name}", shape, dt))

                def sem(name):
                    return ctx.enter_context(nc.semaphore(f"rs_{name}"))

                zb = [sb(f"zb{i}", [P, KD, BLK]) for i in range(2)]
                hb = [sb(f"hb{i}", [P, KD, BLK]) for i in range(2)]
                xb = [sb(f"xb{i}", [P, Q, D]) for i in range(2)]
                x1b = [sb(f"x1b{i}", [P, Q, D]) for i in range(2)]
                bs = [sb(f"bs{i}", [P, Q, 6]) for i in range(2)]
                mvb = [sb(f"mvb{i}", [P, Q, 2]) for i in range(2)]
                sd = sb("sd", [P, NCOL])
                ps_h = [ctx.enter_context(nc.psum_tensor(f"rs_ps{i}", [P, Q, D], F32)) for i in range(2)]
                z_in = [sem(f"z_in{i}") for i in range(2)]
                x_in = [sem(f"x_in{i}") for i in range(2)]
                stored = [sem(f"stored{i}") for i in range(2)]
                h_ready, turned, added, counted, aggregated, kept, sd_ready, inv_ready = (
                    sem(n) for n in ("h_ready", "turned", "added", "counted", "aggregated", "kept", "sd_ready", "inv_ready"))
                with nc.Block() as block:
                    @block.sync
                    def _(sp):
                        def step(t, u):
                            if live(t, NB):
                                s = u % 2
                                if after(t):
                                    sp.wait_ge(h_ready, t - 1)
                                sp.dma_start(zb[s][:].rearrange("p c n -> p (c n)"),
                                             o2t[ds(t * P, P), :]).then_inc(z_in[s], 16)
                                if after(t):
                                    sp.wait_ge(added, t - 1)
                                load_rows(sp, xb[s][:].rearrange("p q d -> p (q d)"), x_r, t, x_in[s])
                            b, s = t - 2, u % 2
                            if live(b, NB):
                                sp.wait_ge(added, b + 1)
                                sp.dma_start(x1_r[ds(b * P, P), :],
                                             x1b[s][:].rearrange("p q d -> p (q d)")).then_inc(stored[s], 16)

                        steps(sp, NB, 2, step)
                        sp.wait_ge(stored[0], 16 * (NB // 2))
                        sp.wait_ge(stored[1], 16 * (NB // 2))

                    @block.scalar
                    def _(act):
                        def step(b, s):
                            act.wait_ge(z_in[s], half(b) * 16 + 16)
                            if after(b):
                                act.wait_ge(turned, b - 1)
                            for c in range(KD):
                                i = nc.scalar.activation(hb[s][:, c, :], zb[s][:, c, :], ACT.Relu,
                                                         bias=bn_t[:, c:c + 1], scale=bn_s[:, c:c + 1])
                            i.then_inc(h_ready, 1)

                        steps(act, NB, 0, step)
                        act.wait_ge(kept, NB)
                        nc.scalar.activation(sd[:], mv1[:, :, 1], ACT.Sqrt, bias=eps[:]).then_inc(sd_ready, 1)

                    @block.tensor
                    def _(pe):
                        def step(b, s):
                            pe.wait_ge(h_ready, b + 1)
                            if after(b):
                                pe.wait_ge(added, b - 1)
                            for q in range(Q):
                                for c in range(KD):
                                    i = nc.tensor.transpose(ps_h[s][:, q, c * P:(c + 1) * P],
                                                            hb[s][:, c, q * P:(q + 1) * P], ident[:])
                            i.then_inc(turned, 1)

                        steps(pe, NB, 0, step)

                    @block.vector
                    def _(dve):
                        v = nc.vector

                        def keep_stats(b, s):
                            dve.wait_ge(aggregated, b + 1)
                            v.tensor_copy(mv1[:, ds(b * Q, Q), :], mvb[s][:]).then_inc(kept, 1)

                        def step(t, u):
                            b, s = t, u % 2
                            if live(b, NB):
                                dve.wait_ge(turned, b + 1)
                                dve.wait_ge(x_in[s], half(b) * 16 + 16)
                                if after(b):
                                    dve.wait_ge(stored[s], half(b) * 16)
                                v.tensor_tensor(x1b[s][:], ps_h[s][:], xb[s][:], ALU.add).then_inc(added, 1)
                            b1, s1 = t - 1, (u - 1) % 2
                            if live(b1, NB):
                                dve.wait_ge(counted, b1 + 1)
                                if live(b1 - 1, NB):
                                    keep_stats(b1 - 1, 1 - s1)
                                for q in range(Q):
                                    i = v.bn_aggr(mvb[s1][:, q, :], bs[s1][:, q, :])
                                i.then_inc(aggregated, 1)
                            if live(b, NB):
                                dve.wait_ge(added, b + 1)
                                for q in range(Q):
                                    i = v.bn_stats(bs[s][:, q, :], x1b[s][:, q, :])
                                i.then_inc(counted, 1)

                        steps(dve, NB, 1, step)
                        keep_stats(NB - 1, (NB - 1) % 2)
                        dve.wait_ge(sd_ready, 1)
                        s0 = snb[:, :, 0, :]
                        v.reciprocal(s0, sd[:].rearrange("p (b q) -> p b q", q=Q)).then_inc(inv_ready, 1)
                        dve.wait_ge(inv_ready, 1)
                        m0 = mv1[:, :, 0].rearrange("p (b q) -> p b q", q=Q)
                        v.tensor_tensor(snb[:, :, 1, :], m0, s0, ALU.mult).then_inc(inv_ready, 1)
                        dve.wait_ge(inv_ready, 2)
                        v.tensor_scalar(snb[:, :, 1, :], snb[:, :, 1, :], -1.0, None, ALU.mult)

        def gru():
            with ExitStack() as ctx:
                def sb(name, shape, dt=F32):
                    return ctx.enter_context(nc.sbuf_tensor(f"gr_{name}", shape, dt))

                def ps(name, shape):
                    return ctx.enter_context(nc.psum_tensor(f"gr_{name}", shape, F32))

                def sem(name):
                    return ctx.enter_context(nc.semaphore(f"gr_{name}"))

                def two(name, shape, dt=F32):
                    return [sb(f"{name}{i}", shape, dt) for i in range(2)]

                xb = [sb(f"xb{i}", [P, Q, D]) for i in range(4)]
                fb = two("fb", [P, Q, D])
                gath = two("gath", [P, Q, D])
                idx = two("idx", [P, Q], I32)
                scal = two("scal", [P, 2, Q])
                h2 = two("h2", [P, Q, D])
                red = two("red", [P, Q, D])
                ht = two("ht", [P, KD, BLK])
                h_hi, h_lo, r_hi, r_lo = (two(n, [P, KD, BLK], F32R) for n in ("h_hi", "h_lo", "r_hi", "r_lo"))
                rg, zg, ng, tg = (two(n, [P, BLK]) for n in ("rg", "zg", "ng", "tg"))
                hn = two("hn", [P, KD, BLK])
                ps_a = ps("ps_a", [P, KD, BLK])
                ps_b = ps("ps_b", [P, KD, BLK])
                ps_r, ps_z, ps_in, ps_hn = (ps(n, [P, BLK]) for n in ("ps_r", "ps_z", "ps_in", "ps_hn"))
                x_in = [sem(f"x_in{i}") for i in range(4)]
                stored = [sem(f"stored{i}") for i in range(4)]
                seg_in = [sem(f"seg_in{i}") for i in range(2)]
                (idx_ready, scal_ready, h2_ready, red_ready, turned, back, r_ps, z_ps, in_ps, hn_ps, r_ready, z_ready,
                 n_ready, reset, summed_n, copied, low, dif, zdif, new_h, finished) = (
                    sem(n) for n in ("idx_ready", "scal_ready", "h2_ready", "red_ready", "turned", "back", "r_ps",
                                     "z_ps", "in_ps", "hn_ps", "r_ready", "z_ready", "n_ready", "reset",
                                     "summed_n", "copied", "low", "dif", "zdif", "new_h", "finished"))

                def quarter(b):
                    return b // 4 if isinstance(b, int) else b >> 2

                with nc.Block() as block:
                    @block.sync
                    def _(sp):
                        def step(t, u):
                            if live(t, NB):
                                if after(t, 4):
                                    sp.wait_ge(finished, t - 3)
                                sp.dma_start(xb[u][:].rearrange("p q d -> p (q d)"),
                                             x1_r[ds(t * P, P), :]).then_inc(x_in[u], 16)
                            b, s = t - 3, (u - 3) % 2
                            if live(b, NB):
                                sp.wait_ge(finished, b + 1)
                                rows = TAIL if isinstance(b, int) and b == NB - 1 else P
                                sp.dma_start(out_r[ds(b * P, rows), :],
                                             fb[s][0:rows].rearrange("p q d -> p (q d)")).then_inc(stored[s], 16)

                        steps(sp, NB, 3, step, unroll=4)
                        sp.wait_ge(stored[0], 16 * (NB // 2))
                        sp.wait_ge(stored[1], 16 * (NB // 2))

                    @block.gpsimd
                    def _(pool):
                        for i in range(2):
                            nc.gpsimd.memset(gath[i][:], 0.0).then_inc(idx_ready, 1)
                        pool.wait_ge(idx_ready, 2)
                        bound = nc.gpsimd.to_reg(E - 1)

                        def step(t, u):
                            if after(t):
                                pool.wait_ge(red_ready, t - 1)
                            nc.gpsimd.tensor_copy(idx[u][:], end_index[:, ds(t * Q, Q)]).then_inc(idx_ready, 1)
                            pool.wait_ge(idx_ready, t + 3)
                            pool.sem_inc(issuing, 1)
                            for q in range(Q):
                                nc.gpsimd.indirect_dma_start(
                                    gath[u][:, q, :], None, seg,
                                    bass.IndirectOffsetOnAxis(ap=idx[u][:, q:q + 1], axis=0),
                                    bounds_check=bound, oob_is_err=False).then_inc(seg_in[u], 16)

                        steps(pool, NB, 0, step)

                    @block.scalar
                    def _(act):
                        def step(t, u):
                            b, s, s4 = t - 1, (u - 1) % 2, (u - 1) % 4
                            if live(b, NB):
                                act.wait_ge(x_in[s4], quarter(b) * 16 + 16)
                                act.wait_ge(scal_ready, b + 1)
                                if after(b):
                                    act.wait_ge(turned, b - 1)
                                for q in range(Q):
                                    i = nc.scalar.activation(h2[s][:, q, :], xb[s4][:, q, :], ACT.Relu,
                                                             bias=scal[s][:, 1, q:q + 1], scale=scal[s][:, 0, q:q + 1])
                                i.then_inc(h2_ready, 1)

                            def gates(b, h):
                                n = 2 * b + h
                                act.wait_ge(r_ps, n + 1)
                                if not isinstance(n, int) or n >= 2:
                                    act.wait_ge(new_h, n - 1)
                                nc.scalar.activation(rg[h][:], ps_r[:], ACT.Sigmoid,
                                                     bias=brz[:, h:h + 1]).then_inc(r_ready, 1)
                                act.wait_ge(summed_n, n + 1)
                                nc.scalar.activation(ng[h][:], tg[h][:], ACT.Tanh,
                                                     bias=bih[:, 4 + h:5 + h]).then_inc(n_ready, 1)
                                act.wait_ge(z_ps, n + 1)
                                nc.scalar.activation(zg[h][:], ps_z[:], ACT.Sigmoid,
                                                     bias=brz[:, 2 + h:3 + h]).then_inc(z_ready, 1)

                            b2 = t - 2
                            if live(b2, NB):
                                gates(b2, 0)
                            if live(b, NB):
                                act.wait_ge(turned, b + 1)
                                if after(b):
                                    act.wait_ge(z_ps, 2 * b - 2)
                                    act.wait_ge(new_h, 2 * b - 2)
                                nc.scalar.activation(h_hi[s][:], ps_a[:], ACT.Copy).then_inc(copied, 1)
                                nc.scalar.activation(ht[s][:], ps_a[:], ACT.Copy).then_inc(copied, 1)
                                nc.scalar.activation(r_hi[s][:], ps_b[:], ACT.Copy).then_inc(copied, 1)
                            if live(b2, NB):
                                gates(b2, 1)

                        steps(act, NB, 2, step, unroll=4)

                    @block.vector
                    def _(dve):
                        v = nc.vector

                        def step(t, u):
                            b, s = t, u % 2
                            if live(b, NB):
                                if after(b):
                                    dve.wait_ge(h2_ready, b - 1)
                                v.tensor_copy(scal[s][:].rearrange("p a q -> p (a q)"),
                                              snb[:, ds(b, 1), :, :].rearrange("p b a q -> p (b a q)")
                                              ).then_inc(scal_ready, 1)
                            b, s = t - 1, (u - 1) % 2
                            if live(b, NB):
                                dve.wait_ge(seg_in[s], half(b) * 16 * Q + 16 * Q)
                                if after(b):
                                    dve.wait_ge(turned, b - 1)
                                v.tensor_tensor(red[s][:], gath[s][:],
                                                has[:, ds(b * Q, Q)].unsqueeze(2).broadcast_to([P, Q, D]),
                                                ALU.mult).then_inc(red_ready, 1)

                            def reset_gate(b, h):
                                n = 2 * b + h
                                dve.wait_ge(hn_ps, n + 1)
                                dve.wait_ge(r_ready, n + 1)
                                if not isinstance(n, int) or n >= 2:
                                    dve.wait_ge(n_ready, n - 1)
                                v.scalar_tensor_tensor(tg[h][:], ps_hn[:], bhh[:, 4 + h:5 + h], rg[h][:],
                                                       ALU.add, ALU.mult).then_inc(reset, 1)

                            def candidate(b, h):
                                n = 2 * b + h
                                dve.wait_ge(in_ps, n + 1)
                                dve.wait_ge(reset, n + 1)
                                v.tensor_tensor(tg[h][:], tg[h][:], ps_in[:], ALU.add).then_inc(summed_n, 1)

                            def new_state(b, s, h):
                                n = 2 * b + h
                                dve.wait_ge(n_ready, n + 1)
                                dve.wait_ge(copied, 3 * b + 3)
                                if after(b):
                                    dve.wait_ge(back, b - 1)
                                v.tensor_tensor(hn[s][:, h, :], ht[s][:, h, :], ng[h][:], ALU.subtract).then_inc(dif, 1)
                                dve.wait_ge(z_ready, n + 1)
                                dve.wait_ge(dif, n + 1)
                                v.tensor_tensor(hn[s][:, h, :], hn[s][:, h, :], zg[h][:], ALU.mult).then_inc(zdif, 1)
                                dve.wait_ge(zdif, n + 1)
                                v.tensor_tensor(hn[s][:, h, :], hn[s][:, h, :], ng[h][:], ALU.add).then_inc(new_h, 1)

                            b2, s2 = t - 2, u % 2
                            if live(b2, NB):
                                reset_gate(b2, 0)
                            b3, s3, u3 = t - 3, (u - 3) % 4, (u - 3) % 2
                            if live(b3, NB):
                                dve.wait_ge(back, b3 + 1)
                                dve.wait_ge(x_in[s3], quarter(b3) * 16 + 16)
                                if after(b3):
                                    dve.wait_ge(stored[u3], half(b3) * 16)
                                v.tensor_tensor(fb[u3][:], ps_a[:].rearrange("p c n -> p (c n)").rearrange(
                                    "p (q d) -> p q d", q=Q), xb[s3][:], ALU.add).then_inc(finished, 1)
                            if live(b2, NB):
                                candidate(b2, 0)
                                new_state(b2, s2, 0)
                            if live(b, NB):
                                if after(b):
                                    dve.wait_ge(z_ps, 2 * b - 2)
                                dve.wait_ge(copied, 3 * b + 2)
                                v.tensor_tensor(h_lo[s][:], ht[s][:], h_hi[s][:].bitcast(F32),
                                                ALU.subtract).then_inc(low, 1)
                                dve.wait_ge(copied, 3 * b + 3)
                                v.tensor_tensor(r_lo[s][:], ps_b[:], r_hi[s][:].bitcast(F32),
                                                ALU.subtract).then_inc(low, 1)
                            if live(b2, NB):
                                reset_gate(b2, 1)
                                candidate(b2, 1)
                                new_state(b2, s2, 1)

                        steps(dve, NB, 3, step, unroll=4)

                    @block.tensor
                    def _(pe):
                        def product(bank, s, sides, chunk, signal):
                            terms = []
                            for side in sides:
                                hi, lo = (h_hi, h_lo) if side == "hh" else (r_hi, r_lo)
                                for c in range(KD):
                                    terms += [(whi[side], hi, c), (whi[side], lo, c), (wlo[side], hi, c)]
                            for n, (w, a, c) in enumerate(terms):
                                i = nc.tensor.matmul(bank[:], w[:, c, chunk * P:(chunk + 1) * P], a[s][:, c, :],
                                                     start=(n == 0), stop=(n == len(terms) - 1))
                            i.then_inc(signal, 1)

                        def step(t, u):
                            b2, s2 = t - 2, u % 2

                            def later(n):
                                return not isinstance(n, int) or n >= 1

                            def first_gates(h):
                                n = 2 * b2 + h
                                if h == 0:
                                    pe.wait_ge(low, 2 * b2 + 2)
                                if later(n):
                                    pe.wait_ge(r_ready, n)
                                product(ps_r, s2, ("hh", "ih"), h, r_ps)
                                if later(n):
                                    pe.wait_ge(reset, n)
                                product(ps_hn, s2, ("hh",), 4 + h, hn_ps)

                            def last_gates(h):
                                n = 2 * b2 + h
                                if later(n):
                                    pe.wait_ge(summed_n, n)
                                product(ps_in, s2, ("ih",), 4 + h, in_ps)
                                if later(n):
                                    pe.wait_ge(z_ready, n)
                                product(ps_z, s2, ("hh", "ih"), 2 + h, z_ps)

                            if live(b2, NB):
                                first_gates(0)
                            b3, s3 = t - 3, (u - 3) % 2
                            if live(b3, NB):
                                pe.wait_ge(new_h, 2 * b3 + 2)
                                if live(b2, NB):
                                    pe.wait_ge(copied, 3 * b2 + 3)
                                    pe.wait_ge(low, 2 * b2 + 1)
                                rows = ps_a[:].rearrange("p c n -> p (c n)")
                                for q in range(Q):
                                    for c in range(KD):
                                        i = nc.tensor.transpose(rows[:, q * D + c * P:q * D + (c + 1) * P],
                                                                hn[s3][:, c, q * P:(q + 1) * P], ident[:])
                                i.then_inc(back, 1)
                            if live(b2, NB):
                                last_gates(0)
                            b, s = t - 1, (u - 1) % 2
                            if live(b, NB):
                                pe.wait_ge(h2_ready, b + 1)
                                pe.wait_ge(red_ready, b + 1)
                                if live(b3, NB):
                                    pe.wait_ge(finished, b3 + 1)
                                if live(b2, NB):
                                    pe.wait_ge(copied, 3 * b2 + 3)
                                    pe.wait_ge(low, 2 * b2 + 2)
                                for dst, src in ((ps_a, h2), (ps_b, red)):
                                    for c in range(KD):
                                        for q in range(Q):
                                            i = nc.tensor.transpose(dst[:, c, q * P:(q + 1) * P],
                                                                    src[s][:, q, c * P:(c + 1) * P], ident[:])
                                i.then_inc(turned, 1)
                            if live(b2, NB):
                                first_gates(1)
                                last_gates(1)

                        steps(pe, NB, 3, step, unroll=4)

        setup()
        edges("e1", x, True, True, False)
        with nc.sbuf_tensor("stats1", [P, KD, NB, 6], F32) as stats1:
            aggregate("c1", x_r, True, o1t, stats1)
            batch_norm_coefficients("b1", stats1, bn_in["b1c"], bn_in["g1c"], bn_in["be1c"])
        lin2()
        edges("e2", g2s, False, False, False)
        with nc.sbuf_tensor("stats2", [P, KD, NB, 6], F32) as stats2:
            aggregate("a2", g2_r, False, o2t, stats2)
            batch_norm_coefficients("b2", stats2, bn_in["b2c"], bn_in["g2c"], bn_in["be2c"])
        residual()
        edges("e3", x1s, True, False, True)
        gru()


def kernel(**inputs):
    import numpy as np
    import concourse.bacc as bacc
    from concourse import mybir
    from concourse.bass_utils import run_bass_kernel_spmd

    tile = 128
    group = 4 * tile
    n_edges = inputs["dst"].shape[0]
    padded = -(-n_edges // group) * group

    def pad(a, fill):
        return np.concatenate([np.asarray(a), np.full(padded - n_edges, fill, np.int32)])

    dst, src, typ = pad(inputs["dst"], 60000), pad(inputs["src"], 0), pad(inputs["edge_type_16"], 0)
    arrays = {
        "x": inputs["x"],
        "dst_row": dst.reshape(1, -1),
        "dst_col": dst.reshape(-1, tile).T,
        "src_col": src.reshape(-1, tile).T,
        "type_row": typ.reshape(1, -1),
    }
    for name in ("W1", "b1", "g1", "be1", "W2", "b2", "g2", "be2"):
        arrays[name] = inputs[f"L0_gnn_{name}"]
    for name in ("relvectors", "w_ih", "w_hh", "b_ih", "b_hh"):
        arrays[name] = inputs[f"L1_gnn_{name}"]
    for name, a in arrays.items():
        if a.ndim == 1:
            arrays[name] = np.asarray(a).reshape(-1, tile).T
    arrays = {f"in_{k}": np.ascontiguousarray(v) for k, v in arrays.items()}

    nc = bacc.Bacc("TRN2", target_bir_lowering=False, num_devices=1)
    args = [nc.dram_tensor(k, a.shape, mybir.dt.from_np(a.dtype), kind="ExternalInput").ap()
            for k, a in arrays.items()]
    out = nc.dram_tensor("out", inputs["x"].shape, mybir.dt.float32, kind="ExternalOutput").ap()
    build_program(nc, *args, out)
    r = run_bass_kernel_spmd(nc, [arrays], core_ids=[0])
    return r.results[0]["out"]
```

```python
def build_program(nc, x, dst_row, dst_col, next_col, src_col, type_row, W1, b1, g1, be1, W2, b2, g2, be2,
                  rel, w_ih, w_hh, b_ih, b_hh, out):
    from contextlib import ExitStack
    import concourse.bass as bass
    from concourse import mybir

    F32 = mybir.dt.float32
    F32R = mybir.dt.float32r
    F16 = mybir.dt.float16
    I32 = mybir.dt.int32
    ALU = mybir.AluOpType
    ACT = mybir.ActivationFunctionType
    AX = mybir.AxisListType

    P = 128
    N, D = x.shape
    E = 25000
    Q = 4
    BLK = P * Q
    NB = -(-N // BLK)
    TAIL = (N - (NB - 1) * BLK) // Q
    NCOL = NB * Q
    NPAD = NB * BLK
    NT = dst_col.shape[1]
    NG = NT // Q
    KD = D // P
    G3 = w_ih.shape[0] // P
    NREL = rel.shape[0]
    EPS = 1e-5
    ROW = Q * D
    DX = D + 2
    NONE = 1.0e6
    ds = bass.ds

    assert TAIL * Q + (NB - 1) * BLK == N and NG * Q == NT

    dinv_tab = nc.dram_tensor("dinv_tab", (P * NCOL, 1), F32, kind="Internal").ap()
    seg = nc.dram_tensor("seg", (NT * P, D), F32, kind="Internal").ap()
    o1t = nc.dram_tensor("o1t", (NB * P, ROW), F32, kind="Internal").ap()
    g2s = nc.dram_tensor("g2s", (NPAD, D), F32, kind="Internal").ap()
    o2t = nc.dram_tensor("o2t", (NB * P, ROW), F32, kind="Internal").ap()
    x1s = nc.dram_tensor("x1s", (NPAD, DX), F32, kind="Internal").ap()
    free_tab = nc.dram_tensor("free_tab", (NPAD, 1), I32, kind="Internal").ap()

    def rows4(t):
        return t.rearrange("(r q) d -> r (q d)", q=Q)

    x_r, g2_r, x1_r = rows4(x), rows4(g2s), rows4(x1s)
    seg_t = seg.rearrange("(t p) d -> p t d", p=P)

    def steps(eng, n, lag, step, unroll=2):
        head = -(-(lag + 4) // unroll) * unroll
        end = head + (n - 1 - head) // unroll * unroll
        for t in range(head):
            step(t, t % unroll)
        with eng.Fori(head // unroll, end // unroll) as k:
            for u in range(unroll):
                step(k * unroll + u, u)
        for t in range(end, n + lag):
            step(t, t % unroll)

    def live(b, n):
        return not isinstance(b, int) or 0 <= b < n

    def after(b, slots=2):
        return not isinstance(b, int) or b >= slots

    def half(b):
        return b // 2 if isinstance(b, int) else b >> 1

    def quarter(b):
        return b // 4 if isinstance(b, int) else b >> 2

    with ExitStack() as keep:
        def ksb(name, shape, dt=F32):
            return keep.enter_context(nc.sbuf_tensor(name, shape, dt))

        ident = ksb("ident", [P, P])
        pidx = ksb("pidx", [P, 1])
        eps = ksb("eps", [P, 1])
        dinv = ksb("dinv", [P, NCOL])
        dinv2 = ksb("dinv2", [P, NCOL])
        has = ksb("has", [P, NCOL])
        dh = ksb("dh", [P, NB, 2, Q])
        end_index = ksb("end_index", [P, NCOL], I32)
        dst_f = ksb("dst_f", [P, NT])
        carry_f = ksb("carry_f", [P, NT])
        src_i = ksb("src_i", [P, NT], I32)
        src_pos = ksb("src_pos", [P, NT], I32)
        w1 = ksb("w1", [P, KD, D])
        w2 = ksb("w2", [P, KD, D])
        rel_sb = ksb("rel_sb", [NREL, D])
        spare = ksb("spare", [P, 1])
        rel_hi = ksb("rel_hi", [NREL, D], F32R)
        rel_lo = ksb("rel_lo", [NREL, D], F32R)
        bn_in = {k: ksb(k, [P, KD]) for k in ("b1c", "g1c", "be1c", "b2c", "g2c", "be2c")}
        bih = ksb("bih", [P, G3])
        bhh = ksb("bhh", [P, G3])
        brz = ksb("brz", [P, G3])
        whi = {k: ksb(f"{k}_hi", [P, KD, G3 * P], F32R) for k in ("ih", "hh")}
        wlo = {k: ksb(f"{k}_lo", [P, KD, G3 * P], F32R) for k in ("ih", "hh")}
        bn_s = ksb("bn_s", [P, KD])
        bn_t = ksb("bn_t", [P, KD])
        issuing = keep.enter_context(nc.semaphore("issuing"))
        dst_i = ksb("dst_i", [P, NT], I32)
        node_id = ksb("node_id", [P, NCOL], I32)
        free_rank = ksb("free_rank", [P, NCOL], I32)
        slot_rank = ksb("slot_rank", [P, NT], I32)
        free_off = ksb("free_off", [P, 1], I32)
        slot_node = [ksb(f"slot_node{i}", [P, NT], I32) for i in range(2)]
        pad_slot = ksb("pad_slot", [P, NT], I32)

        def clear(sems):
            with nc.Block() as block:
                @block.gpsimd
                def _(pool):
                    for s in sems:
                        pool.sem_clear(s)

        def setup():
            with ExitStack() as ctx:
                def sb(name, shape, dt=F32):
                    return ctx.enter_context(nc.sbuf_tensor(name, shape, dt))

                def sem(name):
                    return ctx.enter_context(nc.semaphore(name))

                next_i = sb("next_i", [P, NT], I32)
                no_table = sb("no_table", [P, NCOL], I32)
                ia, ib, ic = (sb(n, [P, NT], I32) for n in ("ia", "ib", "ic"))
                fa, fb = sb("fa", [P, NT]), sb("fb", [P, NT])
                dst_a, dst_p = sb("dst_a", [P, NT], F16), sb("dst_p", [P, NT], F16)
                row_i = sb("row_i", [P, NCOL], I32)
                row_h = sb("row_h", [P, NCOL], F16)
                row_f = sb("row_f", [P, P])
                pidx_i = sb("pidx_i", [P, 1], I32)
                last = sb("last", [P, 1])
                node_mask = sb("node_mask", [P, 1])
                tri = sb("tri", [P, P])
                ones = sb("ones", [P, P])
                one_row = sb("one_row", [P, NT])
                hot_a = [sb(f"hot_a{i}", [P, Q, NCOL], F16) for i in range(2)]
                hot_p = [sb(f"hot_p{i}", [P, Q, P], F16) for i in range(2)]
                wraw = {k: sb(f"w{k}_raw", [P, G3, D]) for k in ("ih", "hh")}
                cnt = sb("cnt", [P, NB, Q])
                node_f, rank_f = sb("node_f", [P, NCOL]), sb("rank_f", [P, NCOL])
                next_f, stay = sb("next_f", [P, NT]), sb("stay", [P, NT])
                deg = sb("deg", [P, NCOL])
                blk_sum = sb("blk_sum", [P, 2, NB])
                base, tot, run = sb("base", [P, 2, NB]), sb("tot", [P, 2, NB]), sb("run", [P, 2, NB])
                cum = sb("cum", [P, 2, NB, Q])
                etot, erun = sb("etot", [P, NT]), sb("erun", [P, NT])
                big = sb("big", [P, NCOL])
                ps_w = [ctx.enter_context(nc.psum_tensor(f"ps_w{i}", [P, KD, G3 * P], F32)) for i in range(2)]
                ps_e = ps_w[0][:].rearrange("p c n -> p (c n)")[:, 0:2 * NT].rearrange("p (a n) -> p a n", a=2)
                ps_c = ctx.enter_context(nc.psum_tensor("ps_c", [P, NCOL], F32))
                ps_b = ctx.enter_context(nc.psum_tensor("ps_b", [P, 2, 2 * NB], F32))
                loaded_dst, loaded_src, loaded_w, tab_stored = (sem(n) for n in (
                    "loaded_dst", "loaded_src", "loaded_w", "tab_stored"))
                iotas, consts, hots, hists, wts, sums, sums_ps, deg_ready, sd_ready, dve_step, tab_ready = (
                    sem(n) for n in ("iotas", "consts", "hots", "hists", "wts", "sums", "sums_ps",
                                     "deg_ready", "sd_ready", "dve_step", "tab_ready"))

                with nc.Block() as block:
                    @block.sync
                    def _(sp):
                        sp.dma_start(dst_i[:], dst_col).then_inc(loaded_dst, 16)
                        sp.dma_start(next_i[:], next_col).then_inc(loaded_w, 16)
                        sp.dma_start(src_i[:], src_col).then_inc(loaded_src, 16)
                        n = 16
                        for k, w in (("ih", w_ih), ("hh", w_hh)):
                            sp.dma_start(wraw[k][:], w.rearrange("(c p) d -> p c d", p=P)).then_inc(loaded_w, 16)
                            n += 16
                        for t, w in ((w1, W1), (w2, W2)):
                            sp.dma_start(t[:], w.rearrange("(c p) d -> p c d", p=P)).then_inc(loaded_w, 16)
                            n += 16
                        sp.dma_start(rel_sb[:], rel).then_inc(loaded_w, 16)
                        n += 16
                        for k, v in (("b1c", b1), ("g1c", g1), ("be1c", be1), ("b2c", b2), ("g2c", g2), ("be2c", be2)):
                            sp.dma_start(bn_in[k][:], v).then_inc(loaded_w, 16)
                            n += 16
                        for t, v in ((bih, b_ih), (bhh, b_hh)):
                            sp.dma_start(t[:], v).then_inc(loaded_w, 16)
                            n += 16
                        assert n == 16 * LOADS_W
                        sp.wait_ge(iotas, 1)
                        sp.dma_start(free_tab.rearrange("(p a) o -> p (a o)", p=P), no_table[:]).then_inc(tab_stored, 16)
                        sp.wait_ge(tab_ready, 1)
                        sp.dma_start(dinv_tab.rearrange("(p a) o -> p (a o)", p=P), dinv[:]).then_inc(tab_stored, 16)
                        sp.wait_ge(tab_stored, 32)

                    @block.gpsimd
                    def _(pool):
                        nc.gpsimd.iota(row_i[:], pattern=[[1, NCOL]], base=0, channel_multiplier=0)
                        nc.gpsimd.memset(ones[:], 1.0)
                        nc.gpsimd.memset(one_row[:], 1.0)
                        nc.gpsimd.memset(eps[:], EPS)
                        nc.gpsimd.memset(no_table[:], 0)
                        nc.gpsimd.iota(node_id[:].rearrange("p (b q) -> p b q", q=Q), pattern=[[BLK, NB], [1, Q]],
                                       base=0, channel_multiplier=Q)
                        nc.gpsimd.iota(pad_slot[:], pattern=[[1, NT]], base=0, channel_multiplier=NT)
                        nc.gpsimd.iota(pidx_i[:], pattern=[[1, 1]], base=0, channel_multiplier=1).then_inc(iotas, 1)

                    @block.scalar
                    def _(act):
                        act.wait_ge(deg_ready, 1)
                        nc.scalar.activation(big[:], deg[:], ACT.Sqrt).then_inc(sd_ready, 1)

                    @block.vector
                    def _(dve):
                        done = [0]

                        def link(ins):
                            done[0] += 1
                            ins.then_inc(dve_step, 1)
                            dve.wait_ge(dve_step, done[0])

                        v = nc.vector
                        dve.wait_ge(iotas, 1)
                        link(v.tensor_copy(pidx[:], pidx_i[:]))
                        v.tensor_copy(row_h[:], row_i[:])
                        link(v.tensor_copy(row_f[:], row_i[:, 0:P]))
                        v.tensor_scalar(tri[:], row_f[:], pidx[:], None, ALU.is_gt)
                        v.tensor_scalar(last[:], pidx[:], float(P - 1), None, ALU.is_equal)
                        v.tensor_scalar(node_mask[:], pidx[:], float(TAIL), None, ALU.is_lt)
                        link(v.tensor_scalar(ident[:], row_f[:], pidx[:], None, ALU.is_equal))
                        v.sem_inc(consts, 1)

                        def column(node_i):
                            v.tensor_scalar(ia[:], node_i[:], 9, 2, ALU.logical_shift_right, ALU.logical_shift_left)
                            link(v.tensor_scalar(ib[:], node_i[:], 3, None, ALU.bitwise_and))
                            v.tensor_scalar(ic[:], node_i[:], 2, P - 1, ALU.logical_shift_right, ALU.bitwise_and)
                            link(v.tensor_tensor(ia[:], ia[:], ib[:], ALU.bitwise_or))

                        dve.wait_ge(loaded_dst, 16)
                        column(dst_i)
                        v.tensor_copy(dst_a[:], ia[:])
                        v.tensor_copy(dst_f[:], dst_i[:])
                        link(v.tensor_copy(dst_p[:], ic[:]))

                        def hot(t, u):
                            if live(t, NG):
                                if after(t):
                                    dve.wait_ge(hists, t - 1)
                                v.tensor_tensor(hot_a[u][:], row_h[:].unsqueeze(1).broadcast_to([P, Q, NCOL]),
                                                dst_a[:, ds(t * Q, Q)].unsqueeze(2).broadcast_to([P, Q, NCOL]),
                                                ALU.is_equal)
                                v.tensor_tensor(hot_p[u][:], row_h[:, 0:P].unsqueeze(1).broadcast_to([P, Q, P]),
                                                dst_p[:, ds(t * Q, Q)].unsqueeze(2).broadcast_to([P, Q, P]),
                                                ALU.is_equal).then_inc(hots, 1)

                        steps(dve, NG, 0, hot)

                        for i, k in enumerate(("ih", "hh")):
                            dve.wait_ge(wts, i + 1)
                            link(v.tensor_copy(whi[k][:], ps_w[i][:]))
                            v.tensor_tensor(wlo[k][:], ps_w[i][:], whi[k][:].bitcast(F32), ALU.subtract)
                        dve.wait_ge(loaded_w, 16 * LOADS_W)
                        v.tensor_tensor(brz[:], bih[:], bhh[:], ALU.add)
                        link(v.tensor_copy(rel_hi[:], rel_sb[:]))
                        v.tensor_tensor(rel_lo[:], rel_sb[:], rel_hi[:].bitcast(F32), ALU.subtract)
                        link(v.tensor_copy(next_f[:], next_i[:]))
                        link(v.tensor_tensor(stay[:], dst_f[:], next_f[:], ALU.is_equal))
                        link(v.tensor_scalar(next_f[:], dst_f[:], float(N), None, ALU.is_lt))
                        link(v.tensor_tensor(stay[:], stay[:], next_f[:], ALU.mult))
                        v.tensor_copy(slot_node[0][:], dst_i[:])
                        link(v.tensor_copy(erun[:], pad_slot[:]))
                        link(v.tensor_scalar(erun[:], erun[:], float(E), NONE, ALU.is_ge, ALU.mult))
                        link(v.tensor_copy(pad_slot[:], erun[:]))

                        v.memset(carry_f[:, 0:1], -1.0)
                        link(v.tensor_scalar(carry_f[:, 1:NT], dst_f[:, 0:NT - 1], 1.0, None, ALU.add))
                        link(v.tensor_scalar(carry_f[:, 1:NT], carry_f[:, 1:NT], last[:], -1.0, ALU.mult, ALU.add))

                        dve.wait_ge(loaded_src, 16)
                        column(src_i)
                        v.tensor_copy(fa[:], ia[:])
                        link(v.tensor_copy(fb[:], ic[:]))
                        link(v.scalar_tensor_tensor(fa[:], fb[:], float(NCOL), fa[:], ALU.mult, ALU.add))
                        link(v.tensor_copy(src_pos[:], fa[:]))

                        dve.wait_ge(hists, NG)
                        c2 = cnt[:].rearrange("p b q -> p (b q)")
                        link(v.tensor_copy(c2, ps_c[:]))
                        v.tensor_scalar(deg[:], c2, 1.0, None, ALU.add).then_inc(deg_ready, 1)
                        v.tensor_scalar(has[:], c2, 0.5, None, ALU.is_gt)
                        link(v.tensor_copy(cum[:, 0, :, 0], cnt[:, :, 0]))
                        link(v.tensor_copy(cum[:, 1, :, 0], has[:].rearrange("p (b q) -> p b q", q=Q)[:, :, 0]))
                        v.tensor_reduce(blk_sum[:, 0, :], cnt[:], AX.X, ALU.add)
                        v.tensor_reduce(blk_sum[:, 1, :], has[:].rearrange("p (b q) -> p b q", q=Q), AX.X,
                                        ALU.add).then_inc(sums, 1)
                        h3 = has[:].rearrange("p (b q) -> p b q", q=Q)
                        for q in range(1, Q):
                            v.tensor_tensor(cum[:, 0, :, q], cum[:, 0, :, q - 1], cnt[:, :, q], ALU.add)
                            link(v.tensor_tensor(cum[:, 1, :, q], cum[:, 1, :, q - 1], h3[:, :, q], ALU.add))
                        dve.wait_ge(sums_ps, 1)
                        link(v.tensor_copy(tot[:].rearrange("p a b -> p (a b)"), ps_b[:, 1, :]))
                        for a in range(2):
                            link(v.tensor_tensor_scan(run[:, a, :], ones[:, 0:NB], tot[:, a, :], 0.0,
                                                      ALU.mult, ALU.add))
                        link(v.tensor_scalar(base[:, 0, 0:1], run[:, 1, NB - 1:NB], -1.0, float(E),
                                             ALU.mult, ALU.add))
                        link(v.tensor_copy(free_off[:], base[:, 0, 0:1]))
                        link(v.tensor_tensor(run[:], run[:], tot[:], ALU.subtract))
                        link(v.tensor_tensor(base[:].rearrange("p a b -> p (a b)"), ps_b[:, 0, :],
                                             run[:].rearrange("p a b -> p (a b)"), ALU.add))
                        for a in range(2):
                            link(v.tensor_tensor(cum[:, a], cum[:, a],
                                                 base[:, a, :].unsqueeze(2).broadcast_to([P, NB, Q]), ALU.add))
                        link(v.tensor_copy(node_f[:], node_id[:]))
                        link(v.tensor_tensor(rank_f[:], node_f[:], cum[:, 1].rearrange("p b q -> p (b q)"),
                                             ALU.subtract))
                        link(v.scalar_tensor_tensor(rank_f[:], has[:], NONE, rank_f[:], ALU.mult, ALU.add))
                        link(v.tensor_scalar(node_f[:], node_f[:], float(N), NONE, ALU.is_ge, ALU.mult))
                        link(v.tensor_tensor(rank_f[:], rank_f[:], node_f[:], ALU.add))
                        link(v.tensor_copy(free_rank[:], rank_f[:]))
                        link(v.tensor_copy(etot[:], ps_e[:, 1, :]))
                        link(v.tensor_tensor_scan(erun[:], one_row[:], etot[:], 0.0, ALU.mult, ALU.add))
                        link(v.tensor_tensor(erun[:], erun[:], etot[:], ALU.subtract))
                        link(v.tensor_tensor(erun[:], erun[:], ps_e[:, 0, :], ALU.add))
                        link(v.tensor_scalar(stay[:], stay[:], -NONE, NONE, ALU.mult, ALU.add))
                        link(v.tensor_tensor(erun[:], erun[:], stay[:], ALU.add))
                        link(v.tensor_copy(slot_rank[:], erun[:]))
                        dve.wait_ge(sd_ready, 1)
                        link(v.reciprocal(dinv[:], big[:]))
                        link(v.tensor_scalar(dinv[:, NCOL - Q:NCOL], dinv[:, NCOL - Q:NCOL], node_mask[:], None,
                                             ALU.mult))
                        v.sem_inc(tab_ready, 1)
                        v.tensor_tensor(dinv2[:], dinv[:], dinv[:], ALU.mult)
                        d3 = dinv[:].rearrange("p (b q) -> p b q", q=Q)
                        v.tensor_copy(dh[:, :, 0, :], d3)
                        v.tensor_tensor(dh[:, :, 1, :], d3, h3, ALU.mult)
                        link(v.tensor_scalar(big[:], has[:], -NONE, NONE - 1.0, ALU.mult, ALU.add))
                        link(v.tensor_tensor(big[:], big[:], cum[:, 0].rearrange("p b q -> p (b q)"), ALU.add))
                        link(v.tensor_copy(end_index[:], big[:]))

                    @block.tensor
                    def _(pe):
                        pe.wait_ge(consts, 1)
                        pe.wait_ge(loaded_w, 16 * LOADS_W)
                        for i, k in enumerate(("ih", "hh")):
                            for c in range(G3):
                                for h in range(KD):
                                    t = nc.tensor.transpose(ps_w[i][:, h, c * P:(c + 1) * P],
                                                            wraw[k][:, c, h * P:(h + 1) * P], ident[:])
                            t.then_inc(wts, 1)

                        def hist(t, u):
                            pe.wait_ge(hots, t + 1)
                            for k in range(Q):
                                m = nc.tensor.matmul(ps_c[:], hot_p[u][:, k, :], hot_a[u][:, k, :],
                                                     start=isinstance(t, int) and t == 0 and k == 0,
                                                     stop=isinstance(t, int) and t == NG - 1 and k == Q - 1)
                            m.then_inc(hists, 1)

                        steps(pe, NG, 0, hist)
                        pe.wait_ge(sums, 1)
                        sums_of = blk_sum[:].rearrange("p a b -> p (a b)")
                        nc.tensor.matmul(ps_e[:, 0, :], tri[:], stay[:], start=True, stop=True)
                        nc.tensor.matmul(ps_e[:, 1, :], ones[:], stay[:], start=True, stop=True)
                        nc.tensor.matmul(ps_b[:, 0, :], tri[:], sums_of, start=True, stop=True)
                        nc.tensor.matmul(ps_b[:, 1, :], ones[:], sums_of, start=True, stop=True).then_inc(sums_ps, 1)

                clear((loaded_dst, loaded_src, loaded_w, tab_stored, iotas, consts, hots, hists, wts, sums, sums_ps,
                       deg_ready, sd_ready, dve_step, tab_ready))

        LOADS_W = 14

        def edges(tag, table, first):
            rows = table.shape[0]
            with ExitStack() as ctx:
                def sb(name, shape, dt=F32):
                    return ctx.enter_context(nc.sbuf_tensor(f"{tag}_{name}", shape, dt))

                phase = []

                def sem(name):
                    phase.append(ctx.enter_context(nc.semaphore(f"{tag}_{name}")))
                    return phase[-1]

                def gather_sem(name):
                    return keep.enter_context(nc.semaphore(f"{tag}_{name}"))

                def two(name, shape, dt=F32):
                    return [sb(f"{name}{i}", shape, dt) for i in range(2)]

                dstb = two("dstb", [P, Q, P], I32)
                eq = two("eq", [P, Q, P])
                cr = two("cr", [P, Q, P])
                idx = two("idx", [P, Q], I32)
                msg = two("msg", [P, Q, D])
                res = two("res", [P, Q, D])
                dst_loaded = [sem(f"dst_loaded{i}") for i in range(2)]
                rows_in = [gather_sem(f"rows_in{i}") for i in range(2)]
                stored = [sem(f"stored{i}") for i in range(2)]
                idx_ready, eq_ready, eq_used, cr_used, summed, msg_ready = (
                    sem(n) for n in ("idx_ready", "eq_ready", "eq_used", "cr_used", "summed", "msg_ready"))
                if first:
                    bs = two("bs", [P, Q, 6])
                    mv = two("mv", [P, Q, 2])
                    sd = two("sd", [P, Q])
                    sc = two("sc", [P, Q])
                    nb = two("nb", [P, Q])
                    stat_step, sd_ready, sc_step, normed = (
                        sem(n) for n in ("stat_step", "sd_ready", "sc_step", "normed"))
                if first:
                    dpos = two("dpos", [P, Q], I32)
                    dsrc = two("dsrc", [P, Q])
                    dinv_in = [gather_sem(f"dinv_in{i}") for i in range(2)]
                bank = [ctx.enter_context(nc.psum_tensor(f"{tag}_bank{k}", [P, 512], F32)) for k in range(Q)]

                with nc.Block() as block:
                    @block.sync
                    def _(sp):
                        def step(t, u):
                            g, s = t, u
                            if live(g, NG):
                                if after(g):
                                    sp.wait_ge(eq_ready, g - 1)
                                sp.dma_start(dstb[s][:].rearrange("p k e -> p (k e)"),
                                             dst_row[0:1, ds(g * BLK + 1, BLK)].broadcast_to([P, BLK])
                                             ).then_inc(dst_loaded[s], 16)
                            g = t - 3
                            s = (u - 3) % 2
                            if live(g, NG):
                                sp.wait_ge(summed, g * Q + Q)
                                sp.dma_start(seg_t[:, ds(g * Q, Q), :], res[s][:]).then_inc(stored[s], 16)

                        steps(sp, NG, 3, step)
                        sp.wait_ge(stored[0], 16 * ((NG + 1) // 2))
                        sp.wait_ge(stored[1], 16 * (NG // 2))

                    @block.gpsimd
                    def _(pool):
                        bound = nc.gpsimd.to_reg(rows - 1)
                        if first:
                            bound_d = nc.gpsimd.to_reg(P * NCOL - 1)

                        def step(t, s):
                            g = t
                            if after(g):
                                pool.wait_ge(eq_used, g * Q - Q)
                            if first:
                                nc.gpsimd.tensor_copy(dpos[s][:], src_pos[:, ds(g * Q, Q)])
                            nc.gpsimd.tensor_copy(idx[s][:], src_i[:, ds(g * Q, Q)]).then_inc(idx_ready, 1)
                            pool.wait_ge(idx_ready, g + 1)
                            pool.sem_inc(issuing, 1)
                            for k in range(Q):
                                nc.gpsimd.indirect_dma_start(
                                    msg[s][:, k, :], None, table,
                                    bass.IndirectOffsetOnAxis(ap=idx[s][:, k:k + 1], axis=0),
                                    bounds_check=bound, oob_is_err=False).then_inc(rows_in[s], 16)
                            if first:
                                for k in range(Q):
                                    nc.gpsimd.indirect_dma_start(
                                        dsrc[s][:, k:k + 1], None, dinv_tab,
                                        bass.IndirectOffsetOnAxis(ap=dpos[s][:, k:k + 1], axis=0),
                                        bounds_check=bound_d, oob_is_err=False).then_inc(dinv_in[s], 16)

                        steps(pool, NG, 0, step)

                    @block.scalar
                    def _(act):
                        def step(t, u):
                            g, s = t - 2, u % 2
                            def evac(k):
                                act.wait_ge(cr_used, g * Q + k + 1)
                                nc.scalar.activation(res[s][:, k, :], bank[k][:, 0:D], ACT.Copy).then_inc(summed, 1)

                            if live(g, NG):
                                if after(g):
                                    act.wait_ge(stored[s], half(g) * 16)
                                evac(0)
                                evac(1)
                            g1, s1 = t - 1, (u - 1) % 2
                            if first and live(g1, NG):
                                act.wait_ge(stat_step, g1 * 2 + 2)
                                nc.scalar.activation(sd[s1][:], mv[s1][:, :, 1], ACT.Sqrt,
                                                     bias=eps[:]).then_inc(sd_ready, 1)
                                act.wait_ge(sc_step, g1 * 3 + 3)
                                for k in range(Q):
                                    i = nc.scalar.activation(msg[s1][:, k, :], msg[s1][:, k, :], ACT.Relu,
                                                             bias=nb[s1][:, k:k + 1], scale=sc[s1][:, k:k + 1])
                                i.then_inc(normed, 1)
                            if live(g, NG):
                                evac(2)
                                evac(3)

                        steps(act, NG, 2, step)

                    @block.vector
                    def _(dve):
                        v = nc.vector
                        v.memset(res[1][:, Q - 1, :], 0.0).then_inc(msg_ready, 1)

                        def step(t, u):
                            g, s = t - 1, (u - 1) % 2
                            if not live(g, NG):
                                return
                            if first:
                                dve.wait_ge(rows_in[s], half(g) * 16 * Q + 16 * Q)
                                for k in range(Q):
                                    i = v.bn_stats(bs[s][:, k, :], msg[s][:, k, :])
                                i.then_inc(stat_step, 1)
                            dve.wait_ge(dst_loaded[s], half(g) * 16 + 16)
                            if after(g):
                                dve.wait_ge(cr_used, g * Q - Q)
                            v.tensor_tensor(eq[s][:], dstb[s][:],
                                            dst_f[:, ds(g * Q, Q)].unsqueeze(2).broadcast_to([P, Q, P]), ALU.is_equal)
                            if first:
                                dve.wait_ge(stat_step, g * 2 + 1)
                            v.tensor_tensor(cr[s][:], dstb[s][:],
                                            carry_f[:, ds(g * Q, Q)].unsqueeze(2).broadcast_to([P, Q, P]),
                                            ALU.is_equal).then_inc(eq_ready, 1)
                            if first:
                                for k in range(Q):
                                    i = v.bn_aggr(mv[s][:, k, :], bs[s][:, k, :])
                                i.then_inc(stat_step, 1)
                                dve.wait_ge(sd_ready, g + 1)
                                v.reciprocal(sc[s][:], sd[s][:]).then_inc(sc_step, 1)
                                dve.wait_ge(sc_step, g * 3 + 1)
                                dve.wait_ge(dinv_in[s], half(g) * 16 * Q + 16 * Q)
                                v.tensor_tensor(sc[s][:], sc[s][:], dsrc[s][:], ALU.mult).then_inc(sc_step, 1)
                                dve.wait_ge(sc_step, g * 3 + 2)
                                v.scalar_tensor_tensor(nb[s][:], mv[s][:, :, 0], -1.0, sc[s][:],
                                                       ALU.mult, ALU.mult).then_inc(sc_step, 1)

                        steps(dve, NG, 1, step)

                    @block.tensor
                    def _(pe):
                        pe.wait_ge(msg_ready, 1)

                        def inside(g, s, k):
                            if k == 0:
                                pe.wait_ge(eq_ready, g + 1)
                                if first:
                                    pe.wait_ge(normed, g + 1)
                                else:
                                    pe.wait_ge(rows_in[s], half(g) * 16 * Q + 16 * Q)
                            if not isinstance(g, int) or g >= 1:
                                pe.wait_ge(summed, g * Q + k - 3)
                            nc.tensor.matmul(bank[k][:, 0:D], eq[s][:, k, :], msg[s][:, k, :],
                                             start=True, stop=False).then_inc(eq_used, 1)

                        def carry(g, s, k):
                            if not isinstance(g, int) or g * Q + k >= 1:
                                pe.wait_ge(summed, g * Q + k)
                            before = res[s][:, k - 1, :] if k else res[1 - s][:, Q - 1, :]
                            nc.tensor.matmul(bank[k][:, 0:D], cr[s][:, k, :], before,
                                             start=False, stop=True).then_inc(cr_used, 1)

                        def step(t, u):
                            g1, s1 = t - 1, (u - 1) % 2
                            g, s = t - 2, u % 2
                            for k in range(Q):
                                if k < 2:
                                    if live(g, NG):
                                        inside(g, s, k + 2)
                                elif live(g1, NG):
                                    inside(g1, s1, k - 2)
                                if live(g, NG):
                                    carry(g, s, k)

                        steps(pe, NG, 2, step)


                clear(phase)

        def batch_norm_coefficients(tag, stats, b_c, g_c, be_c):
            r = NPAD / N
            with ExitStack() as ctx:
                mv = ctx.enter_context(nc.sbuf_tensor(f"{tag}_mv", [P, KD, 2], F32))
                m = ctx.enter_context(nc.sbuf_tensor(f"{tag}_m", [P, KD], F32))
                w = ctx.enter_context(nc.sbuf_tensor(f"{tag}_w", [P, KD], F32))
                dve_step = ctx.enter_context(nc.semaphore(f"{tag}_dve_step"))
                var_ready = ctx.enter_context(nc.semaphore(f"{tag}_var_ready"))
                sd_ready = ctx.enter_context(nc.semaphore(f"{tag}_sd_ready"))
                with nc.Block() as block:
                    @block.scalar
                    def _(act):
                        act.wait_ge(var_ready, 1)
                        nc.scalar.activation(w[:], w[:], ACT.Sqrt, bias=eps[:]).then_inc(sd_ready, 1)

                    @block.vector
                    def _(dve):
                        done = [0]

                        def link(ins):
                            done[0] += 1
                            ins.then_inc(dve_step, 1)
                            dve.wait_ge(dve_step, done[0])

                        v = nc.vector
                        v.bn_aggr(mv[:, 0, :], stats[:, 0, :, :].rearrange("p b k -> p (b k)"))
                        link(v.bn_aggr(mv[:, 1, :], stats[:, 1, :, :].rearrange("p b k -> p (b k)")))
                        link(v.tensor_tensor(w[:], mv[:, :, 0], mv[:, :, 0], ALU.mult))
                        link(v.scalar_tensor_tensor(w[:], w[:], -(r - 1.0), mv[:, :, 1], ALU.mult, ALU.add))
                        v.tensor_scalar(w[:], w[:], r, None, ALU.mult).then_inc(var_ready, 1)
                        link(v.scalar_tensor_tensor(m[:], mv[:, :, 0], r, b_c[:], ALU.mult, ALU.add))
                        dve.wait_ge(sd_ready, 1)
                        link(v.reciprocal(w[:], w[:]))
                        link(v.tensor_tensor(bn_s[:], w[:], g_c[:], ALU.mult))
                        link(v.tensor_tensor(m[:], b_c[:], m[:], ALU.subtract))
                        link(v.tensor_tensor(m[:], m[:], bn_s[:], ALU.mult))
                        link(v.tensor_tensor(bn_t[:], m[:], be_c[:], ALU.add))

        def load_rows(sp, dst, rows, b, arrived):
            if isinstance(b, int) and b == NB - 1 and rows.shape[0] != NB * P:
                sp.dma_start(dst[0:TAIL], rows[b * P:b * P + TAIL, :]).then_inc(arrived, 16)
            else:
                sp.dma_start(dst[:], rows[ds(b * P, P), :]).then_inc(arrived, 16)

        def flat(t):
            return t[:].rearrange("p q d -> p (q d)")

        def aggregate(tag, src, first, dst_t, stats):
            with ExitStack() as ctx:
                def sb(name, shape, dt=F32):
                    return ctx.enter_context(nc.sbuf_tensor(f"{tag}_{name}", shape, dt))

                def ps(name):
                    return ctx.enter_context(nc.psum_tensor(f"{tag}_{name}", [P, KD, BLK], F32))

                def sem(name):
                    return ctx.enter_context(nc.semaphore(f"{tag}_{name}"))

                def two(name, shape, dt=F32):
                    return [sb(f"{name}{i}", shape, dt) for i in range(2)]

                xb = two("xb", [P, Q, D])
                own = two("own", [P, Q, D])
                gath = two("gath", [P, Q, D])
                idx = two("idx", [P, Q], I32)
                scal = two("scal", [P, 2, Q])
                ob = two("ob", [P, KD, BLK])
                ps_t = [ps(f"ps_t{i}") for i in range(2)]
                x_in = [sem(f"x_in{i}") for i in range(2)]
                seg_in = [sem(f"seg_in{i}") for i in range(2)]
                stored = [sem(f"stored{i}") for i in range(2)]
                (cleared, idx_ready, scal_ready, own_ready, combined, turned, copied, counted) = (
                    sem(n) for n in ("cleared", "idx_ready", "scal_ready", "own_ready", "combined", "turned",
                                     "copied", "counted"))
                if first:
                    bs = two("bs", [P, Q, 6])
                    mv = two("mv", [P, Q, 2])
                    sd = two("sd", [P, Q])
                    sc = two("sc", [P, Q])
                    nb = two("nb", [P, Q])
                    ht = two("ht", [P, KD, BLK])
                    ps_m = [ps(f"ps_m{i}") for i in range(2)]
                    stat_step, sd_ready, sc_step, ht_ready, multiplied = (
                        sem(n) for n in ("stat_step", "sd_ready", "sc_step", "ht_ready", "multiplied"))
                made, ps_o = (multiplied, ps_m) if first else (turned, ps_t)
                lag_o = 4 if first else 3

                with nc.Block() as block:
                    @block.sync
                    def _(sp):
                        def step(t, u):
                            if live(t, NB):
                                if isinstance(t, int) and t < 2 and first:
                                    sp.wait_ge(cleared, 1)
                                if after(t):
                                    sp.wait_ge(own_ready, t - 1)
                                load_rows(sp, xb[u % 2][:].rearrange("p q d -> p (q d)"), src, t, x_in[u % 2])
                            b, s = t - lag_o, (u - lag_o) % 2
                            if live(b, NB):
                                sp.wait_ge(copied, b + 1)
                                sp.dma_start(dst_t[ds(b * P, P), :],
                                             ob[s][:].rearrange("p c n -> p (c n)")).then_inc(stored[s], 16)

                        steps(sp, NB, lag_o, step)
                        sp.wait_ge(stored[0], 16 * (NB // 2))
                        sp.wait_ge(stored[1], 16 * (NB // 2))

                    @block.gpsimd
                    def _(pool):
                        for i in range(2):
                            if first:
                                nc.gpsimd.memset(xb[i][:], 0.0)
                            nc.gpsimd.memset(gath[i][:], 0.0).then_inc(idx_ready, 1)
                        pool.wait_ge(idx_ready, 2)
                        pool.sem_inc(cleared, 1)
                        bound = nc.gpsimd.to_reg(E - 1)

                        def step(t, u):
                            if after(t):
                                pool.wait_ge(combined, t - 1)
                            nc.gpsimd.tensor_copy(idx[u][:], end_index[:, ds(t * Q, Q)]).then_inc(idx_ready, 1)
                            pool.wait_ge(idx_ready, t + 3)
                            pool.sem_inc(issuing, 1)
                            for q in range(Q):
                                nc.gpsimd.indirect_dma_start(
                                    gath[u][:, q, :], None, seg,
                                    bass.IndirectOffsetOnAxis(ap=idx[u][:, q:q + 1], axis=0),
                                    bounds_check=bound, oob_is_err=False).then_inc(seg_in[u], 16)

                        steps(pool, NB, 0, step)

                    @block.scalar
                    def _(act):
                        def step(t, u):
                            b, s = t - 2, u % 2
                            if live(b, NB):
                                if after(b):
                                    act.wait_ge(turned, b - 1)
                                act.wait_ge(scal_ready, b + 1)
                                if not first:
                                    act.wait_ge(x_in[s], half(b) * 16 + 16)
                                for q in range(Q):
                                    if first:
                                        i = nc.scalar.activation(own[s][:, q, :], xb[s][:, q, :], ACT.Relu,
                                                                 bias=nb[s][:, q:q + 1], scale=sc[s][:, q:q + 1])
                                    else:
                                        i = nc.scalar.activation(own[s][:, q, :], xb[s][:, q, :], ACT.Copy,
                                                                 scale=scal[s][:, 0, q:q + 1])
                                i.then_inc(own_ready, 1)
                            b, s = t - lag_o, (u - lag_o) % 2
                            if live(b, NB):
                                act.wait_ge(made, b + 1)
                                if after(b):
                                    act.wait_ge(counted, b - 1)
                                    act.wait_ge(stored[s], half(b) * 16)
                                nc.scalar.activation(ob[s][:], ps_o[s][:], ACT.Copy).then_inc(copied, 1)
                            if first:
                                b, s = t - 1, (u - 1) % 2
                                if live(b, NB):
                                    act.wait_ge(stat_step, 2 * b + 2)
                                    nc.scalar.activation(sd[s][:], mv[s][:, :, 1], ACT.Sqrt,
                                                         bias=eps[:]).then_inc(sd_ready, 1)
                                b, s = t - 2, u % 2
                                if live(b, NB):
                                    act.wait_ge(turned, b + 1)
                                    if after(b):
                                        act.wait_ge(multiplied, b - 1)
                                    nc.scalar.activation(ht[s][:], ps_t[s][:], ACT.Copy).then_inc(ht_ready, 1)

                        steps(act, NB, lag_o, step)

                    @block.vector
                    def _(dve):
                        v = nc.vector

                        def step(t, u):
                            b, s = t - 1, (u - 1) % 2
                            if first and live(b, NB):
                                dve.wait_ge(x_in[s], half(b) * 16 + 16)
                                for q in range(Q):
                                    i = v.bn_stats(bs[s][:, q, :], xb[s][:, q, :])
                                i.then_inc(stat_step, 1)
                                if after(b):
                                    dve.wait_ge(combined, b - 1)
                                dve.wait_ge(stat_step, 2 * b + 1)
                                v.tensor_copy(scal[s][:].rearrange("p a q -> p (a q)"),
                                              dh[:, ds(b, 1), :, :].rearrange("p b a q -> p (b a q)"))
                                for q in range(Q):
                                    i = v.bn_aggr(mv[s][:, q, :], bs[s][:, q, :])
                                i.then_inc(stat_step, 1)
                            b, s = t - 2, u % 2
                            if live(b, NB):
                                dve.wait_ge(own_ready, b + 1)
                                dve.wait_ge(seg_in[s], half(b) * 16 * Q + 16 * Q)
                                for q in range(Q):
                                    i = v.scalar_tensor_tensor(own[s][:, q, :], gath[s][:, q, :],
                                                               scal[s][:, 1, q:q + 1], own[s][:, q, :],
                                                               ALU.mult, ALU.add)
                                i.then_inc(combined, 1)
                            b, s = t - 1, (u - 1) % 2
                            if live(b, NB):
                                if first:
                                    dve.wait_ge(sd_ready, b + 1)
                                    v.reciprocal(sc[s][:], sd[s][:]).then_inc(sc_step, 1)
                                    dve.wait_ge(sc_step, 2 * b + 1)
                                    v.tensor_tensor(sc[s][:], sc[s][:], dinv2[:, ds(b * Q, Q)],
                                                    ALU.mult).then_inc(sc_step, 1)
                                    dve.wait_ge(sc_step, 2 * b + 2)
                                    v.scalar_tensor_tensor(nb[s][:], mv[s][:, :, 0], -1.0, sc[s][:],
                                                           ALU.mult, ALU.mult).then_inc(scal_ready, 1)
                                else:
                                    v.tensor_copy(scal[s][:].rearrange("p a q -> p (a q)"),
                                                  dh[:, ds(b, 1), :, :].rearrange("p b a q -> p (b a q)")
                                                  ).then_inc(scal_ready, 1)
                            b, s = t - lag_o, (u - lag_o) % 2
                            if live(b, NB):
                                dve.wait_ge(copied, b + 1)
                                for c in range(KD):
                                    i = v.bn_stats(stats[:, c, ds(b, 1), :].rearrange("p b k -> p (b k)"),
                                                   ob[s][:, c, :])
                                i.then_inc(counted, 1)

                        steps(dve, NB, lag_o, step)

                    @block.tensor
                    def _(pe):
                        def step(t, u):
                            b, s = t - 3, (u - 3) % 2
                            if first and live(b, NB):
                                pe.wait_ge(ht_ready, b + 1)
                                if after(b):
                                    pe.wait_ge(copied, b - 1)
                                for o in range(KD):
                                    for c in range(KD):
                                        i = nc.tensor.matmul(ps_m[s][:, o, :], w1[:, c, o * P:(o + 1) * P],
                                                             ht[s][:, c, :], start=(c == 0), stop=(c == KD - 1))
                                i.then_inc(multiplied, 1)
                            b, s = t - 2, u % 2
                            if live(b, NB):
                                pe.wait_ge(combined, b + 1)
                                if after(b):
                                    if first:
                                        pe.wait_ge(ht_ready, b - 1)
                                    else:
                                        pe.wait_ge(copied, b - 1)
                                for c in range(KD):
                                    for q in range(Q):
                                        i = nc.tensor.transpose(ps_t[s][:, c, q * P:(q + 1) * P],
                                                                own[s][:, q, c * P:(c + 1) * P], ident[:])
                                i.then_inc(turned, 1)

                        steps(pe, NB, 3, step)

        def lin2():
            with ExitStack() as ctx:
                def sb(name, shape, dt=F32):
                    return ctx.enter_context(nc.sbuf_tensor(f"l2_{name}", shape, dt))

                def sem(name):
                    return ctx.enter_context(nc.semaphore(f"l2_{name}"))

                zb = [sb(f"zb{i}", [P, KD, BLK]) for i in range(2)]
                hb = [sb(f"hb{i}", [P, KD, BLK]) for i in range(2)]
                gb = [sb(f"gb{i}", [P, Q, D]) for i in range(2)]
                ps_g = [ctx.enter_context(nc.psum_tensor(f"l2_ps{i}", [P, Q, D], F32)) for i in range(2)]
                z_in = [sem(f"z_in{i}") for i in range(2)]
                stored = [sem(f"stored{i}") for i in range(2)]
                h_ready, multiplied, scaled = (sem(n) for n in ("h_ready", "multiplied", "scaled"))
                rank_st = [sb(f"rank_st{i}", [P, Q], I32) for i in range(2)]
                node_st = [sb(f"node_st{i}", [P, Q], I32) for i in range(2)]
                staged = sem("staged")
                put = [sem(f"put{i}") for i in range(2)]
                with nc.Block() as block:
                    @block.gpsimd
                    def _(pool):
                        bound = nc.gpsimd.to_reg(NPAD - 1)

                        def step(b, s):
                            if after(b):
                                pool.wait_ge(put[s], half(b) * 16 * Q)
                            nc.gpsimd.tensor_copy(rank_st[s][:], free_rank[:, ds(b * Q, Q)])
                            nc.gpsimd.tensor_copy(node_st[s][:], node_id[:, ds(b * Q, Q)]).then_inc(staged, 1)
                            pool.wait_ge(staged, b + 1)
                            pool.sem_inc(issuing, 1)
                            for q in range(Q):
                                nc.gpsimd.indirect_dma_start(
                                    free_tab, bass.IndirectOffsetOnAxis(ap=rank_st[s][:, q:q + 1], axis=0),
                                    node_st[s][:, q:q + 1], None,
                                    bounds_check=bound, oob_is_err=False).then_inc(put[s], 16)

                        steps(pool, NB, 0, step)
                        pool.wait_ge(put[0], 16 * Q * (NB // 2))
                        pool.wait_ge(put[1], 16 * Q * (NB // 2))

                    @block.sync
                    def _(sp):
                        def step(t, u):
                            if live(t, NB):
                                if after(t):
                                    sp.wait_ge(h_ready, t - 1)
                                sp.dma_start(zb[u % 2][:].rearrange("p c n -> p (c n)"),
                                             o1t[ds(t * P, P), :]).then_inc(z_in[u % 2], 16)
                            b, s = t - 2, u % 2
                            if live(b, NB):
                                sp.wait_ge(scaled, b + 1)
                                sp.dma_start(g2_r[ds(b * P, P), :],
                                             gb[s][:].rearrange("p q d -> p (q d)")).then_inc(stored[s], 16)

                        steps(sp, NB, 2, step)
                        sp.wait_ge(stored[0], 16 * (NB // 2))
                        sp.wait_ge(stored[1], 16 * (NB // 2))

                    @block.scalar
                    def _(act):
                        def step(b, s):
                            act.wait_ge(z_in[s], half(b) * 16 + 16)
                            if after(b):
                                act.wait_ge(multiplied, b - 1)
                            for c in range(KD):
                                i = nc.scalar.activation(hb[s][:, c, :], zb[s][:, c, :], ACT.Relu,
                                                         bias=bn_t[:, c:c + 1], scale=bn_s[:, c:c + 1])
                            i.then_inc(h_ready, 1)

                        steps(act, NB, 0, step)

                    @block.tensor
                    def _(pe):
                        def step(b, s):
                            pe.wait_ge(h_ready, b + 1)
                            if after(b):
                                pe.wait_ge(scaled, b - 1)
                            for q in range(Q):
                                for c in range(KD):
                                    i = nc.tensor.matmul(ps_g[s][:, q, :], hb[s][:, c, q * P:(q + 1) * P],
                                                         w2[:, c, :], start=(c == 0), stop=(c == KD - 1))
                            i.then_inc(multiplied, 1)

                        steps(pe, NB, 0, step)

                    @block.vector
                    def _(dve):
                        def step(b, s):
                            dve.wait_ge(multiplied, b + 1)
                            if after(b):
                                dve.wait_ge(stored[s], half(b) * 16)
                            nc.vector.tensor_tensor(gb[s][:], ps_g[s][:],
                                                    dinv[:, ds(b * Q, Q)].unsqueeze(2).broadcast_to([P, Q, D]),
                                                    ALU.mult).then_inc(scaled, 1)

                        steps(dve, NB, 0, step)

        def residual():
            with ExitStack() as ctx:
                def sb(name, shape, dt=F32):
                    return ctx.enter_context(nc.sbuf_tensor(f"rs_{name}", shape, dt))

                def sem(name):
                    return ctx.enter_context(nc.semaphore(f"rs_{name}"))

                def two(name, shape, dt=F32):
                    return [sb(f"{name}{i}", shape, dt) for i in range(2)]

                zb = two("zb", [P, KD, BLK])
                hb = two("hb", [P, KD, BLK])
                xb = two("xb", [P, Q, D])
                x1b = [sb(f"x1b{i}", [P, Q, DX]) for i in range(4)]
                bs, mv, sd = two("bs", [P, Q, 6]), two("mv", [P, Q, 2]), two("sd", [P, Q])
                rank_st, node_st = two("rank_st", [P, Q], I32), two("node_st", [P, Q], I32)
                ps_h = [ctx.enter_context(nc.psum_tensor(f"rs_ps{i}", [P, Q, D], F32)) for i in range(2)]
                z_in = [sem(f"z_in{i}") for i in range(2)]
                x_in = [sem(f"x_in{i}") for i in range(2)]
                stored = [sem(f"stored{i}") for i in range(4)]
                got = [sem(f"got{i}") for i in range(2)]
                h_ready, turned, added, counted, aggregated, sd_ready, inv_ready, row_ready, staged, kept, rest_in = (
                    sem(n) for n in ("h_ready", "turned", "added", "counted", "aggregated", "sd_ready", "inv_ready",
                                     "row_ready", "staged", "kept", "rest_in"))
                with nc.Block() as block:
                    @block.sync
                    def _(sp):
                        off = sp.value_load(free_off[0:1, 0:1], min_val=0, max_val=E)
                        sp.dma_start(slot_node[1][:], free_tab[ds(off, P * NT), :].rearrange(
                            "(p a) o -> p (a o)", p=P)).then_inc(rest_in, 16)

                        def step(t, u):
                            if live(t, NB):
                                s = u % 2
                                if after(t):
                                    sp.wait_ge(h_ready, t - 1)
                                sp.dma_start(zb[s][:].rearrange("p c n -> p (c n)"),
                                             o2t[ds(t * P, P), :]).then_inc(z_in[s], 16)
                                if after(t):
                                    sp.wait_ge(added, t - 1)
                                load_rows(sp, xb[s][:].rearrange("p q d -> p (q d)"), x_r, t, x_in[s])
                            b, s = t - 2, (u - 2) % 4
                            if live(b, NB):
                                sp.wait_ge(row_ready, b + 1)
                                sp.dma_start(x1_r[ds(b * P, P), :],
                                             x1b[s][:].rearrange("p q d -> p (q d)")).then_inc(stored[s], 16)

                        steps(sp, NB, 2, step, unroll=4)
                        for i in range(4):
                            sp.wait_ge(stored[i], 16 * len(range(i, NB, 4)))

                    @block.gpsimd
                    def _(pool):
                        bound = nc.gpsimd.to_reg(NPAD - 1)

                        def step(t, u):
                            g, s = t, u
                            if live(g, NG):
                                if after(g):
                                    pool.wait_ge(kept, g - 1)
                                nc.gpsimd.tensor_copy(rank_st[s][:], slot_rank[:, ds(g * Q, Q)])
                                nc.gpsimd.tensor_copy(node_st[s][:], dst_i[:, ds(g * Q, Q)]).then_inc(staged, 1)
                                pool.wait_ge(staged, g + 1)
                                pool.sem_inc(issuing, 1)
                                for k in range(Q):
                                    nc.gpsimd.indirect_dma_start(
                                        node_st[s][:, k:k + 1], None, free_tab,
                                        bass.IndirectOffsetOnAxis(ap=rank_st[s][:, k:k + 1], axis=0),
                                        bounds_check=bound, oob_is_err=False).then_inc(got[s], 16)
                            g, s = t - 1, (u - 1) % 2
                            if live(g, NG):
                                pool.wait_ge(got[s], half(g) * 16 * Q + 16 * Q)
                                nc.gpsimd.tensor_copy(slot_node[0][:, ds(g * Q, Q)], node_st[s][:]).then_inc(kept, 1)

                        steps(pool, NG, 1, step)

                    @block.scalar
                    def _(act):
                        def step(t, u):
                            b, s = t, u % 2
                            if live(b, NB):
                                act.wait_ge(z_in[s], half(b) * 16 + 16)
                                if after(b):
                                    act.wait_ge(turned, b - 1)
                                for c in range(KD):
                                    i = nc.scalar.activation(hb[s][:, c, :], zb[s][:, c, :], ACT.Relu,
                                                             bias=bn_t[:, c:c + 1], scale=bn_s[:, c:c + 1])
                                i.then_inc(h_ready, 1)
                            b, s = t - 1, (u - 1) % 2
                            if live(b, NB):
                                act.wait_ge(aggregated, b + 1)
                                nc.scalar.activation(sd[s][:], mv[s][:, :, 1], ACT.Sqrt, bias=eps[:]
                                                     ).then_inc(sd_ready, 1)

                        steps(act, NB, 1, step)

                    @block.tensor
                    def _(pe):
                        def step(b, s):
                            pe.wait_ge(h_ready, b + 1)
                            if after(b):
                                pe.wait_ge(added, b - 1)
                            for q in range(Q):
                                for c in range(KD):
                                    i = nc.tensor.transpose(ps_h[s][:, q, c * P:(c + 1) * P],
                                                            hb[s][:, c, q * P:(q + 1) * P], ident[:])
                            i.then_inc(turned, 1)

                        steps(pe, NB, 0, step)

                    @block.vector
                    def _(dve):
                        v = nc.vector

                        def step(t, u):
                            b, s, s4 = t, u % 2, u % 4
                            b1, s1 = t - 1, (u - 1) % 2
                            if live(b, NB):
                                dve.wait_ge(turned, b + 1)
                                dve.wait_ge(x_in[s], half(b) * 16 + 16)
                                if after(b, 4):
                                    dve.wait_ge(stored[s4], quarter(b) * 16)
                                if live(b1, NB):
                                    dve.wait_ge(counted, b1 + 1)
                                v.tensor_tensor(x1b[s4][:, :, 0:D], ps_h[s][:], xb[s][:], ALU.add).then_inc(added, 1)
                            if live(b1, NB):
                                if not live(b, NB):
                                    dve.wait_ge(counted, b1 + 1)
                                for q in range(Q):
                                    i = v.bn_aggr(mv[s1][:, q, :], bs[s1][:, q, :])
                                i.then_inc(aggregated, 1)
                            if live(b, NB):
                                dve.wait_ge(added, b + 1)
                                for q in range(Q):
                                    i = v.bn_stats(bs[s][:, q, :], x1b[s4][:, q, 0:D])
                                i.then_inc(counted, 1)
                            if live(b1, NB):
                                s14 = (u - 1) % 4
                                dve.wait_ge(sd_ready, b1 + 1)
                                v.reciprocal(x1b[s14][:, :, D], sd[s1][:]).then_inc(inv_ready, 1)
                                dve.wait_ge(inv_ready, b1 + 1)
                                v.scalar_tensor_tensor(x1b[s14][:, :, D + 1], mv[s1][:, :, 0], -1.0,
                                                       x1b[s14][:, :, D], ALU.mult, ALU.mult).then_inc(row_ready, 1)

                        steps(dve, NB, 1, step, unroll=4)
                        dve.wait_ge(rest_in, 16)
                        v.tensor_tensor(slot_node[1][:], slot_node[1][:], pad_slot[:], ALU.add)

        def gru(tag, with_edges):
            nodes = slot_node[0 if with_edges else 1]
            with ExitStack() as ctx:
                def sb(name, shape, dt=F32):
                    return ctx.enter_context(nc.sbuf_tensor(f"{tag}_{name}", shape, dt))

                def ps(name, shape):
                    return ctx.enter_context(nc.psum_tensor(f"{tag}_{name}", shape, F32))

                def sem(name):
                    return ctx.enter_context(nc.semaphore(f"{tag}_{name}"))

                def two(name, shape, dt=F32):
                    return [sb(f"{name}{i}", shape, dt) for i in range(2)]

                xb = [sb(f"xb{i}", [P, Q, DX]) for i in range(4)]
                fb = two("fb", [P, Q, D])
                own_idx = two("own_idx", [P, Q], I32)
                out_idx = two("out_idx", [P, Q], I32)
                h2 = two("h2", [P, Q, D])
                ht = two("ht", [P, KD, BLK])
                h_hi, h_lo = (two(n, [P, KD, BLK], F32R) for n in ("h_hi", "h_lo"))
                rg, zg, ng, tg = (two(n, [P, BLK]) for n in ("rg", "zg", "ng", "tg"))
                hn = two("hn", [P, KD, BLK])
                ps_a = ps("ps_a", [P, KD, BLK])
                ps_r, ps_z, ps_hn = (ps(n, [P, BLK]) for n in ("ps_r", "ps_z", "ps_hn"))
                x_in = [sem(f"x_in{i}") for i in range(4)]
                stored = [sem(f"stored{i}") for i in range(2)]
                (staged, h2_ready, turned, back, r_ps, z_ps, hn_ps, r_ready, z_ready,
                 n_ready, reset, copied, low, dif, zdif, new_h, finished) = (
                    sem(n) for n in ("staged", "h2_ready", "turned", "back", "r_ps", "z_ps", "hn_ps", "r_ready",
                                     "z_ready", "n_ready", "reset", "copied", "low", "dif", "zdif", "new_h",
                                     "finished"))
                if with_edges:
                    dstb = two("dstb", [P, BLK + 2], I32)
                    typ = two("typ", [NREL, Q, P], I32)
                    hot = two("hot", [NREL, Q, P], F32R)
                    eq = two("eq", [P, Q, P], F32R)
                    goes_on = two("goes_on", [P, Q, P])
                    is_last = two("is_last", [P, BLK])
                    msg_idx = two("msg_idx", [P, Q], I32)
                    raw = two("raw", [P, Q, DX])
                    msg = sb("msg", [P, Q, D])
                    m_hi, m_lo = (sb(n, [P, Q, D], F32R) for n in ("m_hi", "m_lo"))
                    sums = two("sums", [P, KD, BLK])
                    red = sb("red", [P, KD, BLK])
                    r_hi, r_lo = (two(n, [P, KD, BLK], F32R) for n in ("r_hi", "r_lo"))
                    ps_b = ps("ps_b", [P, KD, BLK])
                    ps_in = ps("ps_in", [P, BLK])
                    rows_in = [sem(f"rows_in{i}") for i in range(2)]
                    dst_in = [sem(f"dst_in{i}") for i in range(2)]
                    (masks, msg_ready, rel_ready, with_rel, m_high, m_split, summed, chained, masked, r_high,
                     in_ps, summed_n) = (
                        sem(n) for n in ("masks", "msg_ready", "rel_ready", "with_rel", "m_high", "m_split",
                                         "summed", "chained", "masked", "r_high", "in_ps", "summed_n"))
                else:
                    in_ps = summed_n = None

                def later(n):
                    return not isinstance(n, int) or n >= 1

                with nc.Block() as block:
                    @block.sync
                    def _(sp):
                        if not with_edges:
                            return

                        def step(t, s):
                            if after(t):
                                sp.wait_ge(masks, t - 1)
                            sp.dma_start(dstb[s][:], dst_row[0:1, ds(t * BLK, BLK + 2)].broadcast_to([P, BLK + 2])
                                         ).then_inc(dst_in[s], 16)
                            sp.dma_start(typ[s][:].rearrange("p k e -> p (k e)"),
                                         type_row[0:1, ds(t * BLK, BLK)].broadcast_to([NREL, BLK])
                                         ).then_inc(dst_in[s], 16)

                        steps(sp, NG, 0, step)

                    @block.gpsimd
                    def _(pool):
                        for i in range(4):
                            nc.gpsimd.memset(xb[i][:], 0.0).then_inc(staged, 1)
                        pool.wait_ge(staged, 4)
                        bound = nc.gpsimd.to_reg(N - 1)

                        def step(t, u):
                            s = u % 2
                            b = t - 4
                            if live(b, NG):
                                if after(b):
                                    pool.wait_ge(stored[s], half(b) * 16 * Q)
                                nc.gpsimd.tensor_copy(out_idx[s][:], nodes[:, ds(b * Q, Q)])
                                pool.wait_ge(finished, b + 1)
                                pool.sem_inc(issuing, 1)
                            if live(t, NG):
                                if after(t):
                                    pool.wait_ge(h2_ready, t - 1)
                                nc.gpsimd.tensor_copy(own_idx[s][:], nodes[:, ds(t * Q, Q)])
                                if with_edges:
                                    nc.gpsimd.tensor_copy(msg_idx[s][:], src_i[:, ds(t * Q, Q)])
                            nc.gpsimd.memset(spare[:], 0.0).then_inc(staged, 1)
                            pool.wait_ge(staged, t + 5)
                            pool.sem_inc(issuing, 1)
                            if live(t, NG):
                                for q in range(Q):
                                    if with_edges:
                                        nc.gpsimd.indirect_dma_start(
                                            raw[s][:, q, :], None, x1s,
                                            bass.IndirectOffsetOnAxis(ap=msg_idx[s][:, q:q + 1], axis=0),
                                            bounds_check=bound, oob_is_err=False).then_inc(rows_in[s], 16)
                                for q in range(Q):
                                    nc.gpsimd.indirect_dma_start(
                                        xb[u][:, q, :], None, x1s,
                                        bass.IndirectOffsetOnAxis(ap=own_idx[s][:, q:q + 1], axis=0),
                                        bounds_check=bound, oob_is_err=False).then_inc(x_in[u], 16)
                            if live(b, NG):
                                for q in range(Q):
                                    nc.gpsimd.indirect_dma_start(
                                        out, bass.IndirectOffsetOnAxis(ap=out_idx[s][:, q:q + 1], axis=0),
                                        fb[s][:, q, :], None,
                                        bounds_check=bound, oob_is_err=False).then_inc(stored[s], 16)

                        steps(pool, NG, 4, step, unroll=4)
                        pool.wait_ge(stored[0], 16 * Q * ((NG + 1) // 2))
                        pool.wait_ge(stored[1], 16 * Q * (NG // 2))

                    @block.scalar
                    def _(act):
                        def step(t, u):
                            b, s, s4 = t - 1, (u - 1) % 2, (u - 1) % 4
                            if live(b, NG):
                                if with_edges:
                                    act.wait_ge(rows_in[s], half(b) * 16 * Q + 16 * Q)
                                    if later(b):
                                        act.wait_ge(m_split, b)
                                    for q in range(Q):
                                        i = nc.scalar.activation(msg[:, q, :], raw[s][:, q, 0:D], ACT.Relu,
                                                                 bias=raw[s][:, q, D + 1:D + 2],
                                                                 scale=raw[s][:, q, D:D + 1])
                                    i.then_inc(msg_ready, 1)
                                act.wait_ge(x_in[s4], quarter(b) * 16 * Q + 16 * Q)
                                if after(b):
                                    act.wait_ge(turned, b - 1)
                                for q in range(Q):
                                    i = nc.scalar.activation(h2[s][:, q, :], xb[s4][:, q, 0:D], ACT.Relu,
                                                             bias=xb[s4][:, q, D + 1:D + 2],
                                                             scale=xb[s4][:, q, D:D + 1])
                                i.then_inc(h2_ready, 1)

                            def reset_of(b, h):
                                n = 2 * b + h
                                act.wait_ge(r_ps, n + 1)
                                if not isinstance(n, int) or n >= 2:
                                    act.wait_ge(new_h, n - 1)
                                nc.scalar.activation(rg[h][:], ps_r[:], ACT.Sigmoid,
                                                     bias=brz[:, h:h + 1]).then_inc(r_ready, 1)

                            def candidate_of(b, h):
                                n = 2 * b + h
                                act.wait_ge(summed_n if with_edges else reset, n + 1)
                                nc.scalar.activation(ng[h][:], tg[h][:], ACT.Tanh,
                                                     bias=bih[:, 4 + h:5 + h]).then_inc(n_ready, 1)

                            def update_of(b, h):
                                n = 2 * b + h
                                act.wait_ge(z_ps, n + 1)
                                nc.scalar.activation(zg[h][:], ps_z[:], ACT.Sigmoid,
                                                     bias=brz[:, 2 + h:3 + h]).then_inc(z_ready, 1)

                            b2 = t - 2
                            if live(b2, NG):
                                reset_of(b2, 0)
                                candidate_of(b2, 0)
                            if with_edges and live(b, NG):
                                act.wait_ge(with_rel, b + 1)
                                if later(b):
                                    act.wait_ge(summed, b)
                                nc.scalar.activation(m_hi[:], msg[:], ACT.Copy).then_inc(m_high, 1)
                            if live(b2, NG):
                                update_of(b2, 0)
                            if live(b, NG):
                                act.wait_ge(turned, b + 1)
                                if after(b):
                                    act.wait_ge(z_ps, 2 * b - 2)
                                    act.wait_ge(new_h, 2 * b - 2)
                                nc.scalar.activation(h_hi[s][:], ps_a[:], ACT.Copy).then_inc(copied, 1)
                                nc.scalar.activation(ht[s][:], ps_a[:], ACT.Copy).then_inc(copied, 1)
                            if live(b2, NG):
                                reset_of(b2, 1)
                            if with_edges and live(b, NG):
                                act.wait_ge(masked, b + 1)
                                nc.scalar.activation(r_hi[s][:], red[:], ACT.Copy).then_inc(r_high, 1)
                            if live(b2, NG):
                                candidate_of(b2, 1)
                                update_of(b2, 1)

                        steps(act, NG, 2, step, unroll=4)

                    @block.vector
                    def _(dve):
                        v = nc.vector
                        if with_edges:
                            v.memset(sums[1][:], 0.0).then_inc(chained, 1)

                        def step(t, u):
                            b, s = t - 1, (u - 1) % 2

                            def reset_gate(b, h):
                                n = 2 * b + h
                                dve.wait_ge(hn_ps, n + 1)
                                dve.wait_ge(r_ready, n + 1)
                                if not isinstance(n, int) or n >= 2:
                                    dve.wait_ge(n_ready, n - 1)
                                v.scalar_tensor_tensor(tg[h][:], ps_hn[:], bhh[:, 4 + h:5 + h], rg[h][:],
                                                       ALU.add, ALU.mult).then_inc(reset, 1)

                            def candidate(b, h):
                                if with_edges:
                                    n = 2 * b + h
                                    dve.wait_ge(in_ps, n + 1)
                                    dve.wait_ge(reset, n + 1)
                                    v.tensor_tensor(tg[h][:], tg[h][:], ps_in[:], ALU.add).then_inc(summed_n, 1)

                            def new_state(b, s, h):
                                n = 2 * b + h
                                dve.wait_ge(n_ready, n + 1)
                                dve.wait_ge(copied, 2 * b + 2)
                                if after(b):
                                    dve.wait_ge(back, b - 1)
                                v.tensor_tensor(hn[s][:, h, :], ht[s][:, h, :], ng[h][:], ALU.subtract).then_inc(dif, 1)
                                dve.wait_ge(z_ready, n + 1)
                                dve.wait_ge(dif, n + 1)
                                v.tensor_tensor(hn[s][:, h, :], hn[s][:, h, :], zg[h][:], ALU.mult).then_inc(zdif, 1)
                                dve.wait_ge(zdif, n + 1)
                                v.tensor_tensor(hn[s][:, h, :], hn[s][:, h, :], ng[h][:], ALU.add).then_inc(new_h, 1)

                            if with_edges and live(b, NG):
                                dve.wait_ge(dst_in[s], half(b) * 32 + 32)
                                if after(b):
                                    dve.wait_ge(summed, b - 1)
                                    dve.wait_ge(masked, b - 1)
                                of_tile = dstb[s][:, 1:BLK + 1].rearrange("p (k e) -> p k e", k=Q)
                                v.tensor_tensor(eq[s][:], of_tile,
                                                dst_f[:, ds(b * Q, Q)].unsqueeze(2).broadcast_to([P, Q, P]),
                                                ALU.is_equal)
                                before = dstb[s][:, 0:BLK].rearrange("p (k e) -> p k e", k=Q)[:, :, 0:1]
                                v.tensor_tensor(goes_on[s][:], of_tile, before.broadcast_to([P, Q, P]), ALU.is_equal)
                                v.tensor_tensor(is_last[s][:], dstb[s][:, 1:BLK + 1], dstb[s][:, 2:BLK + 2],
                                                ALU.not_equal)
                                v.tensor_scalar(hot[s][:], typ[s][:], pidx[0:NREL, :], None,
                                                ALU.is_equal).then_inc(masks, 1)
                            b2, s2 = t - 2, u % 2
                            if live(b2, NG):
                                reset_gate(b2, 0)
                            b3, s3, u3 = t - 3, (u - 3) % 4, (u - 3) % 2
                            if live(b3, NG):
                                dve.wait_ge(back, b3 + 1)
                                dve.wait_ge(x_in[s3], quarter(b3) * 16 * Q + 16 * Q)
                                if after(b3):
                                    dve.wait_ge(stored[u3], half(b3) * 16 * Q)
                                v.tensor_tensor(fb[u3][:], ps_a[:].rearrange("p c n -> p (c n)").rearrange(
                                    "p (q d) -> p q d", q=Q), xb[s3][:, :, 0:D], ALU.add).then_inc(finished, 1)
                            if live(b2, NG):
                                candidate(b2, 0)
                            if with_edges and live(b, NG):
                                dve.wait_ge(rel_ready, b + 1)
                                dve.wait_ge(msg_ready, b + 1)
                                v.tensor_tensor(msg[:], msg[:], ps_b[:].rearrange("p c n -> p (c n)").rearrange(
                                    "p (q d) -> p q d", q=Q), ALU.add).then_inc(with_rel, 1)
                                dve.wait_ge(m_high, b + 1)
                                v.tensor_tensor(m_lo[:], msg[:], m_hi[:].bitcast(F32),
                                                ALU.subtract).then_inc(m_split, 1)
                            if live(b2, NG):
                                new_state(b2, s2, 0)
                            if live(b, NG):
                                if with_edges:
                                    dve.wait_ge(summed, b + 1)
                                    for k in range(Q):
                                        dve.wait_ge(chained, b * Q + k + 1)
                                        for c in range(KD):
                                            end = (sums[s][:, c, k * P - 1:k * P] if k else
                                                   sums[1 - s][:, c, BLK - 1:BLK])
                                            i = v.scalar_tensor_tensor(
                                                sums[s][:, c, k * P:(k + 1) * P], goes_on[s][:, k, :], end,
                                                ps_b[:, c, k * P:(k + 1) * P], ALU.mult, ALU.add)
                                        i.then_inc(chained, 1)
                                if after(b):
                                    dve.wait_ge(z_ps, 2 * b - 2)
                                dve.wait_ge(copied, 2 * b + 2)
                                v.tensor_tensor(h_lo[s][:], ht[s][:], h_hi[s][:].bitcast(F32),
                                                ALU.subtract).then_inc(low, 1)
                                if with_edges:
                                    dve.wait_ge(chained, b * Q + Q + 1)
                                    if later(b):
                                        dve.wait_ge(low, 2 * b)
                                    v.tensor_tensor(red[:], sums[s][:],
                                                    is_last[s][:].unsqueeze(1).broadcast_to([P, KD, BLK]),
                                                    ALU.mult).then_inc(masked, 1)
                            if live(b2, NG):
                                reset_gate(b2, 1)
                            if with_edges and live(b, NG):
                                dve.wait_ge(r_high, b + 1)
                                v.tensor_tensor(r_lo[s][:], red[:], r_hi[s][:].bitcast(F32),
                                                ALU.subtract).then_inc(low, 1)
                            if live(b2, NG):
                                candidate(b2, 1)
                                new_state(b2, s2, 1)

                        steps(dve, NG, 3, step, unroll=4)

                    @block.tensor
                    def _(pe):
                        lows = 2 if with_edges else 1
                        both = ("hh", "ih") if with_edges else ("hh",)

                        def product(bank, s, sides, chunk, signal):
                            terms = []
                            for side in sides:
                                hi, lo = (h_hi, h_lo) if side == "hh" else (r_hi, r_lo)
                                for c in range(KD):
                                    terms += [(whi[side], hi, c), (whi[side], lo, c), (wlo[side], hi, c)]
                            for n, (w, a, c) in enumerate(terms):
                                i = nc.tensor.matmul(bank[:], w[:, c, chunk * P:(chunk + 1) * P], a[s][:, c, :],
                                                     start=(n == 0), stop=(n == len(terms) - 1))
                            i.then_inc(signal, 1)

                        def step(t, u):
                            b, s = t - 1, (u - 1) % 2
                            b2, s2 = t - 2, u % 2
                            b3, s3 = t - 3, (u - 3) % 2

                            def first_gates(h):
                                n = 2 * b2 + h
                                if h == 0:
                                    pe.wait_ge(low, lows * b2 + lows)
                                if later(n):
                                    pe.wait_ge(r_ready, n)
                                product(ps_r, s2, both, h, r_ps)
                                if later(n):
                                    pe.wait_ge(reset, n)
                                product(ps_hn, s2, ("hh",), 4 + h, hn_ps)

                            def last_gates(h):
                                n = 2 * b2 + h
                                if with_edges:
                                    if later(n):
                                        pe.wait_ge(summed_n, n)
                                    product(ps_in, s2, ("ih",), 4 + h, in_ps)
                                if later(n):
                                    pe.wait_ge(z_ready, n)
                                product(ps_z, s2, both, 2 + h, z_ps)

                            if live(b2, NG):
                                first_gates(0)
                            if live(b3, NG):
                                pe.wait_ge(new_h, 2 * b3 + 2)
                                if live(b2, NG):
                                    pe.wait_ge(copied, 2 * b2 + 2)
                                rows = ps_a[:].rearrange("p c n -> p (c n)")
                                for q in range(Q):
                                    for c in range(KD):
                                        i = nc.tensor.transpose(rows[:, q * D + c * P:q * D + (c + 1) * P],
                                                                hn[s3][:, c, q * P:(q + 1) * P], ident[:])
                                i.then_inc(back, 1)
                            if with_edges and live(b, NG):
                                pe.wait_ge(masks, b + 1)
                                if later(b):
                                    pe.wait_ge(chained, b * Q + 1)
                                vec = ps_b[:].rearrange("p c n -> p (c n)").rearrange("p (q d) -> p q d", q=Q)
                                for q in range(Q):
                                    nc.tensor.matmul(vec[:, q, :], hot[s][:, q, :], rel_hi[:], start=True, stop=False)
                                    i = nc.tensor.matmul(vec[:, q, :], hot[s][:, q, :], rel_lo[:],
                                                         start=False, stop=True)
                                i.then_inc(rel_ready, 1)
                            if live(b2, NG):
                                last_gates(0)
                            if live(b, NG):
                                pe.wait_ge(h2_ready, b + 1)
                                if live(b3, NG):
                                    pe.wait_ge(finished, b3 + 1)
                                if live(b2, NG):
                                    pe.wait_ge(copied, 2 * b2 + 2)
                                for c in range(KD):
                                    for q in range(Q):
                                        i = nc.tensor.transpose(ps_a[:, c, q * P:(q + 1) * P],
                                                                h2[s][:, q, c * P:(c + 1) * P], ident[:])
                                i.then_inc(turned, 1)
                                if with_edges:
                                    pe.wait_ge(m_split, b + 1)
                                    for c in range(KD):
                                        for k in range(Q):
                                            for m in (m_hi, m_lo):
                                                i = nc.tensor.matmul(ps_b[:, c, k * P:(k + 1) * P],
                                                                     m[:, k, c * P:(c + 1) * P], eq[s][:, k, :],
                                                                     start=(m is m_hi), stop=(m is m_lo))
                                    i.then_inc(summed, 1)
                            if live(b2, NG):
                                first_gates(1)
                                last_gates(1)

                        steps(pe, NG, 3, step, unroll=4)

        setup()
        edges("e1", x, True)
        with nc.sbuf_tensor("stats1", [P, KD, NB, 6], F32) as stats1:
            aggregate("c1", x_r, True, o1t, stats1)
            batch_norm_coefficients("b1", stats1, bn_in["b1c"], bn_in["g1c"], bn_in["be1c"])
        lin2()
        edges("e2", g2s, False)
        with nc.sbuf_tensor("stats2", [P, KD, NB, 6], F32) as stats2:
            aggregate("a2", g2_r, False, o2t, stats2)
            batch_norm_coefficients("b2", stats2, bn_in["b2c"], bn_in["g2c"], bn_in["be2c"])
        residual()
        gru("ge", True)
        gru("gf", False)


def kernel(**inputs):
    import numpy as np
    import concourse.bacc as bacc
    from concourse import mybir
    from concourse.bass_utils import run_bass_kernel_spmd

    tile = 128
    group = 4 * tile
    n_edges = inputs["dst"].shape[0]
    padded = -(-n_edges // group) * group

    def pad(a, fill):
        return np.concatenate([np.asarray(a), np.full(padded - n_edges, fill, np.int32)])

    dst, src, typ = pad(inputs["dst"], 60000), pad(inputs["src"], 0), pad(inputs["edge_type_16"], 0)
    around = np.concatenate([[-1], dst, [60000]]).astype(np.int32)
    arrays = {
        "x": inputs["x"],
        "dst_row": around.reshape(1, -1),
        "dst_col": dst.reshape(-1, tile).T,
        "next_col": around[2:].reshape(-1, tile).T,
        "src_col": src.reshape(-1, tile).T,
        "type_row": typ.reshape(1, -1),
    }
    for name in ("W1", "b1", "g1", "be1", "W2", "b2", "g2", "be2"):
        arrays[name] = inputs[f"L0_gnn_{name}"]
    for name in ("relvectors", "w_ih", "w_hh", "b_ih", "b_hh"):
        arrays[name] = inputs[f"L1_gnn_{name}"]
    for name, a in arrays.items():
        if a.ndim == 1:
            arrays[name] = np.asarray(a).reshape(-1, tile).T
    arrays = {f"in_{k}": np.ascontiguousarray(v) for k, v in arrays.items()}

    nc = bacc.Bacc("TRN2", target_bir_lowering=False, num_devices=1)
    args = [nc.dram_tensor(k, a.shape, mybir.dt.from_np(a.dtype), kind="ExternalInput").ap()
            for k, a in arrays.items()]
    out = nc.dram_tensor("out", inputs["x"].shape, mybir.dt.float32, kind="ExternalOutput").ap()
    build_program(nc, *args, out)
    r = run_bass_kernel_spmd(nc, [arrays], core_ids=[0])
    return r.results[0]["out"]
```

```python
def build_program(nc, x, dst_row, dst_col, next_col, src_col, type_row, W1, b1, g1, be1, W2, b2, g2, be2,
                  rel, w_ih, w_hh, b_ih, b_hh, out):
    from contextlib import ExitStack
    import concourse.bass as bass
    from concourse import mybir

    F32 = mybir.dt.float32
    F32R = mybir.dt.float32r
    F16 = mybir.dt.float16
    I32 = mybir.dt.int32
    ALU = mybir.AluOpType
    ACT = mybir.ActivationFunctionType
    AX = mybir.AxisListType

    P = 128
    N, D = x.shape
    E = 25000
    Q = 4
    BLK = P * Q
    NB = -(-N // BLK)
    TAIL = (N - (NB - 1) * BLK) // Q
    NCOL = NB * Q
    NPAD = NB * BLK
    NT = dst_col.shape[1]
    NG = NT // Q
    KD = D // P
    G3 = w_ih.shape[0] // P
    NREL = rel.shape[0]
    EPS = 1e-5
    ROW = Q * D
    DX = D + 2
    NONE = 1.0e6
    ds = bass.ds

    assert TAIL * Q + (NB - 1) * BLK == N and NG * Q == NT

    dinv_tab = nc.dram_tensor("dinv_tab", (P * NCOL, 1), F32, kind="Internal").ap()
    seg = nc.dram_tensor("seg", (NT * P, D), F32, kind="Internal").ap()
    o1t = nc.dram_tensor("o1t", (NB * P, ROW), F32, kind="Internal").ap()
    g2s = nc.dram_tensor("g2s", (NPAD, D), F32, kind="Internal").ap()
    o2t = nc.dram_tensor("o2t", (NB * P, ROW), F32, kind="Internal").ap()
    x1s = nc.dram_tensor("x1s", (NPAD, DX), F32, kind="Internal").ap()
    free_tab = nc.dram_tensor("free_tab", (NPAD, 1), I32, kind="Internal").ap()

    def rows4(t):
        return t.rearrange("(r q) d -> r (q d)", q=Q)

    x_r, g2_r, x1_r = rows4(x), rows4(g2s), rows4(x1s)
    seg_t = seg.rearrange("(t p) d -> p t d", p=P)

    def steps(eng, n, lag, step, unroll=2):
        head = -(-(lag + 4) // unroll) * unroll
        end = head + (n - 1 - head) // unroll * unroll
        for t in range(head):
            step(t, t % unroll)
        with eng.Fori(head // unroll, end // unroll) as k:
            for u in range(unroll):
                step(k * unroll + u, u)
        for t in range(end, n + lag):
            step(t, t % unroll)

    def live(b, n):
        return not isinstance(b, int) or 0 <= b < n

    def after(b, slots=2):
        return not isinstance(b, int) or b >= slots

    def half(b):
        return b // 2 if isinstance(b, int) else b >> 1

    def quarter(b):
        return b // 4 if isinstance(b, int) else b >> 2

    with ExitStack() as keep:
        def ksb(name, shape, dt=F32):
            return keep.enter_context(nc.sbuf_tensor(name, shape, dt))

        ident = ksb("ident", [P, P])
        pidx = ksb("pidx", [P, 1])
        eps = ksb("eps", [P, 1])
        dinv = ksb("dinv", [P, NCOL])
        dinv2 = ksb("dinv2", [P, NCOL])
        has = ksb("has", [P, NCOL])
        dh = ksb("dh", [P, NB, 2, Q])
        end_index = ksb("end_index", [P, NCOL], I32)
        dst_f = ksb("dst_f", [P, NT])
        carry_f = ksb("carry_f", [P, NT])
        src_i = ksb("src_i", [P, NT], I32)
        src_pos = ksb("src_pos", [P, NT], I32)
        w1 = ksb("w1", [P, KD, D])
        w2 = ksb("w2", [P, KD, D])
        w2_hi, w2_lo = ksb("w2_hi", [P, KD, D], F32R), ksb("w2_lo", [P, KD, D], F32R)
        rel_sb = ksb("rel_sb", [NREL, D])
        spare = ksb("spare", [P, 1])
        rel_hi = ksb("rel_hi", [NREL, D], F32R)
        rel_lo = ksb("rel_lo", [NREL, D], F32R)
        bn_in = {k: ksb(k, [P, KD]) for k in ("b1c", "g1c", "be1c", "b2c", "g2c", "be2c")}
        bih = ksb("bih", [P, G3])
        bhh = ksb("bhh", [P, G3])
        brz = ksb("brz", [P, G3])
        whi = {k: ksb(f"{k}_hi", [P, KD, G3 * P], F32R) for k in ("ih", "hh")}
        wlo = {k: ksb(f"{k}_lo", [P, KD, G3 * P], F32R) for k in ("ih", "hh")}
        bn_s = ksb("bn_s", [P, KD])
        bn_t = ksb("bn_t", [P, KD])
        issuing = keep.enter_context(nc.semaphore("issuing"))
        dst_i = ksb("dst_i", [P, NT], I32)
        node_id = ksb("node_id", [P, NCOL], I32)
        free_rank = ksb("free_rank", [P, NCOL], I32)
        slot_rank = ksb("slot_rank", [P, NT], I32)
        free_off = ksb("free_off", [P, 1], I32)
        slot_node = [ksb(f"slot_node{i}", [P, NT], I32) for i in range(2)]
        pad_slot = ksb("pad_slot", [P, NT], I32)

        dma_sems = [keep.enter_context(nc.semaphore(f"swdge{i}")) for i in range(46)]

        class Phase:
            before = None

            def __init__(self, tag):
                self.tag = tag
                self.memory, self.signals = ExitStack(), ExitStack()
                self.sems = []
                self.previous, Phase.before = Phase.before, self

            def sb(self, name, shape, dt=F32, n=None):
                if n is None:
                    return self.memory.enter_context(nc.sbuf_tensor(f"{self.tag}_{name}", shape, dt))
                return [self.sb(f"{name}{i}", shape, dt) for i in range(n)]

            def ps(self, name, shape, n=None):
                if n is None:
                    return self.memory.enter_context(nc.psum_tensor(f"{self.tag}_{name}", shape, F32))
                return [self.ps(f"{name}{i}", shape) for i in range(n)]

            def sem(self, name, n=None):
                if n is not None:
                    return [self.sem(f"{name}{i}") for i in range(n)]
                self.sems.append(self.signals.enter_context(nc.semaphore(f"{self.tag}_{name}")))
                return self.sems[-1]

            def gather_sems(self, n):
                return [dma_sems.pop() for _ in range(n)]

            def zero_previous(self, pool):
                if self.previous:
                    for s in self.previous.sems:
                        pool.sem_clear(s)

            def end(self):
                self.memory.close()
                if self.previous:
                    self.previous.signals.close()

        def setup():
            phase = Phase("su")
            sb, sem, ctx = phase.sb, phase.sem, phase.memory
            if True:
                next_i = sb("next_i", [P, NT], I32)
                no_table = sb("no_table", [P, NCOL], I32)
                ia, ib, ic = (sb(n, [P, NT], I32) for n in ("ia", "ib", "ic"))
                fa, fb = sb("fa", [P, NT]), sb("fb", [P, NT])
                dst_a, dst_p = sb("dst_a", [P, NT]), sb("dst_p", [P, NT])
                row_i = sb("row_i", [P, NCOL], I32)
                row_h = sb("row_h", [P, NCOL], F16)
                row_f = sb("row_f", [P, P])
                pidx_i = sb("pidx_i", [P, 1], I32)
                last = sb("last", [P, 1])
                node_mask = sb("node_mask", [P, 1])
                tri = sb("tri", [P, P])
                ones = sb("ones", [P, P])
                one_row = sb("one_row", [P, NT])
                hot_a = [sb(f"hot_a{i}", [P, Q, NCOL], F16) for i in range(2)]
                hot_p = [sb(f"hot_p{i}", [P, Q, P], F16) for i in range(2)]
                wraw = {k: sb(f"w{k}_raw", [P, G3, D]) for k in ("ih", "hh")}
                cnt = sb("cnt", [P, NB, Q])
                node_f, rank_f = sb("node_f", [P, NCOL]), sb("rank_f", [P, NCOL])
                next_f, stay = sb("next_f", [P, NT]), sb("stay", [P, NT])
                deg = sb("deg", [P, NCOL])
                blk_sum = sb("blk_sum", [P, 2, NB])
                base, tot, run = sb("base", [P, 2, NB]), sb("tot", [P, 2, NB]), sb("run", [P, 2, NB])
                cum = sb("cum", [P, 2, NB, Q])
                etot, erun = sb("etot", [P, NT]), sb("erun", [P, NT])
                big = sb("big", [P, NCOL])
                ps_w = phase.ps("ps_w", [P, KD, G3 * P], n=2)
                ps_e = ps_w[0][:].rearrange("p c n -> p (c n)")[:, 0:2 * NT].rearrange("p (a n) -> p a n", a=2)
                ps_c = ctx.enter_context(nc.psum_tensor("ps_c", [P, NCOL], F32))
                ps_b = ctx.enter_context(nc.psum_tensor("ps_b", [P, 2, 2 * NB], F32))
                loaded_dst, loaded_src, loaded_w, tab_stored = (sem(n) for n in (
                    "loaded_dst", "loaded_src", "loaded_w", "tab_stored"))
                iotas, consts, hots, hists, wts, sums, sums_ps, deg_ready, sd_ready, dve_step, tab_ready = (
                    sem(n) for n in ("iotas", "consts", "hots", "hists", "wts", "sums", "sums_ps",
                                     "deg_ready", "sd_ready", "dve_step", "tab_ready"))

                with nc.Block() as block:
                    @block.sync
                    def _(sp):
                        sp.dma_start(dst_i[:], dst_col).then_inc(loaded_dst, 16)
                        sp.dma_start(next_i[:], next_col).then_inc(loaded_w, 16)
                        sp.dma_start(src_i[:], src_col).then_inc(loaded_src, 16)
                        n = 16
                        for k, w in (("ih", w_ih), ("hh", w_hh)):
                            sp.dma_start(wraw[k][:], w.rearrange("(c p) d -> p c d", p=P)).then_inc(loaded_w, 16)
                            n += 16
                        for t, w in ((w1, W1), (w2, W2)):
                            sp.dma_start(t[:], w.rearrange("(c p) d -> p c d", p=P)).then_inc(loaded_w, 16)
                            n += 16
                        sp.dma_start(rel_sb[:], rel).then_inc(loaded_w, 16)
                        n += 16
                        for k, v in (("b1c", b1), ("g1c", g1), ("be1c", be1), ("b2c", b2), ("g2c", g2), ("be2c", be2)):
                            sp.dma_start(bn_in[k][:], v).then_inc(loaded_w, 16)
                            n += 16
                        for t, v in ((bih, b_ih), (bhh, b_hh)):
                            sp.dma_start(t[:], v).then_inc(loaded_w, 16)
                            n += 16
                        assert n == 16 * LOADS_W
                        sp.wait_ge(iotas, 1)
                        sp.dma_start(free_tab.rearrange("(p a) o -> p (a o)", p=P), no_table[:]).then_inc(tab_stored, 16)
                        sp.wait_ge(tab_ready, 1)
                        sp.dma_start(dinv_tab.rearrange("(p a) o -> p (a o)", p=P), dinv[:]).then_inc(tab_stored, 16)
                        sp.wait_ge(tab_stored, 32)

                    @block.gpsimd
                    def _(pool):
                        phase.zero_previous(pool)
                        nc.gpsimd.iota(row_i[:], pattern=[[1, NCOL]], base=0, channel_multiplier=0)
                        nc.gpsimd.memset(ones[:], 1.0)
                        nc.gpsimd.memset(one_row[:], 1.0)
                        nc.gpsimd.memset(eps[:], EPS)
                        nc.gpsimd.memset(no_table[:], 0)
                        nc.gpsimd.iota(node_id[:].rearrange("p (b q) -> p b q", q=Q), pattern=[[BLK, NB], [1, Q]],
                                       base=0, channel_multiplier=Q)
                        nc.gpsimd.iota(pad_slot[:], pattern=[[1, NT]], base=0, channel_multiplier=NT)
                        nc.gpsimd.iota(pidx_i[:], pattern=[[1, 1]], base=0, channel_multiplier=1).then_inc(iotas, 1)

                    @block.scalar
                    def _(act):
                        act.wait_ge(deg_ready, 1)
                        nc.scalar.activation(big[:], deg[:], ACT.Sqrt).then_inc(sd_ready, 1)

                    @block.vector
                    def _(dve):
                        done = [0]

                        def link(ins):
                            done[0] += 1
                            ins.then_inc(dve_step, 1)
                            dve.wait_ge(dve_step, done[0])

                        v = nc.vector
                        dve.wait_ge(iotas, 1)
                        link(v.tensor_copy(pidx[:], pidx_i[:]))
                        v.tensor_copy(row_h[:], row_i[:])
                        link(v.tensor_copy(row_f[:], row_i[:, 0:P]))
                        v.tensor_scalar(tri[:], row_f[:], pidx[:], None, ALU.is_gt)
                        v.tensor_scalar(last[:], pidx[:], float(P - 1), None, ALU.is_equal)
                        v.tensor_scalar(node_mask[:], pidx[:], float(TAIL), None, ALU.is_lt)
                        link(v.tensor_scalar(ident[:], row_f[:], pidx[:], None, ALU.is_equal))
                        v.sem_inc(consts, 1)

                        def column(node_i):
                            v.tensor_scalar(ia[:], node_i[:], 9, 2, ALU.logical_shift_right, ALU.logical_shift_left)
                            link(v.tensor_scalar(ib[:], node_i[:], 3, None, ALU.bitwise_and))
                            v.tensor_scalar(ic[:], node_i[:], 2, P - 1, ALU.logical_shift_right, ALU.bitwise_and)
                            link(v.tensor_tensor(ia[:], ia[:], ib[:], ALU.bitwise_or))

                        dve.wait_ge(loaded_dst, 16)
                        column(dst_i)
                        v.tensor_copy(dst_a[:], ia[:])
                        v.tensor_copy(dst_f[:], dst_i[:])
                        link(v.tensor_copy(dst_p[:], ic[:]))

                        def hot(t, u):
                            if live(t, NG):
                                if after(t):
                                    dve.wait_ge(hists, t - 1)
                                for k in range(Q):
                                    v.tensor_scalar(hot_a[u][:, k, :], row_h[:], dst_a[:, ds(t * Q + k, 1)], None,
                                                    ALU.is_equal)
                                    i = v.tensor_scalar(hot_p[u][:, k, :], row_h[:, 0:P],
                                                        dst_p[:, ds(t * Q + k, 1)], None, ALU.is_equal)
                                i.then_inc(hots, 1)

                        steps(dve, NG, 0, hot)

                        for i, k in enumerate(("ih", "hh")):
                            dve.wait_ge(wts, i + 1)
                            link(v.tensor_copy(whi[k][:], ps_w[i][:]))
                            v.tensor_tensor(wlo[k][:], ps_w[i][:], whi[k][:].bitcast(F32), ALU.subtract)
                        dve.wait_ge(loaded_w, 16 * LOADS_W)
                        v.tensor_tensor(brz[:], bih[:], bhh[:], ALU.add)
                        link(v.tensor_copy(w2_hi[:], w2[:]))
                        v.tensor_tensor(w2_lo[:], w2[:], w2_hi[:].bitcast(F32), ALU.subtract)
                        link(v.tensor_copy(rel_hi[:], rel_sb[:]))
                        v.tensor_tensor(rel_lo[:], rel_sb[:], rel_hi[:].bitcast(F32), ALU.subtract)
                        link(v.tensor_copy(next_f[:], next_i[:]))
                        link(v.tensor_tensor(stay[:], dst_f[:], next_f[:], ALU.is_equal))
                        link(v.tensor_scalar(next_f[:], dst_f[:], float(N), None, ALU.is_lt))
                        link(v.tensor_tensor(stay[:], stay[:], next_f[:], ALU.mult))
                        v.tensor_copy(slot_node[0][:], dst_i[:])
                        link(v.tensor_copy(erun[:], pad_slot[:]))
                        link(v.tensor_scalar(erun[:], erun[:], float(E), NONE, ALU.is_ge, ALU.mult))
                        link(v.tensor_copy(pad_slot[:], erun[:]))

                        v.memset(carry_f[:, 0:1], -1.0)
                        link(v.tensor_scalar(carry_f[:, 1:NT], dst_f[:, 0:NT - 1], 1.0, None, ALU.add))
                        link(v.tensor_scalar(carry_f[:, 1:NT], carry_f[:, 1:NT], last[:], -1.0, ALU.mult, ALU.add))

                        dve.wait_ge(loaded_src, 16)
                        column(src_i)
                        v.tensor_copy(fa[:], ia[:])
                        link(v.tensor_copy(fb[:], ic[:]))
                        link(v.scalar_tensor_tensor(fa[:], fb[:], float(NCOL), fa[:], ALU.mult, ALU.add))
                        link(v.tensor_copy(src_pos[:], fa[:]))

                        dve.wait_ge(hists, NG)
                        c2 = cnt[:].rearrange("p b q -> p (b q)")
                        link(v.tensor_copy(c2, ps_c[:]))
                        v.tensor_scalar(deg[:], c2, 1.0, None, ALU.add).then_inc(deg_ready, 1)
                        v.tensor_scalar(has[:], c2, 0.5, None, ALU.is_gt)
                        link(v.tensor_copy(cum[:, 0, :, 0], cnt[:, :, 0]))
                        link(v.tensor_copy(cum[:, 1, :, 0], has[:].rearrange("p (b q) -> p b q", q=Q)[:, :, 0]))
                        v.tensor_reduce(blk_sum[:, 0, :], cnt[:], AX.X, ALU.add)
                        v.tensor_reduce(blk_sum[:, 1, :], has[:].rearrange("p (b q) -> p b q", q=Q), AX.X,
                                        ALU.add).then_inc(sums, 1)
                        h3 = has[:].rearrange("p (b q) -> p b q", q=Q)
                        for q in range(1, Q):
                            v.tensor_tensor(cum[:, 0, :, q], cum[:, 0, :, q - 1], cnt[:, :, q], ALU.add)
                            link(v.tensor_tensor(cum[:, 1, :, q], cum[:, 1, :, q - 1], h3[:, :, q], ALU.add))
                        dve.wait_ge(sums_ps, 1)
                        link(v.tensor_copy(tot[:].rearrange("p a b -> p (a b)"), ps_b[:, 1, :]))
                        for a in range(2):
                            link(v.tensor_tensor_scan(run[:, a, :], ones[:, 0:NB], tot[:, a, :], 0.0,
                                                      ALU.mult, ALU.add))
                        link(v.tensor_scalar(base[:, 0, 0:1], run[:, 1, NB - 1:NB], -1.0, float(E),
                                             ALU.mult, ALU.add))
                        link(v.tensor_copy(free_off[:], base[:, 0, 0:1]))
                        link(v.tensor_tensor(run[:], run[:], tot[:], ALU.subtract))
                        link(v.tensor_tensor(base[:].rearrange("p a b -> p (a b)"), ps_b[:, 0, :],
                                             run[:].rearrange("p a b -> p (a b)"), ALU.add))
                        for a in range(2):
                            link(v.tensor_tensor(cum[:, a], cum[:, a],
                                                 base[:, a, :].unsqueeze(2).broadcast_to([P, NB, Q]), ALU.add))
                        link(v.tensor_copy(node_f[:], node_id[:]))
                        link(v.tensor_tensor(rank_f[:], node_f[:], cum[:, 1].rearrange("p b q -> p (b q)"),
                                             ALU.subtract))
                        link(v.scalar_tensor_tensor(rank_f[:], has[:], NONE, rank_f[:], ALU.mult, ALU.add))
                        link(v.tensor_scalar(node_f[:], node_f[:], float(N), NONE, ALU.is_ge, ALU.mult))
                        link(v.tensor_tensor(rank_f[:], rank_f[:], node_f[:], ALU.add))
                        link(v.tensor_copy(free_rank[:], rank_f[:]))
                        link(v.tensor_copy(etot[:], ps_e[:, 1, :]))
                        link(v.tensor_tensor_scan(erun[:], one_row[:], etot[:], 0.0, ALU.mult, ALU.add))
                        link(v.tensor_tensor(erun[:], erun[:], etot[:], ALU.subtract))
                        link(v.tensor_tensor(erun[:], erun[:], ps_e[:, 0, :], ALU.add))
                        link(v.tensor_scalar(stay[:], stay[:], -NONE, NONE, ALU.mult, ALU.add))
                        link(v.tensor_tensor(erun[:], erun[:], stay[:], ALU.add))
                        link(v.tensor_copy(slot_rank[:], erun[:]))
                        dve.wait_ge(sd_ready, 1)
                        link(v.reciprocal(dinv[:], big[:]))
                        link(v.tensor_scalar(dinv[:, NCOL - Q:NCOL], dinv[:, NCOL - Q:NCOL], node_mask[:], None,
                                             ALU.mult))
                        v.sem_inc(tab_ready, 1)
                        v.tensor_tensor(dinv2[:], dinv[:], dinv[:], ALU.mult)
                        d3 = dinv[:].rearrange("p (b q) -> p b q", q=Q)
                        v.tensor_copy(dh[:, :, 0, :], d3)
                        v.tensor_tensor(dh[:, :, 1, :], d3, h3, ALU.mult)
                        link(v.tensor_scalar(big[:], has[:], -NONE, NONE - 1.0, ALU.mult, ALU.add))
                        link(v.tensor_tensor(big[:], big[:], cum[:, 0].rearrange("p b q -> p (b q)"), ALU.add))
                        link(v.tensor_copy(end_index[:], big[:]))

                    @block.tensor
                    def _(pe):
                        pe.wait_ge(consts, 1)
                        pe.wait_ge(loaded_w, 16 * LOADS_W)
                        for i, k in enumerate(("ih", "hh")):
                            for c in range(G3):
                                for h in range(KD):
                                    t = nc.tensor.transpose(ps_w[i][:, h, c * P:(c + 1) * P],
                                                            wraw[k][:, c, h * P:(h + 1) * P], ident[:])
                            t.then_inc(wts, 1)

                        def hist(t, u):
                            pe.wait_ge(hots, t + 1)
                            for k in range(Q):
                                m = nc.tensor.matmul(ps_c[:], hot_p[u][:, k, :], hot_a[u][:, k, :],
                                                     start=isinstance(t, int) and t == 0 and k == 0,
                                                     stop=isinstance(t, int) and t == NG - 1 and k == Q - 1)
                            m.then_inc(hists, 1)

                        steps(pe, NG, 0, hist)
                        pe.wait_ge(sums, 1)
                        sums_of = blk_sum[:].rearrange("p a b -> p (a b)")
                        nc.tensor.matmul(ps_e[:, 0, :], tri[:], stay[:], start=True, stop=True)
                        nc.tensor.matmul(ps_e[:, 1, :], ones[:], stay[:], start=True, stop=True)
                        nc.tensor.matmul(ps_b[:, 0, :], tri[:], sums_of, start=True, stop=True)
                        nc.tensor.matmul(ps_b[:, 1, :], ones[:], sums_of, start=True, stop=True).then_inc(sums_ps, 1)

            phase.end()

        LOADS_W = 14

        def edges(tag, table, first):
            rows = table.shape[0]
            ph = Phase(tag)
            dstb = ph.sb("dstb", [P, BLK + 1], I32, n=2)
            eq = ph.sb("eq", [P, Q, P], n=2)
            goes_on = ph.sb("goes_on", [P, Q, P], n=2)
            idx = ph.sb("idx", [P, Q], I32, n=4)
            msg = ph.sb("msg", [P, Q, D], n=4)
            sums = ph.sb("sums", [P, KD, BLK], n=2)
            res = ph.sb("res", [P, Q, D], n=2)
            ps_s = ph.ps("ps_s", [P, KD, BLK], n=2)
            ps_t = ph.ps("ps_t", [P, Q, D], n=2)
            rows_in = ph.gather_sems(4)
            dst_in, stored = ph.sem("dst_in", n=2), ph.sem("stored", n=2)
            staged, masks, summed, chained, turned, copied = (
                ph.sem(n) for n in ("staged", "masks", "summed", "chained", "turned", "copied"))
            if first:
                bs, mv = ph.sb("bs", [P, Q, 6], n=2), ph.sb("mv", [P, Q, 2], n=2)
                sd, sc, nb = (ph.sb(n, [P, Q], n=2) for n in ("sd", "sc", "nb"))
                dpos, dsrc = ph.sb("dpos", [P, Q], I32, n=4), ph.sb("dsrc", [P, Q], n=4)
                dinv_in = ph.gather_sems(4)
                counted, aggregated, sd_ready, inv_ready, sc_ready, nb_ready, normed = (
                    ph.sem(n) for n in ("counted", "aggregated", "sd_ready", "inv_ready", "sc_ready", "nb_ready",
                                        "normed"))

            with nc.Block() as block:
                @block.sync
                def _(sp):
                    def step(t, u):
                        if live(t, NG):
                            if after(t):
                                sp.wait_ge(masks, t - 1)
                            sp.dma_start(dstb[u % 2][:], dst_row[0:1, ds(t * BLK, BLK + 1)].broadcast_to([P, BLK + 1])
                                         ).then_inc(dst_in[u % 2], 16)
                        g, s = t - 4, u % 2
                        if live(g, NG):
                            sp.wait_ge(copied, g + 1)
                            sp.dma_start(seg_t[:, ds(g * Q, Q), :], res[s][:]).then_inc(stored[s], 16)

                    steps(sp, NG, 4, step)
                    sp.wait_ge(stored[0], 16 * ((NG + 1) // 2))
                    sp.wait_ge(stored[1], 16 * (NG // 2))

                @block.gpsimd
                def _(pool):
                    bound = nc.gpsimd.to_reg(rows - 1)
                    if first:
                        bound_d = nc.gpsimd.to_reg(P * NCOL - 1)

                    def step(g, s):
                        if after(g, 4):
                            pool.wait_ge(summed, g - 3)
                        if first:
                            nc.gpsimd.tensor_copy(dpos[s][:], src_pos[:, ds(g * Q, Q)])
                        nc.gpsimd.tensor_copy(idx[s][:], src_i[:, ds(g * Q, Q)]).then_inc(staged, 1)
                        pool.wait_ge(staged, g + 1)
                        pool.sem_inc(issuing, 1)
                        for k in range(Q):
                            nc.gpsimd.indirect_dma_start(
                                msg[s][:, k, :], None, table,
                                bass.IndirectOffsetOnAxis(ap=idx[s][:, k:k + 1], axis=0),
                                bounds_check=bound, oob_is_err=False).then_inc(rows_in[s], 16)
                        if first:
                            for k in range(Q):
                                nc.gpsimd.indirect_dma_start(
                                    dsrc[s][:, k:k + 1], None, dinv_tab,
                                    bass.IndirectOffsetOnAxis(ap=dpos[s][:, k:k + 1], axis=0),
                                    bounds_check=bound_d, oob_is_err=False).then_inc(dinv_in[s], 16)

                    steps(pool, NG, 0, step, unroll=4)
                    ph.zero_previous(pool)

                @block.scalar
                def _(act):
                    def step(t, u):
                        g, s = t - 4, u % 2
                        if live(g, NG):
                            act.wait_ge(turned, g + 1)
                            if after(g):
                                act.wait_ge(stored[s], half(g) * 16)
                            nc.scalar.activation(res[s][:], ps_t[s][:], ACT.Copy).then_inc(copied, 1)
                        g, s, s4 = t - 1, (u - 1) % 2, (u - 1) % 4
                        if first and live(g, NG):
                            act.wait_ge(aggregated, g + 1)
                            nc.scalar.activation(sd[s][:], mv[s][:, :, 1], ACT.Sqrt, bias=eps[:]).then_inc(sd_ready, 1)
                            act.wait_ge(nb_ready, g + 1)
                            for k in range(Q):
                                i = nc.scalar.activation(msg[s4][:, k, :], msg[s4][:, k, :], ACT.Relu,
                                                         bias=nb[s][:, k:k + 1], scale=sc[s][:, k:k + 1])
                            i.then_inc(normed, 1)

                    steps(act, NG, 4, step, unroll=4)

                @block.vector
                def _(dve):
                    v = nc.vector
                    v.memset(sums[1][:], 0.0).then_inc(chained, 1)

                    def step(t, u):
                        g, s, s4 = t - 1, (u - 1) % 2, (u - 1) % 4
                        if first and live(g, NG):
                            dve.wait_ge(rows_in[s4], quarter(g) * 16 * Q + 16 * Q)
                            for k in range(Q):
                                i = v.bn_stats(bs[s][:, k, :], msg[s4][:, k, :])
                            i.then_inc(counted, 1)
                        if live(g, NG):
                            dve.wait_ge(dst_in[s], half(g) * 16 + 16)
                            if after(g):
                                dve.wait_ge(summed, g - 1)
                            of_tile = dstb[s][:, 1:BLK + 1].rearrange("p (k e) -> p k e", k=Q)
                            before = dstb[s][:, 0:BLK].rearrange("p (k e) -> p k e", k=Q)[:, :, 0:1]
                            v.tensor_tensor(eq[s][:], of_tile,
                                            dst_f[:, ds(g * Q, Q)].unsqueeze(2).broadcast_to([P, Q, P]), ALU.is_equal)
                        if first and live(g, NG):
                            dve.wait_ge(counted, g + 1)
                        g3, s3 = t - 3, (u - 3) % 2
                        if live(g3, NG):
                            dve.wait_ge(summed, g3 + 1)
                            if after(g3):
                                dve.wait_ge(turned, g3 - 1)
                            for k in range(Q):
                                dve.wait_ge(chained, g3 * Q + k + 1)
                                for c in range(KD):
                                    end = sums[s3][:, c, k * P - 1:k * P] if k else sums[1 - s3][:, c, BLK - 1:BLK]
                                    i = v.scalar_tensor_tensor(
                                        sums[s3][:, c, k * P:(k + 1) * P], goes_on[s3][:, k, :], end,
                                        ps_s[s3][:, c, k * P:(k + 1) * P], ALU.mult, ALU.add)
                                i.then_inc(chained, 1)
                        if live(g, NG):
                            if after(g):
                                dve.wait_ge(chained, g * Q - Q + 1)
                            v.tensor_tensor(goes_on[s][:], of_tile, before.broadcast_to([P, Q, P]),
                                            ALU.is_equal).then_inc(masks, 1)
                            if first:
                                for k in range(Q):
                                    i = v.bn_aggr(mv[s][:, k, :], bs[s][:, k, :])
                                i.then_inc(aggregated, 1)
                                dve.wait_ge(sd_ready, g + 1)
                                v.reciprocal(sc[s][:], sd[s][:]).then_inc(inv_ready, 1)
                                dve.wait_ge(inv_ready, g + 1)
                                dve.wait_ge(dinv_in[s4], quarter(g) * 16 * Q + 16 * Q)
                                v.tensor_tensor(sc[s][:], sc[s][:], dsrc[s4][:], ALU.mult).then_inc(sc_ready, 1)
                                dve.wait_ge(sc_ready, g + 1)
                                v.scalar_tensor_tensor(nb[s][:], mv[s][:, :, 0], -1.0, sc[s][:],
                                                       ALU.mult, ALU.mult).then_inc(nb_ready, 1)

                    steps(dve, NG, 3, step, unroll=4)

                @block.tensor
                def _(pe):
                    def step(t, u):
                        g, s, s4 = t - 2, u % 2, (u - 2) % 4
                        if live(g, NG):
                            pe.wait_ge(masks, g + 1)
                            if first:
                                pe.wait_ge(normed, g + 1)
                            else:
                                pe.wait_ge(rows_in[s4], quarter(g) * 16 * Q + 16 * Q)
                            if after(g):
                                pe.wait_ge(chained, g * Q - Q + 1)
                            for c in range(KD):
                                for k in range(Q):
                                    i = nc.tensor.matmul(ps_s[s][:, c, k * P:(k + 1) * P],
                                                         msg[s4][:, k, c * P:(c + 1) * P], eq[s][:, k, :],
                                                         start=True, stop=True)
                            i.then_inc(summed, 1)
                        g, s = t - 3, (u - 3) % 2
                        if live(g, NG):
                            pe.wait_ge(chained, g * Q + Q + 1)
                            if after(g):
                                pe.wait_ge(copied, g - 1)
                            for k in range(Q):
                                for c in range(KD):
                                    i = nc.tensor.transpose(ps_t[s][:, k, c * P:(c + 1) * P],
                                                            sums[s][:, c, k * P:(k + 1) * P], ident[:])
                            i.then_inc(turned, 1)

                    steps(pe, NG, 3, step, unroll=4)
            ph.end()

        def batch_norm_coefficients(tag, stats, b_c, g_c, be_c):
            r = NPAD / N
            ph = Phase(tag)
            mv = ph.sb("mv", [P, KD, 2])
            m, w = ph.sb("m", [P, KD]), ph.sb("w", [P, KD])
            dve_step, var_ready, sd_ready = (ph.sem(n) for n in ("dve_step", "var_ready", "sd_ready"))
            if True:
                with nc.Block() as block:
                    @block.gpsimd
                    def _(pool):
                        ph.zero_previous(pool)

                    @block.scalar
                    def _(act):
                        act.wait_ge(var_ready, 1)
                        nc.scalar.activation(w[:], w[:], ACT.Sqrt, bias=eps[:]).then_inc(sd_ready, 1)

                    @block.vector
                    def _(dve):
                        done = [0]

                        def link(ins):
                            done[0] += 1
                            ins.then_inc(dve_step, 1)
                            dve.wait_ge(dve_step, done[0])

                        v = nc.vector
                        v.bn_aggr(mv[:, 0, :], stats[:, 0, :, :].rearrange("p b k -> p (b k)"))
                        link(v.bn_aggr(mv[:, 1, :], stats[:, 1, :, :].rearrange("p b k -> p (b k)")))
                        link(v.tensor_tensor(w[:], mv[:, :, 0], mv[:, :, 0], ALU.mult))
                        link(v.scalar_tensor_tensor(w[:], w[:], -(r - 1.0), mv[:, :, 1], ALU.mult, ALU.add))
                        v.tensor_scalar(w[:], w[:], r, None, ALU.mult).then_inc(var_ready, 1)
                        link(v.scalar_tensor_tensor(m[:], mv[:, :, 0], r, b_c[:], ALU.mult, ALU.add))
                        dve.wait_ge(sd_ready, 1)
                        link(v.reciprocal(w[:], w[:]))
                        link(v.tensor_tensor(bn_s[:], w[:], g_c[:], ALU.mult))
                        link(v.tensor_tensor(m[:], b_c[:], m[:], ALU.subtract))
                        link(v.tensor_tensor(m[:], m[:], bn_s[:], ALU.mult))
                        link(v.tensor_tensor(bn_t[:], m[:], be_c[:], ALU.add))
            ph.end()

        def load_rows(sp, dst, rows, b, arrived):
            if isinstance(b, int) and b == NB - 1 and rows.shape[0] != NB * P:
                sp.dma_start(dst[0:TAIL], rows[b * P:b * P + TAIL, :]).then_inc(arrived, 16)
            else:
                sp.dma_start(dst[:], rows[ds(b * P, P), :]).then_inc(arrived, 16)

        def flat(t):
            return t[:].rearrange("p q d -> p (q d)")

        def aggregate(tag, src, first, dst_t, stats):
            ph = Phase(tag)
            xb = ph.sb("xb", [P, Q, D], n=4)
            own = ph.sb("own", [P, Q, D], n=4)
            gath = ph.sb("gath", [P, Q, D], n=4)
            idx = ph.sb("idx", [P, Q], I32, n=4)
            scal = ph.sb("scal", [P, 2, Q], n=4)
            ob = ph.sb("ob", [P, KD, BLK], n=2)
            ps_t = ph.ps("ps_t", [P, KD, BLK], n=2)
            seg_in = ph.gather_sems(4)
            x_in, stored = ph.sem("x_in", n=4), ph.sem("stored", n=2)
            (cleared, staged, scal_ready, own_ready, combined, turned, copied, counted) = (
                ph.sem(n) for n in ("cleared", "staged", "scal_ready", "own_ready", "combined", "turned",
                                    "copied", "counted"))
            if first:
                bs, mv = ph.sb("bs", [P, Q, 6], n=2), ph.sb("mv", [P, Q, 2], n=2)
                sd, sc, nb = (ph.sb(n, [P, Q], n=2) for n in ("sd", "sc", "nb"))
                ht = ph.sb("ht", [P, KD, BLK], n=2)
                ps_m = ph.ps("ps_m", [P, KD, BLK], n=2)
                stat_step, sd_ready, sc_step, ht_ready, multiplied = (
                    ph.sem(n) for n in ("stat_step", "sd_ready", "sc_step", "ht_ready", "multiplied"))
            if True:
                made, ps_o = (multiplied, ps_m) if first else (turned, ps_t)
                lag_c, lag_o = (3, 6) if first else (2, 4)

                with nc.Block() as block:
                    @block.sync
                    def _(sp):
                        def step(t, u):
                            if live(t, NB):
                                if isinstance(t, int) and t < 4 and first:
                                    sp.wait_ge(cleared, t + 1)
                                if after(t, 4):
                                    sp.wait_ge(own_ready, t - 3)
                                load_rows(sp, xb[u][:].rearrange("p q d -> p (q d)"), src, t, x_in[u])
                            b, s = t - lag_o, (u - lag_o) % 2
                            if live(b, NB):
                                sp.wait_ge(copied, b + 1)
                                sp.dma_start(dst_t[ds(b * P, P), :],
                                             ob[s][:].rearrange("p c n -> p (c n)")).then_inc(stored[s], 16)

                        steps(sp, NB, lag_o, step, unroll=4)
                        sp.wait_ge(stored[0], 16 * (NB // 2))
                        sp.wait_ge(stored[1], 16 * (NB // 2))

                    @block.gpsimd
                    def _(pool):
                        bound = nc.gpsimd.to_reg(E - 1)

                        def step(t, u):
                            if after(t, 4):
                                pool.wait_ge(combined, t - 3)
                            nc.gpsimd.tensor_copy(idx[u][:], end_index[:, ds(t * Q, Q)]).then_inc(staged, 1)
                            if isinstance(t, int) and t < 4:
                                pool.wait_ge(cleared, t + 1)
                            pool.wait_ge(staged, t + 1)
                            pool.sem_inc(issuing, 1)
                            for q in range(Q):
                                nc.gpsimd.indirect_dma_start(
                                    gath[u][:, q, :], None, seg,
                                    bass.IndirectOffsetOnAxis(ap=idx[u][:, q:q + 1], axis=0),
                                    bounds_check=bound, oob_is_err=False).then_inc(seg_in[u], 16)

                        steps(pool, NB, 0, step, unroll=4)
                        ph.zero_previous(pool)

                    @block.scalar
                    def _(act):
                        def step(t, u):
                            b, s = t - lag_o, (u - lag_o) % 2
                            if live(b, NB):
                                act.wait_ge(made, b + 1)
                                if after(b):
                                    act.wait_ge(counted, b - 1)
                                    act.wait_ge(stored[s], half(b) * 16)
                                nc.scalar.activation(ob[s][:], ps_o[s][:], ACT.Copy).then_inc(copied, 1)
                            if first:
                                b, s = t - 4, u % 2
                                if live(b, NB):
                                    act.wait_ge(turned, b + 1)
                                    if after(b):
                                        act.wait_ge(multiplied, b - 1)
                                    nc.scalar.activation(ht[s][:], ps_t[s][:], ACT.Copy).then_inc(ht_ready, 1)
                            b, s, s4 = t - 2, u % 2, (u - 2) % 4
                            if live(b, NB):
                                if after(b, 4):
                                    act.wait_ge(turned, b - 3)
                                act.wait_ge(scal_ready, b + 1)
                                if not first:
                                    act.wait_ge(x_in[s4], quarter(b) * 16 + 16)
                                for q in range(Q):
                                    if first:
                                        i = nc.scalar.activation(own[s4][:, q, :], xb[s4][:, q, :], ACT.Relu,
                                                                 bias=nb[s][:, q:q + 1], scale=sc[s][:, q:q + 1])
                                    else:
                                        i = nc.scalar.activation(own[s4][:, q, :], xb[s4][:, q, :], ACT.Copy,
           scale=scal[s4][:, 0, q:q + 1])
                                i.then_inc(own_ready, 1)
                            if first:
                                b, s = t - 1, (u - 1) % 2
                                if live(b, NB):
                                    act.wait_ge(stat_step, 2 * b + 2)
                                    nc.scalar.activation(sd[s][:], mv[s][:, :, 1], ACT.Sqrt,
                                                         bias=eps[:]).then_inc(sd_ready, 1)

                        steps(act, NB, lag_o, step, unroll=4)

                    @block.vector
                    def _(dve):
                        v = nc.vector
                        for i in range(4):
                            if first:
                                v.memset(xb[i][:], 0.0)
                            v.memset(gath[i][:], 0.0).then_inc(cleared, 1)

                        def step(t, u):
                            b, s = t - 2, u % 2
                            b1, s1, s14 = t - 1, (u - 1) % 2, (u - 1) % 4
                            if first and live(b1, NB):
                                dve.wait_ge(x_in[s14], quarter(b1) * 16 + 16)
                                for q in range(Q):
                                    i = v.bn_stats(bs[s1][:, q, :], xb[s14][:, q, :])
                                i.then_inc(stat_step, 1)
                            if first and live(b, NB):
                                dve.wait_ge(sc_step, 2 * b + 1)
                                v.tensor_tensor(sc[s][:], sc[s][:], dinv2[:, ds(b * Q, Q)],
                                                ALU.mult).then_inc(sc_step, 1)
                            b3, s3 = t - lag_c, (u - lag_c) % 4
                            if live(b3, NB):
                                dve.wait_ge(own_ready, b3 + 1)
                                dve.wait_ge(seg_in[s3], quarter(b3) * 16 * Q + 16 * Q)
                            for q in range(Q):
                                if first and live(b, NB) and q == 2:
                                    dve.wait_ge(sc_step, 2 * b + 2)
                                    v.scalar_tensor_tensor(nb[s][:], mv[s][:, :, 0], -1.0, sc[s][:],
                                                           ALU.mult, ALU.mult).then_inc(scal_ready, 1)
                                if live(b3, NB):
                                    i = v.scalar_tensor_tensor(own[s3][:, q, :], gath[s3][:, q, :],
                                                               scal[s3][:, 1, q:q + 1], own[s3][:, q, :],
                                                               ALU.mult, ALU.add)
                            if live(b3, NB):
                                i.then_inc(combined, 1)
                            if live(b1, NB):
                                if first:
                                    dve.wait_ge(stat_step, 2 * b1 + 1)
                                if after(b1, 4):
                                    dve.wait_ge(combined, b1 - 3)
                                i = v.tensor_copy(scal[s14][:].rearrange("p a q -> p (a q)"),
                                                  dh[:, ds(b1, 1), :, :].rearrange("p b a q -> p (b a q)"))
                                if first:
                                    for q in range(Q):
                                        i = v.bn_aggr(mv[s1][:, q, :], bs[s1][:, q, :])
                                    i.then_inc(stat_step, 1)
                                else:
                                    i.then_inc(scal_ready, 1)
                            b, s = t - lag_o, (u - lag_o) % 2
                            if live(b, NB):
                                dve.wait_ge(copied, b + 1)
                                for c in range(KD):
                                    i = v.bn_stats(stats[:, c, ds(b, 1), :].rearrange("p b k -> p (b k)"),
                                                   ob[s][:, c, :])
                                i.then_inc(counted, 1)
                            if first and live(b1, NB):
                                dve.wait_ge(sd_ready, b1 + 1)
                                v.reciprocal(sc[s1][:], sd[s1][:]).then_inc(sc_step, 1)

                        steps(dve, NB, lag_o, step, unroll=4)

                    @block.tensor
                    def _(pe):
                        def step(t, u):
                            b, s = t - 5, (u - 5) % 2
                            if first and live(b, NB):
                                pe.wait_ge(ht_ready, b + 1)
                                if after(b):
                                    pe.wait_ge(copied, b - 1)
                                for o in range(KD):
                                    for c in range(KD):
                                        i = nc.tensor.matmul(ps_m[s][:, o, :], w1[:, c, o * P:(o + 1) * P],
                                                             ht[s][:, c, :], start=(c == 0), stop=(c == KD - 1))
                                i.then_inc(multiplied, 1)
                            b, s, s4 = t - lag_c, (u - lag_c) % 2, (u - lag_c) % 4
                            if live(b, NB):
                                pe.wait_ge(combined, b + 1)
                                if after(b):
                                    if first:
                                        pe.wait_ge(ht_ready, b - 1)
                                    else:
                                        pe.wait_ge(copied, b - 1)
                                for c in range(KD):
                                    for q in range(Q):
                                        i = nc.tensor.transpose(ps_t[s][:, c, q * P:(q + 1) * P],
                                                                own[s4][:, q, c * P:(c + 1) * P], ident[:])
                                i.then_inc(turned, 1)

                        steps(pe, NB, lag_o - 1, step, unroll=4)
            ph.end()

        FIRST = NB * 2 // 3

        class FreeNodes:

            def __init__(self, ph):
                self.rank, self.node = ph.sb("rank_st", [P, Q], I32, n=4), ph.sb("node_st", [P, Q], I32, n=4)
                self.staged, self.put = ph.sem("put_staged"), ph.gather_sems(4)

            def write(self, pool, start, n):
                bound = nc.gpsimd.to_reg(NPAD - 1)

                def step(b, s):
                    if after(b, 4):
                        pool.wait_ge(self.put[s], quarter(b) * 16 * Q)
                    nc.gpsimd.tensor_copy(self.rank[s][:], free_rank[:, ds((b + start) * Q, Q)])
                    nc.gpsimd.tensor_copy(self.node[s][:], node_id[:, ds((b + start) * Q, Q)]
                                          ).then_inc(self.staged, 1)
                    pool.wait_ge(self.staged, b + 1)
                    pool.sem_inc(issuing, 1)
                    for q in range(Q):
                        nc.gpsimd.indirect_dma_start(
                            free_tab, bass.IndirectOffsetOnAxis(ap=self.rank[s][:, q:q + 1], axis=0),
                            self.node[s][:, q:q + 1], None,
                            bounds_check=bound, oob_is_err=False).then_inc(self.put[s], 16)

                steps(pool, n, 0, step, unroll=4)
                for i in range(4):
                    pool.wait_ge(self.put[i], 16 * Q * len(range(i, n, 4)))

        def lin2():
            ph = Phase("l2")
            zb = ph.sb("zb", [P, KD, BLK], n=4)
            hb = ph.sb("hb", [P, KD, BLK], n=2)
            h_hi, h_lo = (ph.sb(n, [P, KD, BLK], F32R, n=2) for n in ("h_hi", "h_lo"))
            gb = ph.sb("gb", [P, Q, D], n=4)
            ps_g = ph.ps("ps_g", [P, Q, D], n=2)
            z_in, stored = ph.sem("z_in", n=4), ph.sem("stored", n=4)
            h_ready, high, low, multiplied, scaled = (
                ph.sem(n) for n in ("h_ready", "high", "low", "multiplied", "scaled"))
            free = FreeNodes(ph)
            with nc.Block() as block:
                @block.sync
                def _(sp):
                    def step(t, u):
                        if live(t, NB):
                            if after(t, 4):
                                sp.wait_ge(h_ready, t - 3)
                            sp.dma_start(zb[u][:].rearrange("p c n -> p (c n)"),
                                         o1t[ds(t * P, P), :]).then_inc(z_in[u], 16)
                        b, s = t - 4, u
                        if live(b, NB):
                            sp.wait_ge(scaled, b + 1)
                            sp.dma_start(g2_r[ds(b * P, P), :],
                                         gb[s][:].rearrange("p q d -> p (q d)")).then_inc(stored[s], 16)

                    steps(sp, NB, 4, step, unroll=4)
                    for i in range(4):
                        sp.wait_ge(stored[i], 16 * len(range(i, NB, 4)))

                @block.gpsimd
                def _(pool):
                    free.write(pool, 0, FIRST)
                    ph.zero_previous(pool)

                @block.scalar
                def _(act):
                    def step(b, u):
                        s = u % 2
                        act.wait_ge(z_in[u], quarter(b) * 16 + 16)
                        if after(b):
                            act.wait_ge(low, b - 1)
                        for c in range(KD):
                            i = nc.scalar.activation(hb[s][:, c, :], zb[u][:, c, :], ACT.Relu,
                                                     bias=bn_t[:, c:c + 1], scale=bn_s[:, c:c + 1])
                        i.then_inc(h_ready, 1)
                        act.wait_ge(h_ready, b + 1)
                        if after(b):
                            act.wait_ge(multiplied, b - 1)
                        nc.scalar.activation(h_hi[s][:], hb[s][:], ACT.Copy).then_inc(high, 1)

                    steps(act, NB, 0, step, unroll=4)

                @block.tensor
                def _(pe):
                    def step(b, s):
                        pe.wait_ge(low, b + 1)
                        if after(b):
                            pe.wait_ge(scaled, b - 1)
                        for q in range(Q):
                            terms = [(a, w, c) for c in range(KD)
                                     for a, w in ((h_hi, w2_hi), (h_hi, w2_lo), (h_lo, w2_hi))]
                            for n, (a, w, c) in enumerate(terms):
                                i = nc.tensor.matmul(ps_g[s][:, q, :], a[s][:, c, q * P:(q + 1) * P], w[:, c, :],
                                                     start=(n == 0), stop=(n == len(terms) - 1))
                        i.then_inc(multiplied, 1)

                    steps(pe, NB, 0, step)

                @block.vector
                def _(dve):
                    v = nc.vector

                    def step(t, u):
                        b, s = t, u % 2
                        if live(b, NB):
                            dve.wait_ge(high, b + 1)
                            if after(b):
                                dve.wait_ge(multiplied, b - 1)
                            v.tensor_tensor(h_lo[s][:], hb[s][:], h_hi[s][:].bitcast(F32), ALU.subtract
                                            ).then_inc(low, 1)
                        b, s, s4 = t - 1, (u - 1) % 2, (u - 1) % 4
                        if live(b, NB):
                            dve.wait_ge(multiplied, b + 1)
                            if after(b, 4):
                                dve.wait_ge(stored[s4], quarter(b) * 16)
                            v.tensor_tensor(gb[s4][:], ps_g[s][:],
                                            dinv[:, ds(b * Q, Q)].unsqueeze(2).broadcast_to([P, Q, D]),
                                            ALU.mult).then_inc(scaled, 1)

                    steps(dve, NB, 1, step, unroll=4)
            ph.end()

        def residual():
            ph = Phase("rs")
            zb = ph.sb("zb", [P, KD, BLK], n=4)
            hb = ph.sb("hb", [P, KD, BLK], n=2)
            xb = ph.sb("xb", [P, Q, D], n=4)
            x1b = ph.sb("x1b", [P, Q, DX], n=4)
            bs, mv, sd = (ph.sb(n, [P, Q, k], n=2) for n, k in (("bs", 6), ("mv", 2), ("sd", 1)))
            rank_st, node_st = ph.sb("slot_rank_st", [P, Q], I32, n=4), ph.sb("slot_node_st", [P, Q], I32, n=4)
            ps_h = ph.ps("ps_h", [P, Q, D], n=2)
            z_in, x_in, stored, got = ph.sem("z_in", n=4), ph.sem("x_in", n=4), ph.sem("stored", n=4), ph.gather_sems(4)
            (h_ready, turned, added, counted, aggregated, sd_ready, inv_ready, row_ready, staged, kept, rest_in,
             table_ready) = (ph.sem(n) for n in (
                "h_ready", "turned", "added", "counted", "aggregated", "sd_ready", "inv_ready", "row_ready", "staged",
                "kept", "rest_in", "table_ready"))
            free = FreeNodes(ph)
            if True:
                with nc.Block() as block:
                    @block.sync
                    def _(sp):
                        def step(t, u):
                            if live(t, NB):
                                s = u
                                if after(t, 4):
                                    sp.wait_ge(h_ready, t - 3)
                                sp.dma_start(zb[s][:].rearrange("p c n -> p (c n)"),
                                             o2t[ds(t * P, P), :]).then_inc(z_in[s], 16)
                                if after(t, 4):
                                    sp.wait_ge(added, t - 3)
                                load_rows(sp, xb[s][:].rearrange("p q d -> p (q d)"), x_r, t, x_in[s])
                            b, s = t - 5, (u - 5) % 4
                            if live(b, NB):
                                sp.wait_ge(row_ready, b + 1)
                                sp.dma_start(x1_r[ds(b * P, P), :],
                                             x1b[s][:].rearrange("p q d -> p (q d)")).then_inc(stored[s], 16)

                        steps(sp, NB, 5, step, unroll=4)
                        off = sp.value_load(free_off[0:1, 0:1], min_val=0, max_val=E)
                        sp.wait_ge(table_ready, 1)
                        sp.dma_start(slot_node[1][:], free_tab[ds(off, P * NT), :].rearrange(
                            "(p a) o -> p (a o)", p=P)).then_inc(rest_in, 16)
                        for i in range(4):
                            sp.wait_ge(stored[i], 16 * len(range(i, NB, 4)))

                    @block.gpsimd
                    def _(pool):
                        free.write(pool, FIRST, NB - FIRST)
                        pool.sem_inc(table_ready, 1)
                        bound = nc.gpsimd.to_reg(NPAD - 1)

                        def step(t, u):
                            g, s = t, u
                            if live(g, NG):
                                if after(g, 4):
                                    pool.wait_ge(kept, g - 3)
                                nc.gpsimd.tensor_copy(rank_st[s][:], slot_rank[:, ds(g * Q, Q)])
                                nc.gpsimd.tensor_copy(node_st[s][:], dst_i[:, ds(g * Q, Q)]).then_inc(staged, 1)
                                pool.wait_ge(staged, g + 1)
                                pool.sem_inc(issuing, 1)
                                for k in range(Q):
                                    nc.gpsimd.indirect_dma_start(
                                        node_st[s][:, k:k + 1], None, free_tab,
                                        bass.IndirectOffsetOnAxis(ap=rank_st[s][:, k:k + 1], axis=0),
                                        bounds_check=bound, oob_is_err=False).then_inc(got[s], 16)
                            g, s = t - 3, (u - 3) % 4
                            if live(g, NG):
                                pool.wait_ge(got[s], quarter(g) * 16 * Q + 16 * Q)
                                nc.gpsimd.tensor_copy(slot_node[0][:, ds(g * Q, Q)], node_st[s][:]).then_inc(kept, 1)

                        steps(pool, NG, 3, step, unroll=4)
                        ph.zero_previous(pool)

                    @block.scalar
                    def _(act):
                        def step(t, u):
                            b, s = t, u % 2
                            if live(b, NB):
                                act.wait_ge(z_in[u], quarter(b) * 16 + 16)
                                if after(b):
                                    act.wait_ge(turned, b - 1)
                                for c in range(KD):
                                    i = nc.scalar.activation(hb[s][:, c, :], zb[u][:, c, :], ACT.Relu,
                                                             bias=bn_t[:, c:c + 1], scale=bn_s[:, c:c + 1])
                                i.then_inc(h_ready, 1)
                            b, s = t - 2, u % 2
                            if live(b, NB):
                                act.wait_ge(aggregated, b + 1)
                                nc.scalar.activation(sd[s][:, :, 0], mv[s][:, :, 1], ACT.Sqrt, bias=eps[:]
                                                     ).then_inc(sd_ready, 1)

                        steps(act, NB, 2, step, unroll=4)

                    @block.tensor
                    def _(pe):
                        def step(b, s):
                            pe.wait_ge(h_ready, b + 1)
                            if after(b):
                                pe.wait_ge(added, b - 1)
                            for q in range(Q):
                                for c in range(KD):
                                    i = nc.tensor.transpose(ps_h[s][:, q, c * P:(c + 1) * P],
                                                            hb[s][:, c, q * P:(q + 1) * P], ident[:])
                            i.then_inc(turned, 1)

                        steps(pe, NB, 0, step)

                    @block.vector
                    def _(dve):
                        v = nc.vector

                        def step(t, u):
                            b, s, s4 = t, u % 2, u % 4
                            b1, s1 = t - 1, (u - 1) % 2
                            b2, s2, s24 = t - 2, u % 2, (u - 2) % 4
                            if live(b2, NB):
                                dve.wait_ge(sd_ready, b2 + 1)
                                v.reciprocal(x1b[s24][:, :, D], sd[s2][:, :, 0]).then_inc(inv_ready, 1)
                            if live(b, NB):
                                dve.wait_ge(turned, b + 1)
                                dve.wait_ge(x_in[s4], quarter(b) * 16 + 16)
                                if after(b, 4):
                                    dve.wait_ge(stored[s4], quarter(b) * 16)
                                if live(b1, NB):
                                    dve.wait_ge(counted, b1 + 1)
                                v.tensor_tensor(x1b[s4][:, :, 0:D], ps_h[s][:], xb[s4][:], ALU.add).then_inc(added, 1)
                            if live(b2, NB):
                                dve.wait_ge(inv_ready, b2 + 1)
                                v.scalar_tensor_tensor(x1b[s24][:, :, D + 1], mv[s2][:, :, 0], -1.0,
                                                       x1b[s24][:, :, D], ALU.mult, ALU.mult).then_inc(row_ready, 1)
                            if live(b1, NB):
                                if not live(b, NB):
                                    dve.wait_ge(counted, b1 + 1)
                                for q in range(Q):
                                    i = v.bn_aggr(mv[s1][:, q, :], bs[s1][:, q, :])
                                i.then_inc(aggregated, 1)
                            if live(b, NB):
                                dve.wait_ge(added, b + 1)
                                for q in range(Q):
                                    i = v.bn_stats(bs[s][:, q, :], x1b[s4][:, q, 0:D])
                                i.then_inc(counted, 1)

                        steps(dve, NB, 2, step, unroll=4)
                        dve.wait_ge(rest_in, 16)
                        v.tensor_tensor(slot_node[1][:], slot_node[1][:], pad_slot[:], ALU.add)
            ph.end()

        def gru(tag, with_edges):
            nodes = slot_node[0 if with_edges else 1]
            ph = Phase(tag)
            sb, ps, sem = ph.sb, ph.ps, ph.sem
            if True:
                def two(name, shape, dt=F32):
                    return ph.sb(name, shape, dt, n=2)

                xb = [sb(f"xb{i}", [P, Q, DX]) for i in range(4)]
                fb = two("fb", [P, Q, D])
                own_idx = two("own_idx", [P, Q], I32)
                out_idx = two("out_idx", [P, Q], I32)
                h2 = two("h2", [P, Q, D])
                ht = two("ht", [P, KD, BLK])
                h_hi, h_lo = (two(n, [P, KD, BLK], F32R) for n in ("h_hi", "h_lo"))
                rg, zg, ng, tg = (two(n, [P, BLK]) for n in ("rg", "zg", "ng", "tg"))
                hn = two("hn", [P, KD, BLK])
                ps_a = ps("ps_a", [P, KD, BLK])
                ps_r, ps_z, ps_hn = (ps(n, [P, BLK]) for n in ("ps_r", "ps_z", "ps_hn"))
                x_in, stored = ph.gather_sems(4), ph.gather_sems(2)
                (staged, h2_ready, turned, back, r_ps, z_ps, hn_ps, r_ready, z_ready,
                 n_ready, reset, copied, low, dif, zdif, new_h, finished, cleared) = (
                    sem(n) for n in ("staged", "h2_ready", "turned", "back", "r_ps", "z_ps", "hn_ps", "r_ready",
                                     "z_ready", "n_ready", "reset", "copied", "low", "dif", "zdif", "new_h",
                                     "finished", "cleared"))
                if with_edges:
                    dstb = two("dstb", [P, BLK + 2], I32)
                    typ = two("typ", [NREL, Q, P], I32)
                    hot = two("hot", [NREL, Q, P], F32R)
                    eq = two("eq", [P, Q, P], F32R)
                    goes_on = two("goes_on", [P, Q, P])
                    is_last = two("is_last", [P, BLK])
                    msg_idx = two("msg_idx", [P, Q], I32)
                    raw = two("raw", [P, Q, DX])
                    msg = sb("msg", [P, Q, D])
                    m_hi, m_lo = (sb(n, [P, Q, D], F32R) for n in ("m_hi", "m_lo"))
                    sums = two("sums", [P, KD, BLK])
                    red = sb("red", [P, KD, BLK])
                    r_hi, r_lo = (two(n, [P, KD, BLK], F32R) for n in ("r_hi", "r_lo"))
                    ps_b = ps("ps_b", [P, KD, BLK])
                    ps_in = ps("ps_in", [P, BLK])
                    rows_in = ph.gather_sems(2)
                    dst_in = [sem(f"dst_in{i}") for i in range(2)]
                    (masks, msg_ready, rel_ready, with_rel, m_high, m_split, summed, chained, masked, r_high,
                     in_ps, summed_n) = (
                        sem(n) for n in ("masks", "msg_ready", "rel_ready", "with_rel", "m_high", "m_split",
                                         "summed", "chained", "masked", "r_high", "in_ps", "summed_n"))
                    ps_f = ps_a
                else:
                    in_ps = summed_n = None
                    ps_f = ps("ps_f", [P, KD, BLK])

                def later(n):
                    return not isinstance(n, int) or n >= 1

                with nc.Block() as block:
                    @block.sync
                    def _(sp):
                        if not with_edges:
                            return

                        def step(t, s):
                            if after(t):
                                sp.wait_ge(masks, t - 1)
                            sp.dma_start(dstb[s][:], dst_row[0:1, ds(t * BLK, BLK + 2)].broadcast_to([P, BLK + 2])
                                         ).then_inc(dst_in[s], 16)
                            sp.dma_start(typ[s][:].rearrange("p k e -> p (k e)"),
                                         type_row[0:1, ds(t * BLK, BLK)].broadcast_to([NREL, BLK])
                                         ).then_inc(dst_in[s], 16)

                        steps(sp, NG, 0, step)

                    @block.gpsimd
                    def _(pool):
                        bound = nc.gpsimd.to_reg(N - 1)

                        def step(t, u):
                            s = u % 2
                            b = t - 4
                            if live(t, NG):
                                if after(t):
                                    pool.wait_ge(h2_ready, t - 1)
                                nc.gpsimd.tensor_copy(own_idx[s][:], nodes[:, ds(t * Q, Q)])
                                if with_edges:
                                    nc.gpsimd.tensor_copy(msg_idx[s][:], src_i[:, ds(t * Q, Q)])
                            nc.gpsimd.memset(spare[:], 0.0).then_inc(staged, 1)
                            pool.wait_ge(staged, 2 * t + 1)
                            pool.sem_inc(issuing, 1)
                            if with_edges and live(t, NG):
                                for q in range(Q):
                                    nc.gpsimd.indirect_dma_start(
                                        raw[s][:, q, :], None, x1s,
                                        bass.IndirectOffsetOnAxis(ap=msg_idx[s][:, q:q + 1], axis=0),
                                        bounds_check=bound, oob_is_err=False).then_inc(rows_in[s], 16)
                            if live(b, NG):
                                if after(b):
                                    pool.wait_ge(stored[s], half(b) * 16 * Q)
                                pool.wait_ge(finished, b + 1)
                                nc.gpsimd.tensor_copy(out_idx[s][:], nodes[:, ds(b * Q, Q)])
                            if isinstance(t, int) and t < 4:
                                pool.wait_ge(cleared, t + 1)
                            nc.gpsimd.memset(spare[:], 0.0).then_inc(staged, 1)
                            pool.wait_ge(staged, 2 * t + 2)
                            pool.sem_inc(issuing, 1)
                            if live(t, NG):
                                for q in range(Q):
                                    nc.gpsimd.indirect_dma_start(
                                        xb[u][:, q, :], None, x1s,
                                        bass.IndirectOffsetOnAxis(ap=own_idx[s][:, q:q + 1], axis=0),
                                        bounds_check=bound, oob_is_err=False).then_inc(x_in[u], 16)
                            if live(b, NG):
                                for q in range(Q):
                                    nc.gpsimd.indirect_dma_start(
                                        out, bass.IndirectOffsetOnAxis(ap=out_idx[s][:, q:q + 1], axis=0),
                                        fb[s][:, q, :], None,
                                        bounds_check=bound, oob_is_err=False).then_inc(stored[s], 16)

                        steps(pool, NG, 4, step, unroll=4)
                        ph.zero_previous(pool)
                        pool.wait_ge(stored[0], 16 * Q * ((NG + 1) // 2))
                        pool.wait_ge(stored[1], 16 * Q * (NG // 2))

                    @block.scalar
                    def _(act):
                        def step(t, u):
                            b, s = t - 1, (u - 1) % 2
                            b2 = t - 2

                            def reset_of(b, h):
                                n = 2 * b + h
                                act.wait_ge(r_ps, n + 1)
                                if later(n - 1):
                                    act.wait_ge(reset, n - 1)
                                nc.scalar.activation(rg[h][:], ps_r[:], ACT.Sigmoid,
                                                     bias=brz[:, h:h + 1]).then_inc(r_ready, 1)

                            def candidate_of(b, h):
                                n = 2 * b + h
                                act.wait_ge(summed_n if with_edges else reset, n + 1)
                                if later(n - 1):
                                    act.wait_ge(new_h, n - 1)
                                nc.scalar.activation(ng[h][:], tg[h][:], ACT.Tanh,
                                                     bias=bih[:, 4 + h:5 + h]).then_inc(n_ready, 1)

                            def update_of(b, h):
                                n = 2 * b + h
                                act.wait_ge(z_ps, n + 1)
                                nc.scalar.activation(zg[h][:], ps_z[:], ACT.Sigmoid,
                                                     bias=brz[:, 2 + h:3 + h]).then_inc(z_ready, 1)

                            if live(b, NG):
                                act.wait_ge(turned, b + 1)
                                if after(b):
                                    act.wait_ge(z_ps, 2 * b - 2)
                                    act.wait_ge(dif, 2 * b - 2)
                                nc.scalar.activation(h_hi[s][:], ps_a[:], ACT.Copy).then_inc(copied, 1)
                                nc.scalar.activation(ht[s][:], ps_a[:], ACT.Copy).then_inc(copied, 1)
                                if with_edges:
                                    act.wait_ge(with_rel, b + 1)
                                    if later(b):
                                        act.wait_ge(summed, b)
                                    nc.scalar.activation(m_hi[:], msg[:], ACT.Copy).then_inc(m_high, 1)
                            if live(b2, NG):
                                reset_of(b2, 0)
                                candidate_of(b2, 0)
                                update_of(b2, 0)
                            if live(t, NG):
                                s1 = u % 2
                                if with_edges:
                                    act.wait_ge(rows_in[s1], half(t) * 16 * Q + 16 * Q)
                                    if later(t):
                                        act.wait_ge(m_split, t)
                                    for q in range(Q):
                                        i = nc.scalar.activation(msg[:, q, :], raw[s1][:, q, 0:D], ACT.Relu,
                                                                 bias=raw[s1][:, q, D + 1:D + 2],
                                                                 scale=raw[s1][:, q, D:D + 1])
                                    i.then_inc(msg_ready, 1)
                                act.wait_ge(x_in[u], quarter(t) * 16 * Q + 16 * Q)
                                if after(t):
                                    act.wait_ge(turned, t - 1)
                                for q in range(Q):
                                    i = nc.scalar.activation(h2[s1][:, q, :], xb[u][:, q, 0:D], ACT.Relu,
                                                             bias=xb[u][:, q, D + 1:D + 2],
                                                             scale=xb[u][:, q, D:D + 1])
                                i.then_inc(h2_ready, 1)
                            if live(b2, NG):
                                reset_of(b2, 1)
                            if with_edges and live(b, NG):
                                act.wait_ge(masked, b + 1)
                                nc.scalar.activation(r_hi[s][:], red[:], ACT.Copy).then_inc(r_high, 1)
                            if live(b2, NG):
                                candidate_of(b2, 1)
                                update_of(b2, 1)

                        steps(act, NG, 2, step, unroll=4)

                    @block.vector
                    def _(dve):
                        v = nc.vector
                        for i in range(4):
                            v.memset(xb[i][:], 0.0).then_inc(cleared, 1)
                        if with_edges:
                            v.memset(sums[1][:], 0.0).then_inc(chained, 1)

                        def step(t, u):
                            b, s = t - 1, (u - 1) % 2

                            def reset_gate(b, h):
                                n = 2 * b + h
                                dve.wait_ge(hn_ps, n + 1)
                                dve.wait_ge(r_ready, n + 1)
                                if not isinstance(n, int) or n >= 2:
                                    dve.wait_ge(n_ready, n - 1)
                                v.scalar_tensor_tensor(tg[h][:], ps_hn[:], bhh[:, 4 + h:5 + h], rg[h][:],
                                                       ALU.add, ALU.mult).then_inc(reset, 1)

                            def candidate(b, h):
                                if with_edges:
                                    n = 2 * b + h
                                    dve.wait_ge(in_ps, n + 1)
                                    dve.wait_ge(reset, n + 1)
                                    v.tensor_tensor(tg[h][:], tg[h][:], ps_in[:], ALU.add).then_inc(summed_n, 1)

                            def difference(b, s, h):
                                n = 2 * b + h
                                dve.wait_ge(n_ready, n + 1)
                                dve.wait_ge(copied, 2 * b + 2)
                                if after(b):
                                    dve.wait_ge(back, b - 1)
                                v.tensor_tensor(hn[s][:, h, :], ht[s][:, h, :], ng[h][:], ALU.subtract).then_inc(dif, 1)

                            def new_state(b, s, h):
                                n = 2 * b + h
                                dve.wait_ge(z_ready, n + 1)
                                dve.wait_ge(dif, n + 1)
                                v.tensor_tensor(hn[s][:, h, :], hn[s][:, h, :], zg[h][:], ALU.mult).then_inc(zdif, 1)
                                dve.wait_ge(zdif, n + 1)
                                v.tensor_tensor(hn[s][:, h, :], hn[s][:, h, :], ng[h][:], ALU.add).then_inc(new_h, 1)

                            b2, s2 = t - 2, u % 2
                            b3, s3, u3 = t - 3, (u - 3) % 4, (u - 3) % 2

                            def add_residual():
                                if live(b3, NG):
                                    dve.wait_ge(back, b3 + 1)
                                    dve.wait_ge(x_in[s3], quarter(b3) * 16 * Q + 16 * Q)
                                    if after(b3):
                                        dve.wait_ge(stored[u3], half(b3) * 16 * Q)
                                    v.tensor_tensor(fb[u3][:], ps_f[:].rearrange("p c n -> p (c n)").rearrange(
                                        "p (q d) -> p q d", q=Q), xb[s3][:, :, 0:D], ALU.add).then_inc(finished, 1)

                            if live(b3, NG):
                                new_state(b3, u3, 1)
                            if with_edges and live(b, NG):
                                dve.wait_ge(rel_ready, b + 1)
                                dve.wait_ge(msg_ready, b + 1)
                                v.tensor_tensor(msg[:], msg[:], ps_b[:].rearrange("p c n -> p (c n)").rearrange(
                                    "p (q d) -> p q d", q=Q), ALU.add).then_inc(with_rel, 1)
                            if live(b, NG):
                                if after(b):
                                    dve.wait_ge(z_ps, 2 * b - 2)
                                dve.wait_ge(copied, 2 * b + 2)
                                v.tensor_tensor(h_lo[s][:], ht[s][:], h_hi[s][:].bitcast(F32),
                                                ALU.subtract).then_inc(low, 1)
                                if with_edges:
                                    dve.wait_ge(m_high, b + 1)
                                    v.tensor_tensor(m_lo[:], msg[:], m_hi[:].bitcast(F32),
                                                    ALU.subtract).then_inc(m_split, 1)
                            if live(b2, NG):
                                reset_gate(b2, 0)
                            if with_edges and live(t, NG):
                                dve.wait_ge(dst_in[s2], half(t) * 32 + 32)
                                if after(t):
                                    dve.wait_ge(summed, t - 1)
                                    dve.wait_ge(masked, t - 1)
                                of_tile = dstb[s2][:, 1:BLK + 1].rearrange("p (k e) -> p k e", k=Q)
                                v.tensor_tensor(eq[s2][:], of_tile,
                                                dst_f[:, ds(t * Q, Q)].unsqueeze(2).broadcast_to([P, Q, P]),
                                                ALU.is_equal)
                                before = dstb[s2][:, 0:BLK].rearrange("p (k e) -> p k e", k=Q)[:, :, 0:1]
                                v.tensor_tensor(goes_on[s2][:], of_tile, before.broadcast_to([P, Q, P]), ALU.is_equal)
                                v.tensor_tensor(is_last[s2][:], dstb[s2][:, 1:BLK + 1], dstb[s2][:, 2:BLK + 2],
                                                ALU.not_equal)
                                v.tensor_scalar(hot[s2][:], typ[s2][:], pidx[0:NREL, :], None,
                                                ALU.is_equal).then_inc(masks, 1)
                            if not with_edges:
                                add_residual()
                            if live(b2, NG):
                                candidate(b2, 0)
                            if with_edges and live(b, NG):
                                dve.wait_ge(summed, b + 1)
                                for k in range(Q):
                                    dve.wait_ge(chained, b * Q + k + 1)
                                    for c in range(KD):
                                        end = (sums[s][:, c, k * P - 1:k * P] if k else
                                               sums[1 - s][:, c, BLK - 1:BLK])
                                        i = v.scalar_tensor_tensor(
                                            sums[s][:, c, k * P:(k + 1) * P], goes_on[s][:, k, :], end,
                                            ps_b[:, c, k * P:(k + 1) * P], ALU.mult, ALU.add)
                                    i.then_inc(chained, 1)
                            if live(b2, NG):
                                difference(b2, s2, 0)
                            if with_edges and live(b, NG):
                                dve.wait_ge(chained, b * Q + Q + 1)
                                if later(b):
                                    dve.wait_ge(low, 2 * b)
                                v.tensor_tensor(red[:], sums[s][:],
                                                is_last[s][:].unsqueeze(1).broadcast_to([P, KD, BLK]),
                                                ALU.mult).then_inc(masked, 1)
                            if live(b2, NG):
                                new_state(b2, s2, 0)
                            if with_edges:
                                add_residual()
                            if live(b2, NG):
                                reset_gate(b2, 1)
                            if with_edges and live(b, NG):
                                dve.wait_ge(r_high, b + 1)
                                v.tensor_tensor(r_lo[s][:], red[:], r_hi[s][:].bitcast(F32),
                                                ALU.subtract).then_inc(low, 1)
                            if live(b2, NG):
                                candidate(b2, 1)
                                difference(b2, s2, 1)

                        steps(dve, NG, 3, step, unroll=4)

                    @block.tensor
                    def _(pe):
                        lows = 2 if with_edges else 1
                        both = ("hh", "ih") if with_edges else ("hh",)

                        def product(bank, s, sides, chunk, signal):
                            terms = []
                            for side in sides:
                                hi, lo = (h_hi, h_lo) if side == "hh" else (r_hi, r_lo)
                                for c in range(KD):
                                    terms += [(whi[side], hi, c), (whi[side], lo, c), (wlo[side], hi, c)]
                            for n, (w, a, c) in enumerate(terms):
                                i = nc.tensor.matmul(bank[:], w[:, c, chunk * P:(chunk + 1) * P], a[s][:, c, :],
                                                     start=(n == 0), stop=(n == len(terms) - 1))
                            i.then_inc(signal, 1)

                        def step(t, u):
                            b, s = t - 1, (u - 1) % 2
                            b2, s2 = t - 2, u % 2
                            b3, s3 = t - 3, (u - 3) % 2

                            def rows_of_state():
                                if live(b3, NG):
                                    pe.wait_ge(new_h, 2 * b3 + 2)
                                    if with_edges and live(b, NG):
                                        pe.wait_ge(copied, 2 * b + 2)
                                    if not with_edges and later(b3):
                                        pe.wait_ge(finished, b3)
                                    rows = ps_f[:].rearrange("p c n -> p (c n)")
                                    for q in range(Q):
                                        for c in range(KD):
                                            i = nc.tensor.transpose(rows[:, q * D + c * P:q * D + (c + 1) * P],
                                                                    hn[s3][:, c, q * P:(q + 1) * P], ident[:])
                                    i.then_inc(back, 1)

                            def reset_products(h):
                                n = 2 * b2 + h
                                if later(n):
                                    pe.wait_ge(r_ready, n)
                                product(ps_r, s2, both, h, r_ps)
                                if later(n):
                                    pe.wait_ge(reset, n)
                                product(ps_hn, s2, ("hh",), 4 + h, hn_ps)
                                if with_edges:
                                    if later(n):
                                        pe.wait_ge(summed_n, n)
                                    product(ps_in, s2, ("ih",), 4 + h, in_ps)

                            def update_products(h):
                                n = 2 * b2 + h
                                if later(n):
                                    pe.wait_ge(z_ready, n)
                                product(ps_z, s2, both, 2 + h, z_ps)

                            if live(b, NG):
                                pe.wait_ge(h2_ready, b + 1)
                                if with_edges and live(t - 4, NG):
                                    pe.wait_ge(finished, t - 3)
                                elif later(b):
                                    pe.wait_ge(copied, 2 * b)
                                for c in range(KD):
                                    for q in range(Q):
                                        i = nc.tensor.transpose(ps_a[:, c, q * P:(q + 1) * P],
                                                                h2[s][:, q, c * P:(c + 1) * P], ident[:])
                                i.then_inc(turned, 1)
                            if with_edges and live(b, NG):
                                pe.wait_ge(masks, b + 1)
                                if later(b):
                                    pe.wait_ge(chained, b * Q + 1)
                                vec = ps_b[:].rearrange("p c n -> p (c n)").rearrange("p (q d) -> p q d", q=Q)
                                for q in range(Q):
                                    nc.tensor.matmul(vec[:, q, :], hot[s][:, q, :], rel_hi[:], start=True, stop=False)
                                    i = nc.tensor.matmul(vec[:, q, :], hot[s][:, q, :], rel_lo[:],
                                                         start=False, stop=True)
                                i.then_inc(rel_ready, 1)
                            if live(b2, NG):
                                pe.wait_ge(low, lows * b2 + lows)
                                reset_products(0)
                            if with_edges and live(b, NG):
                                pe.wait_ge(m_split, b + 1)
                                for c in range(KD):
                                    for k in range(Q):
                                        for m in (m_hi, m_lo):
                                            i = nc.tensor.matmul(ps_b[:, c, k * P:(k + 1) * P],
                                                                 m[:, k, c * P:(c + 1) * P], eq[s][:, k, :],
                                                                 start=(m is m_hi), stop=(m is m_lo))
                                i.then_inc(summed, 1)
                            if not with_edges:
                                rows_of_state()
                            if live(b2, NG):
                                update_products(0)
                            if with_edges:
                                rows_of_state()
                            if live(b2, NG):
                                reset_products(1)
                                update_products(1)

                        steps(pe, NG, 3, step, unroll=4)
            ph.end()

        setup()
        edges("e1", x, True)
        with nc.sbuf_tensor("stats1", [P, KD, NB, 6], F32) as stats1:
            aggregate("c1", x_r, True, o1t, stats1)
            batch_norm_coefficients("b1", stats1, bn_in["b1c"], bn_in["g1c"], bn_in["be1c"])
        lin2()
        edges("e2", g2s, False)
        with nc.sbuf_tensor("stats2", [P, KD, NB, 6], F32) as stats2:
            aggregate("a2", g2_r, False, o2t, stats2)
            batch_norm_coefficients("b2", stats2, bn_in["b2c"], bn_in["g2c"], bn_in["be2c"])
        residual()
        gru("ge", True)
        gru("gf", False)


def kernel(**inputs):
    import numpy as np
    import concourse.bacc as bacc
    from concourse import mybir
    from concourse.bass_utils import run_bass_kernel_spmd

    tile = 128
    group = 4 * tile
    n_edges = inputs["dst"].shape[0]
    padded = -(-n_edges // group) * group

    def pad(a, fill):
        return np.concatenate([np.asarray(a), np.full(padded - n_edges, fill, np.int32)])

    dst, src, typ = pad(inputs["dst"], 60000), pad(inputs["src"], 0), pad(inputs["edge_type_16"], 0)
    around = np.concatenate([[-1], dst, [60000]]).astype(np.int32)
    arrays = {
        "x": inputs["x"],
        "dst_row": around.reshape(1, -1),
        "dst_col": dst.reshape(-1, tile).T,
        "next_col": around[2:].reshape(-1, tile).T,
        "src_col": src.reshape(-1, tile).T,
        "type_row": typ.reshape(1, -1),
    }
    for name in ("W1", "b1", "g1", "be1", "W2", "b2", "g2", "be2"):
        arrays[name] = inputs[f"L0_gnn_{name}"]
    for name in ("relvectors", "w_ih", "w_hh", "b_ih", "b_hh"):
        arrays[name] = inputs[f"L1_gnn_{name}"]
    for name, a in arrays.items():
        if a.ndim == 1:
            arrays[name] = np.asarray(a).reshape(-1, tile).T
    arrays = {f"in_{k}": np.ascontiguousarray(v) for k, v in arrays.items()}

    nc = bacc.Bacc("TRN2", target_bir_lowering=False, num_devices=1)
    args = [nc.dram_tensor(k, a.shape, mybir.dt.from_np(a.dtype), kind="ExternalInput").ap()
            for k, a in arrays.items()]
    out = nc.dram_tensor("out", inputs["x"].shape, mybir.dt.float32, kind="ExternalOutput").ap()
    build_program(nc, *args, out)
    r = run_bass_kernel_spmd(nc, [arrays], core_ids=[0])
    return r.results[0]["out"]
```
